# Optimizing a Trainium2 kernel written in Bass

```python
import numpy as np
import jax
import jax.numpy as jnp

def _softmax(x, axis=-1):
    return jax.nn.softmax(x, axis=axis)

def _gelu(x):
    return jax.nn.gelu(x, approximate=True)

def _silu(x):
    return jax.nn.silu(x)

def _sigmoid(x):
    return jax.nn.sigmoid(x)

def _layernorm(x, axis=-1, eps=1e-05):
    m = jnp.mean(x, axis=axis, keepdims=True)
    v = jnp.var(x, axis=axis, keepdims=True)
    return (x - m) / jnp.sqrt(v + eps)

def _scatter_add(tgt, idx, src, axis=0):
    return tgt.at[idx].add(src)

def _segment_sum(src, seg, n):
    return jax.ops.segment_sum(src, seg, n)
kernel_name = 'mk_hybrid_d2_jaxref_r8_a6b881'

def setup_inputs(seed: int=0):
    np.random.seed(seed)
    _w = jnp.asarray

    def _L0_attn_a_setup():
        import jax, jax.numpy as jnp
        import numpy as np
        import math
        WINDOW = 64
        N_HEAD = 16
        key = jax.random.key(seed)
        ks = jax.random.split(key, 5)
        B, L, D = (2, 512, 128)
        s = 0.02
        return {'x': jax.random.normal(ks[0], (B, L, D), dtype=jnp.float32), 'Wq': jax.random.normal(ks[1], (D, D), dtype=jnp.float32) * s, 'bq': jnp.zeros((D,), jnp.float32), 'Wk': jax.random.normal(ks[2], (D, D), dtype=jnp.float32) * s, 'bk': jnp.zeros((D,), jnp.float32), 'Wv': jax.random.normal(ks[3], (D, D), dtype=jnp.float32) * s, 'bv': jnp.zeros((D,), jnp.float32), 'Wo': jax.random.normal(ks[4], (D, D), dtype=jnp.float32) * s, 'bo': jnp.zeros((D,), jnp.float32)}
    _L0_attn_a_in = _L0_attn_a_setup()

    def _L0_attn_b_setup():
        import jax, jax.numpy as jnp
        import numpy as np
        D_MODEL = 128
        key = jax.random.key(seed)
        k1, k2, k3 = jax.random.split(key, 3)
        x = jax.random.normal(k1, (4, 256, D_MODEL), dtype=jnp.float32)
        wqk = jax.random.normal(k2, (D_MODEL, D_MODEL), dtype=jnp.float32) * 0.02
        wov = jax.random.normal(k3, (D_MODEL, D_MODEL), dtype=jnp.float32) * 0.02
        return {'x': x, 'wqk': wqk, 'wov': wov}
    _L0_attn_b_in = _L0_attn_b_setup()

    def _L0_ffn_setup():
        import jax, jax.numpy as jnp
        import numpy as np
        D = 128
        H = 128
        E = 8
        K = 2
        I = 2 * 128
        ROUTE_SCALE = 1.0
        key = jax.random.key(seed)
        ks = jax.random.split(key, 12)
        s = lambda *sh: 1.0 / np.sqrt(sh[-1])
        return {'x': jax.random.normal(ks[0], (1, 256, D), jnp.float32), 'gate_w': jax.random.normal(ks[1], (E, D), jnp.float32) * s(E, D), 'w1': jax.random.normal(ks[2], (E, H, D), jnp.float32) * s(H, D), 'b1': jax.random.normal(ks[3], (E, H), jnp.float32) * 0.01, 'w2': jax.random.normal(ks[4], (E, D, H), jnp.float32) * s(D, H), 'b2': jax.random.normal(ks[5], (E, D), jnp.float32) * 0.01, 'w3': jax.random.normal(ks[6], (E, H, D), jnp.float32) * s(H, D), 'b3': jax.random.normal(ks[7], (E, H), jnp.float32) * 0.01, 'sw1': jax.random.normal(ks[8], (I, D), jnp.float32) * s(I, D), 'sw2': jax.random.normal(ks[9], (I, D), jnp.float32) * s(I, D), 'sw3': jax.random.normal(ks[10], (D, I), jnp.float32) * s(D, I)}
    _L0_ffn_in = _L0_ffn_setup()

    def _L1_attn_a_setup():
        import jax, jax.numpy as jnp
        import numpy as np
        D_MODEL = 128
        NHEAD = 16
        HEAD_DIM = D_MODEL // NHEAD
        NPOS_MAX = 125
        SEQ = 128
        BATCH = 4

        def _cope(query, attn_logits, pos_emb):
            gates = jax.nn.sigmoid(attn_logits)
            pos = jnp.cumsum(gates[..., ::-1], axis=-1)[..., ::-1]
            pos = jnp.minimum(pos, NPOS_MAX - 1)
            pos_ceil = jnp.ceil(pos).astype(jnp.int32)
            pos_floor = jnp.floor(pos).astype(jnp.int32)
            logits_int = jnp.einsum('hbsd,dn->hbsn', query, pos_emb[0])
            logits_ceil = jnp.take_along_axis(logits_int, pos_ceil, axis=-1)
            logits_floor = jnp.take_along_axis(logits_int, pos_floor, axis=-1)
            w = pos - pos_floor.astype(pos.dtype)
            return logits_ceil * w + logits_floor * (1.0 - w)
        key = jax.random.key(seed)
        ks = jax.random.split(key, 10)
        s = 0.02
        return {'x': jax.random.normal(ks[0], (SEQ, BATCH, D_MODEL), dtype=jnp.float32), 'Wq': jax.random.normal(ks[1], (D_MODEL, D_MODEL), dtype=jnp.float32) * s, 'bq': jnp.zeros((D_MODEL,), dtype=jnp.float32), 'Wk': jax.random.normal(ks[2], (D_MODEL, D_MODEL), dtype=jnp.float32) * s, 'bk': jnp.zeros((D_MODEL,), dtype=jnp.float32), 'Wv': jax.random.normal(ks[3], (D_MODEL, D_MODEL), dtype=jnp.float32) * s, 'bv': jnp.zeros((D_MODEL,), dtype=jnp.float32), 'Wo': jax.random.normal(ks[4], (D_MODEL, D_MODEL), dtype=jnp.float32) * s, 'bo': jnp.zeros((D_MODEL,), dtype=jnp.float32), 'pos_emb': jax.random.normal(ks[5], (1, HEAD_DIM, NPOS_MAX), dtype=jnp.float32) * s}
    _L1_attn_a_in = _L1_attn_a_setup()

    def _L1_attn_b_setup():
        import jax, jax.numpy as jnp
        import numpy as np

        def _phm(x, A, S, b):
            f = A.shape[0]
            din = f * S.shape[1]
            dout = f * S.shape[2]
            W = jnp.einsum('nij,nkl->ikjl', A, S).reshape(din, dout)
            return x @ W + b

        def _ln(x, g, b, eps=1e-05):
            mu = jnp.mean(x, axis=-1, keepdims=True)
            var = jnp.mean((x - mu) ** 2, axis=-1, keepdims=True)
            return (x - mu) * jax.lax.rsqrt(var + eps) * g + b
        key = jax.random.key(seed)
        ks = jax.random.split(key, 10)
        L, N, E, f = (256, 4, 128, 4)
        p = lambda k, sh: jax.random.normal(k, sh, jnp.float32) * 0.02
        return {'query': jax.random.normal(ks[0], (L, N, E), jnp.float32), 'qA': p(ks[1], (f, f, f)), 'qS': p(ks[2], (f, E // f, E // f)), 'qb': jnp.zeros((E,), jnp.float32), 'kA': p(ks[3], (f, f, f)), 'kS': p(ks[4], (f, E // f, E // f)), 'kb': jnp.zeros((E,), jnp.float32), 'vA': p(ks[5], (f, f, f)), 'vS': p(ks[6], (f, E // f, E // f)), 'vb': jnp.zeros((E,), jnp.float32), 'oA': p(ks[7], (f, f, f)), 'oS': p(ks[8], (f, E // f, E // f)), 'ob': jnp.zeros((E,), jnp.float32), 'g1': jnp.ones((E,), jnp.float32), 'b1': jnp.zeros((E,), jnp.float32), 'g2': jnp.ones((E,), jnp.float32), 'b2': jnp.zeros((E,), jnp.float32)}
    _L1_attn_b_in = _L1_attn_b_setup()

    def _L1_ffn_setup():
        import jax, jax.numpy as jnp
        import numpy as np
        DIM = 128
        DEPTH = 6
        HEADS = 16
        DIM_HEAD = 64
        WINDOW = 32
        INNER = HEADS * DIM_HEAD
        DIM_INNER = int(DIM * 4 * 2 / 3)
        QK_SCALE = 8.0

        def shift_tokens(t):
            a, s = jnp.split(t, 2, -1)
            s = jnp.pad(s, ((0, 0), (1, 0), (0, 0)))[:, :-1]
            return jnp.concatenate([a, s], -1)

        def l2norm(t):
            return t / jnp.maximum(jnp.linalg.norm(t, axis=-1, keepdims=True), 1e-12)

        def rotate_half(x):
            x1, x2 = jnp.split(x, 2, -1)
            return jnp.concatenate([-x2, x1], -1)

        def rotary_tables(n):
            half = jnp.arange(0, DIM_HEAD, 2, dtype=jnp.float32)
            inv_freq = 1.0 / 10000.0 ** (half / DIM_HEAD)
            t = jnp.arange(n, dtype=jnp.float32)
            freqs = t[:, None] * inv_freq[None, :]
            freqs = jnp.concatenate([freqs, freqs], -1)
            base_scale = (half + 0.4 * DIM_HEAD) / (1.4 * DIM_HEAD)
            power = (t - n // 2) / (WINDOW // 2)
            scale = base_scale[None, :] ** power[:, None]
            scale = jnp.concatenate([scale, scale], -1)
            return (freqs, scale)

        def local_attention(q, k, v):
            b, h, n, d = q.shape
            w = WINDOW
            nw = n // w
            bq = q.reshape(b, h, nw, w, d)
            bk = k.reshape(b, h, nw, w, d)
            bv = v.reshape(b, h, nw, w, d)

            def look(t):
                p = jnp.pad(t, ((0, 0), (0, 0), (1, 0), (0, 0), (0, 0)))
                return jnp.concatenate([p[:, :, :nw], p[:, :, 1:]], axis=3)
            bk2, bv2 = (look(bk), look(bv))
            seq = jnp.arange(n).reshape(nw, w)
            seq_p = jnp.pad(seq, ((1, 0), (0, 0)), constant_values=-1)
            jt = jnp.concatenate([seq_p[:nw], seq_p[1:]], axis=1)
            it = seq[:, :, None]
            jb = jt[:, None, :]
            mask = (it < jb) | (it > jb + w) | (jb == -1)
            sim = jnp.einsum('bhwie,bhwje->bhwij', bq, bk2) * QK_SCALE
            sim = jnp.where(mask, -jnp.finfo(sim.dtype).max, sim)
            attn = jax.nn.softmax(sim, -1)
            out = jnp.einsum('bhwij,bhwje->bhwie', attn, bv2)
            return out.reshape(b, h, n, d)

        def attn_layer(x, Wqkv, qs, ksc, Wo):
            b, n, _ = x.shape
            qkv = x @ Wqkv
            q, k, v = jnp.split(qkv, 3, -1)
            sh = lambda t: t.reshape(b, n, HEADS, DIM_HEAD).transpose(0, 2, 1, 3)
            q, k, v = (sh(q), sh(k), sh(v))
            q = l2norm(q) * qs
            k = l2norm(k) * ksc
            freqs, scale = rotary_tables(n)
            cos, sin = (jnp.cos(freqs), jnp.sin(freqs))
            q = q * cos * scale + rotate_half(q) * sin * scale
            inv = 1.0 / scale
            k = k * cos * inv + rotate_half(k) * sin * inv
            out = local_attention(q, k, v)
            out = out.transpose(0, 2, 1, 3).reshape(b, n, INNER)
            return out @ Wo

        def ffn_layer(x, g, bln, W1, b1, W2, b2):
            mu = x.mean(-1, keepdims=True)
            var = ((x - mu) ** 2).mean(-1, keepdims=True)
            xn = (x - mu) / jnp.sqrt(var + 1e-05) * g + bln
            hg = xn @ W1 + b1
            a, gate = jnp.split(hg, 2, -1)
            return a * jax.nn.gelu(gate, approximate=False) @ W2 + b2
        key = jax.random.key(seed)
        ks = jax.random.split(key, 8)
        B, N = (2, 256)
        init = lambda k, shape: jax.random.normal(k, shape, jnp.float32) * 0.02
        return {'x': jax.random.normal(ks[0], (B, N, DIM), jnp.float32), 'Wqkv': init(ks[1], (DEPTH, DIM, 3 * INNER)), 'q_scale': jnp.ones((DEPTH, DIM_HEAD), jnp.float32), 'k_scale': jnp.ones((DEPTH, DIM_HEAD), jnp.float32), 'Wo': init(ks[2], (DEPTH, INNER, DIM)), 'ln_g': jnp.ones((DEPTH, DIM), jnp.float32), 'ln_b': jnp.zeros((DEPTH, DIM), jnp.float32), 'W1': init(ks[3], (DEPTH, DIM, 2 * DIM_INNER)), 'b1': jnp.zeros((DEPTH, 2 * DIM_INNER), jnp.float32), 'W2': init(ks[4], (DEPTH, DIM_INNER, DIM)), 'b2': jnp.zeros((DEPTH, DIM), jnp.float32)}
    _L1_ffn_in = _L1_ffn_setup()
    _d = {'L0_attn_a_x': _L0_attn_a_in['x'], 'L0_attn_a_Wq': _L0_attn_a_in['Wq'], 'L0_attn_a_bq': _L0_attn_a_in['bq'], 'L0_attn_a_Wk': _L0_attn_a_in['Wk'], 'L0_attn_a_bk': _L0_attn_a_in['bk'], 'L0_attn_a_Wv': _L0_attn_a_in['Wv'], 'L0_attn_a_bv': _L0_attn_a_in['bv'], 'L0_attn_a_Wo': _L0_attn_a_in['Wo'], 'L0_attn_a_bo': _L0_attn_a_in['bo'], 'L0_attn_b_wqk': _L0_attn_b_in['wqk'], 'L0_attn_b_wov': _L0_attn_b_in['wov'], 'L0_ffn_gate_w': _L0_ffn_in['gate_w'], 'L0_ffn_w1': _L0_ffn_in['w1'], 'L0_ffn_b1': _L0_ffn_in['b1'], 'L0_ffn_w2': _L0_ffn_in['w2'], 'L0_ffn_b2': _L0_ffn_in['b2'], 'L0_ffn_w3': _L0_ffn_in['w3'], 'L0_ffn_b3': _L0_ffn_in['b3'], 'L0_ffn_sw1': _L0_ffn_in['sw1'], 'L0_ffn_sw2': _L0_ffn_in['sw2'], 'L0_ffn_sw3': _L0_ffn_in['sw3'], 'L1_attn_a_Wq': _L1_attn_a_in['Wq'], 'L1_attn_a_bq': _L1_attn_a_in['bq'], 'L1_attn_a_Wk': _L1_attn_a_in['Wk'], 'L1_attn_a_bk': _L1_attn_a_in['bk'], 'L1_attn_a_Wv': _L1_attn_a_in['Wv'], 'L1_attn_a_bv': _L1_attn_a_in['bv'], 'L1_attn_a_Wo': _L1_attn_a_in['Wo'], 'L1_attn_a_bo': _L1_attn_a_in['bo'], 'L1_attn_a_pos_emb': _L1_attn_a_in['pos_emb'], 'L1_attn_b_qA': _L1_attn_b_in['qA'], 'L1_attn_b_qS': _L1_attn_b_in['qS'], 'L1_attn_b_qb': _L1_attn_b_in['qb'], 'L1_attn_b_kA': _L1_attn_b_in['kA'], 'L1_attn_b_kS': _L1_attn_b_in['kS'], 'L1_attn_b_kb': _L1_attn_b_in['kb'], 'L1_attn_b_vA': _L1_attn_b_in['vA'], 'L1_attn_b_vS': _L1_attn_b_in['vS'], 'L1_attn_b_vb': _L1_attn_b_in['vb'], 'L1_attn_b_oA': _L1_attn_b_in['oA'], 'L1_attn_b_oS': _L1_attn_b_in['oS'], 'L1_attn_b_ob': _L1_attn_b_in['ob'], 'L1_attn_b_g1': _L1_attn_b_in['g1'], 'L1_attn_b_b1': _L1_attn_b_in['b1'], 'L1_attn_b_g2': _L1_attn_b_in['g2'], 'L1_attn_b_b2': _L1_attn_b_in['b2'], 'L1_ffn_Wqkv': _L1_ffn_in['Wqkv'], 'L1_ffn_q_scale': _L1_ffn_in['q_scale'], 'L1_ffn_k_scale': _L1_ffn_in['k_scale'], 'L1_ffn_Wo': _L1_ffn_in['Wo'], 'L1_ffn_ln_g': _L1_ffn_in['ln_g'], 'L1_ffn_ln_b': _L1_ffn_in['ln_b'], 'L1_ffn_W1': _L1_ffn_in['W1'], 'L1_ffn_b1': _L1_ffn_in['b1'], 'L1_ffn_W2': _L1_ffn_in['W2'], 'L1_ffn_b2': _L1_ffn_in['b2']}
    _x0 = _d['L0_attn_a_x']
    _d['L0_attn_a_x'] = jax.random.normal(jax.random.fold_in(jax.random.key(seed), 1), (2, 1024, 128), dtype=_x0.dtype)
    del _x0
    return _d

def reference(L0_attn_a_x, L0_attn_a_Wq, L0_attn_a_bq, L0_attn_a_Wk, L0_attn_a_bk, L0_attn_a_Wv, L0_attn_a_bv, L0_attn_a_Wo, L0_attn_a_bo, L0_attn_b_wqk, L0_attn_b_wov, L0_ffn_gate_w, L0_ffn_w1, L0_ffn_b1, L0_ffn_w2, L0_ffn_b2, L0_ffn_w3, L0_ffn_b3, L0_ffn_sw1, L0_ffn_sw2, L0_ffn_sw3, L1_attn_a_Wq, L1_attn_a_bq, L1_attn_a_Wk, L1_attn_a_bk, L1_attn_a_Wv, L1_attn_a_bv, L1_attn_a_Wo, L1_attn_a_bo, L1_attn_a_pos_emb, L1_attn_b_qA, L1_attn_b_qS, L1_attn_b_qb, L1_attn_b_kA, L1_attn_b_kS, L1_attn_b_kb, L1_attn_b_vA, L1_attn_b_vS, L1_attn_b_vb, L1_attn_b_oA, L1_attn_b_oS, L1_attn_b_ob, L1_attn_b_g1, L1_attn_b_b1, L1_attn_b_g2, L1_attn_b_b2, L1_ffn_Wqkv, L1_ffn_q_scale, L1_ffn_k_scale, L1_ffn_Wo, L1_ffn_ln_g, L1_ffn_ln_b, L1_ffn_W1, L1_ffn_b1, L1_ffn_W2, L1_ffn_b2):

    def _L0_attn_a_ref(x, Wq, bq, Wk, bk, Wv, bv, Wo, bo):
        import jax, jax.numpy as jnp
        import numpy as np
        import math
        WINDOW = 64
        N_HEAD = 16
        B, L, D = x.shape
        W, H = (WINDOW, N_HEAD)
        dh = D // H
        C = L // W
        scale = 1.0 / math.sqrt(dh)
        q = x @ Wq.T + bq
        k = x @ Wk.T + bk
        v = x @ Wv.T + bv
        kp = jnp.pad(k, ((0, 0), (W, 0), (0, 0)))
        vp = jnp.pad(v, ((0, 0), (W, 0), (0, 0)))
        idx = jnp.arange(C)[:, None] * W + jnp.arange(2 * W)[None, :]
        kc = kp[:, idx].reshape(B, C, 2 * W, H, dh)
        vc = vp[:, idx].reshape(B, C, 2 * W, H, dh)
        qc = q.reshape(B, C, W, H, dh)
        scores = jnp.einsum('bcqhd,bckhd->bchqk', qc, kc) * scale
        valid = idx >= W
        scores = jnp.where(valid[None, :, None, None, :], scores, jnp.float32(-1000000000.0))
        attn = jax.nn.softmax(scores, axis=-1)
        out = jnp.einsum('bchqk,bckhd->bcqhd', attn, vc).reshape(B, L, D)
        return out @ Wo.T + bo

    def _L0_attn_b_ref(x, wqk, wov):
        import jax, jax.numpy as jnp
        import numpy as np
        D_MODEL = 128
        b, n, d = x.shape
        mask = jnp.triu(jnp.full((n, n), -jnp.inf, dtype=x.dtype), k=1)
        q = jnp.einsum('bnd,de->bne', x, wqk)
        scores = jnp.einsum('bne,bme->bnm', q, x) + mask
        attn = jax.nn.softmax(scores, axis=-1)
        ctx = jnp.einsum('bnm,bmd->bnd', attn, x)
        return jnp.einsum('bnd,de->bne', ctx, wov)

    def _L0_ffn_ref(x, gate_w, w1, b1, w2, b2, w3, b3, sw1, sw2, sw3):
        import jax, jax.numpy as jnp
        import numpy as np
        D = 128
        H = 128
        E = 8
        K = 2
        I = 2 * 128
        ROUTE_SCALE = 1.0
        B, S, _ = x.shape
        xt = x.reshape(-1, D)
        logits = xt @ gate_w.T
        scores = jax.nn.softmax(logits.astype(jnp.float32), axis=-1)
        top_vals, idx = jax.lax.top_k(scores, K)
        weights = jnp.take_along_axis(scores, idx, axis=1).astype(x.dtype) * ROUTE_SCALE
        xs = xt[:, None, :] * weights[:, :, None]
        y = jnp.zeros_like(xt)
        for e in range(E):
            mask = (idx == e).astype(x.dtype)
            h = jax.nn.silu(jnp.einsum('tkd,hd->tkh', xs, w1[e]) + b1[e])
            x2 = jnp.einsum('tkh,dh->tkd', h, w2[e]) + b2[e]
            x3 = jnp.einsum('tkd,hd->tkh', xs, w3[e]) + b3[e]
            y = y + jnp.sum(x2 * x3 * mask[:, :, None], axis=1)
        z = jax.nn.silu(xt @ sw1.T) * (xt @ sw2.T) @ sw3.T
        return (y + z).reshape(B, S, D)

    def _L1_attn_a_ref(x, Wq, bq, Wk, bk, Wv, bv, Wo, bo, pos_emb):
        import jax, jax.numpy as jnp
        import numpy as np
        D_MODEL = 128
        NHEAD = 16
        HEAD_DIM = D_MODEL // NHEAD
        NPOS_MAX = 125
        SEQ = 128
        BATCH = 4

        def _cope(query, attn_logits, pos_emb):
            gates = jax.nn.sigmoid(attn_logits)
            pos = jnp.cumsum(gates[..., ::-1], axis=-1)[..., ::-1]
            pos = jnp.minimum(pos, NPOS_MAX - 1)
            pos_ceil = jnp.ceil(pos).astype(jnp.int32)
            pos_floor = jnp.floor(pos).astype(jnp.int32)
            logits_int = jnp.einsum('hbsd,dn->hbsn', query, pos_emb[0])
            logits_ceil = jnp.take_along_axis(logits_int, pos_ceil, axis=-1)
            logits_floor = jnp.take_along_axis(logits_int, pos_floor, axis=-1)
            w = pos - pos_floor.astype(pos.dtype)
            return logits_ceil * w + logits_floor * (1.0 - w)
        S, B, _ = x.shape

        def split_heads(t):
            return t.reshape(S, B, NHEAD, HEAD_DIM).transpose(2, 1, 0, 3)
        q = split_heads(x @ Wq + bq)
        k = split_heads(x @ Wk + bk)
        v = split_heads(x @ Wv + bv)
        scale = 1.0 / HEAD_DIM ** 0.5
        attn_logits = jnp.einsum('hbsd,hbtd->hbst', q, k) * scale
        attn_logits = attn_logits + _cope(q, attn_logits, pos_emb)
        attn = jax.nn.softmax(attn_logits, axis=-1)
        out = jnp.einsum('hbst,hbtd->hbsd', attn, v)
        out = out.transpose(2, 1, 0, 3).reshape(S, B, D_MODEL)
        return out @ Wo + bo

    def _L1_attn_b_ref(query, qA, qS, qb, kA, kS, kb, vA, vS, vb, oA, oS, ob, g1, b1, g2, b2):
        import jax, jax.numpy as jnp
        import numpy as np

        def _phm(x, A, S, b):
            f = A.shape[0]
            din = f * S.shape[1]
            dout = f * S.shape[2]
            W = jnp.einsum('nij,nkl->ikjl', A, S).reshape(din, dout)
            return x @ W + b

        def _ln(x, g, b, eps=1e-05):
            mu = jnp.mean(x, axis=-1, keepdims=True)
            var = jnp.mean((x - mu) ** 2, axis=-1, keepdims=True)
            return (x - mu) * jax.lax.rsqrt(var + eps) * g + b
        L, N, E = query.shape
        H = 16
        D = E // H
        eps = 1e-06
        key_raw = query
        val_raw = query
        qn = _ln(query, g1, b1)
        q = jax.nn.relu(_phm(qn, qA, qS, qb))
        k = jax.nn.relu(_phm(key_raw, kA, kS, kb))
        v = _phm(val_raw, vA, vS, vb)
        resh = lambda t: t.reshape(L, N * H, D).transpose(1, 0, 2)
        q, k, v = (resh(q), resh(k), resh(v))
        idx = np.pi / 2 * jnp.arange(1, L + 1, dtype=query.dtype)[None, :, None] / L
        s, c = (jnp.sin(idx), jnp.cos(idx))
        q_ = jnp.concatenate([q * s, q * c], axis=-1)
        k_ = jnp.concatenate([k * s, k * c], axis=-1)
        kv = jnp.einsum('nld,nlm->ndm', k_, v)
        z = 1.0 / jnp.maximum(jnp.einsum('nld,nd->nl', q_, k_.sum(axis=1)), eps)
        attn = jnp.einsum('nld,ndm->nlm', q_, kv) * z[..., None]
        attn = attn.transpose(1, 0, 2).reshape(L, N, E)
        attn = attn + qn
        out = _ln(attn, g2, b2)
        return _phm(out, oA, oS, ob) + out

    def _L1_ffn_ref(x, Wqkv, q_scale, k_scale, Wo, ln_g, ln_b, W1, b1, W2, b2):
        import jax, jax.numpy as jnp
        import numpy as np
        DIM = 128
        DEPTH = 6
        HEADS = 16
        DIM_HEAD = 64
        WINDOW = 32
        INNER = HEADS * DIM_HEAD
        DIM_INNER = int(DIM * 4 * 2 / 3)
        QK_SCALE = 8.0

        def shift_tokens(t):
            a, s = jnp.split(t, 2, -1)
            s = jnp.pad(s, ((0, 0), (1, 0), (0, 0)))[:, :-1]
            return jnp.concatenate([a, s], -1)

        def l2norm(t):
            return t / jnp.maximum(jnp.linalg.norm(t, axis=-1, keepdims=True), 1e-12)

        def rotate_half(x):
            x1, x2 = jnp.split(x, 2, -1)
            return jnp.concatenate([-x2, x1], -1)

        def rotary_tables(n):
            half = jnp.arange(0, DIM_HEAD, 2, dtype=jnp.float32)
            inv_freq = 1.0 / 10000.0 ** (half / DIM_HEAD)
            t = jnp.arange(n, dtype=jnp.float32)
            freqs = t[:, None] * inv_freq[None, :]
            freqs = jnp.concatenate([freqs, freqs], -1)
            base_scale = (half + 0.4 * DIM_HEAD) / (1.4 * DIM_HEAD)
            power = (t - n // 2) / (WINDOW // 2)
            scale = base_scale[None, :] ** power[:, None]
            scale = jnp.concatenate([scale, scale], -1)
            return (freqs, scale)

        def local_attention(q, k, v):
            b, h, n, d = q.shape
            w = WINDOW
            nw = n // w
            bq = q.reshape(b, h, nw, w, d)
            bk = k.reshape(b, h, nw, w, d)
            bv = v.reshape(b, h, nw, w, d)

            def look(t):
                p = jnp.pad(t, ((0, 0), (0, 0), (1, 0), (0, 0), (0, 0)))
                return jnp.concatenate([p[:, :, :nw], p[:, :, 1:]], axis=3)
            bk2, bv2 = (look(bk), look(bv))
            seq = jnp.arange(n).reshape(nw, w)
            seq_p = jnp.pad(seq, ((1, 0), (0, 0)), constant_values=-1)
            jt = jnp.concatenate([seq_p[:nw], seq_p[1:]], axis=1)
            it = seq[:, :, None]
            jb = jt[:, None, :]
            mask = (it < jb) | (it > jb + w) | (jb == -1)
            sim = jnp.einsum('bhwie,bhwje->bhwij', bq, bk2) * QK_SCALE
            sim = jnp.where(mask, -jnp.finfo(sim.dtype).max, sim)
            attn = jax.nn.softmax(sim, -1)
            out = jnp.einsum('bhwij,bhwje->bhwie', attn, bv2)
            return out.reshape(b, h, n, d)

        def attn_layer(x, Wqkv, qs, ksc, Wo):
            b, n, _ = x.shape
            qkv = x @ Wqkv
            q, k, v = jnp.split(qkv, 3, -1)
            sh = lambda t: t.reshape(b, n, HEADS, DIM_HEAD).transpose(0, 2, 1, 3)
            q, k, v = (sh(q), sh(k), sh(v))
            q = l2norm(q) * qs
            k = l2norm(k) * ksc
            freqs, scale = rotary_tables(n)
            cos, sin = (jnp.cos(freqs), jnp.sin(freqs))
            q = q * cos * scale + rotate_half(q) * sin * scale
            inv = 1.0 / scale
            k = k * cos * inv + rotate_half(k) * sin * inv
            out = local_attention(q, k, v)
            out = out.transpose(0, 2, 1, 3).reshape(b, n, INNER)
            return out @ Wo

        def ffn_layer(x, g, bln, W1, b1, W2, b2):
            mu = x.mean(-1, keepdims=True)
            var = ((x - mu) ** 2).mean(-1, keepdims=True)
            xn = (x - mu) / jnp.sqrt(var + 1e-05) * g + bln
            hg = xn @ W1 + b1
            a, gate = jnp.split(hg, 2, -1)
            return a * jax.nn.gelu(gate, approximate=False) @ W2 + b2
        for i in range(DEPTH):
            x = attn_layer(shift_tokens(x), Wqkv[i], q_scale[i], k_scale[i], Wo[i]) + x
            x = ffn_layer(shift_tokens(x), ln_g[i], ln_b[i], W1[i], b1[i], W2[i], b2[i]) + x
        return x
    x = L0_attn_a_x
    x = x + _L0_attn_a_ref(_layernorm(x, axis=-1), L0_attn_a_Wq, L0_attn_a_bq, L0_attn_a_Wk, L0_attn_a_bk, L0_attn_a_Wv, L0_attn_a_bv, L0_attn_a_Wo, L0_attn_a_bo)
    x = x + _L0_ffn_ref(_layernorm(x, axis=-1), L0_ffn_gate_w, L0_ffn_w1, L0_ffn_b1, L0_ffn_w2, L0_ffn_b2, L0_ffn_w3, L0_ffn_b3, L0_ffn_sw1, L0_ffn_sw2, L0_ffn_sw3)
    x = x + _L0_attn_b_ref(_layernorm(x, axis=-1), L0_attn_b_wqk, L0_attn_b_wov)
    x = x + _L0_ffn_ref(_layernorm(x, axis=-1), L0_ffn_gate_w, L0_ffn_w1, L0_ffn_b1, L0_ffn_w2, L0_ffn_b2, L0_ffn_w3, L0_ffn_b3, L0_ffn_sw1, L0_ffn_sw2, L0_ffn_sw3)
    x = x + _L1_attn_a_ref(_layernorm(x, axis=-1), L1_attn_a_Wq, L1_attn_a_bq, L1_attn_a_Wk, L1_attn_a_bk, L1_attn_a_Wv, L1_attn_a_bv, L1_attn_a_Wo, L1_attn_a_bo, L1_attn_a_pos_emb)
    x = x + _L1_ffn_ref(_layernorm(x, axis=-1), L1_ffn_Wqkv, L1_ffn_q_scale, L1_ffn_k_scale, L1_ffn_Wo, L1_ffn_ln_g, L1_ffn_ln_b, L1_ffn_W1, L1_ffn_b1, L1_ffn_W2, L1_ffn_b2)
    x = x + _L1_attn_b_ref(_layernorm(x, axis=-1), L1_attn_b_qA, L1_attn_b_qS, L1_attn_b_qb, L1_attn_b_kA, L1_attn_b_kS, L1_attn_b_kb, L1_attn_b_vA, L1_attn_b_vS, L1_attn_b_vb, L1_attn_b_oA, L1_attn_b_oS, L1_attn_b_ob, L1_attn_b_g1, L1_attn_b_b1, L1_attn_b_g2, L1_attn_b_b2)
    x = x + _L1_ffn_ref(_layernorm(x, axis=-1), L1_ffn_Wqkv, L1_ffn_q_scale, L1_ffn_k_scale, L1_ffn_Wo, L1_ffn_ln_g, L1_ffn_ln_b, L1_ffn_W1, L1_ffn_b1, L1_ffn_W2, L1_ffn_b2)
    return x

_drawn_inputs = setup_inputs


def setup_inputs(seed=0):
    import zlib

    import numpy as np

    out = dict(_drawn_inputs(seed))
    spreads = {'L0_attn_a_bq': (0.0, 0.8),
     'L0_attn_a_bk': (0.0, 2.0),
     'L0_attn_a_bv': (0.0, 0.1),
     'L0_attn_a_bo': (0.0, 0.1),
     'L1_attn_a_bq': (0.0, 2.0),
     'L1_attn_a_bk': (0.0, 2.0),
     'L1_attn_a_bv': (0.0, 0.502),
     'L1_attn_a_bo': (0.0, 0.1),
     'L1_attn_b_qb': (0.0, 0.742),
     'L1_attn_b_kb': (0.0, 1.785),
     'L1_attn_b_vb': (0.0, 0.303),
     'L1_attn_b_ob': (0.0, 0.302),
     'L1_attn_b_g1': (1.0, 0.2),
     'L1_attn_b_b1': (0.0, 0.297),
     'L1_attn_b_g2': (1.0, 0.2),
     'L1_attn_b_b2': (0.0, 0.316),
     'L1_ffn_q_scale': (1.0, 0.6),
     'L1_ffn_k_scale': (1.0, 0.6),
     'L1_ffn_ln_g': (1.0, 0.6),
     'L1_ffn_ln_b': (0.0, 0.8),
     'L1_ffn_b1': (0.0, 0.767),
     'L1_ffn_b2': (0.0, 0.1)}
    factors = {'L0_attn_a_Wq': 8.0,
     'L0_attn_a_Wk': 8.0,
     'L0_attn_a_Wv': 8.0,
     'L0_ffn_b1': 8.0,
     'L0_ffn_b2': 8.0,
     'L0_ffn_b3': 8.0,
     'L1_attn_a_Wq': 24.865,
     'L1_attn_a_Wk': 23.78,
     'L1_attn_a_pos_emb': 64.0,
     'L1_attn_b_qA': 8.0,
     'L1_attn_b_qS': 8.0,
     'L1_attn_b_kA': 8.0,
     'L1_attn_b_kS': 8.0,
     'L1_attn_b_vA': 8.0,
     'L1_attn_b_vS': 8.0,
     'L1_attn_b_oA': 8.0,
     'L1_attn_b_oS': 8.0,
     'L1_ffn_W1': 2.968,
     'L1_ffn_W2': 2.909}
    for name, (base, spread) in spreads.items():
        noise = np.random.default_rng([zlib.crc32(name.encode()), seed]).standard_normal(out[name].shape)
        drawn = base * np.exp(spread * noise) if base else spread * noise
        out[name] = jnp.asarray(drawn.astype(out[name].dtype))
    for name, factor in factors.items():
        out[name] = (out[name] * factor).astype(out[name].dtype)
    return out
```

```python
from contextlib import ExitStack

import numpy as np

import concourse.bass as bass
from concourse import mybir

F32 = mybir.dt.float32
ALU = mybir.AluOpType
ACT = mybir.ActivationFunctionType
AX = mybir.AxisListType.X

P = 128
B, L, D = 2, 1024, 128
NT = B * L // P
TB = L // P
NG = NT // 4
EPS = 1e-5
NEG = -3.0e38

A_WIN, A_H, A_DH = 64, 16, 8
E_N, I_SH = 8, 256
H, DH = 16, 8
DEPTH, LH, LD, LW = 6, 16, 64, 32
INNER = LH * LD
HID = int(D * 4 * 2 / 3)
HCH = [128, 128, HID - 256]


class Lane:

    def __init__(self, engine, sem, step=1):
        self.engine, self.sem, self.step = engine, sem, step
        self.reset()

    def reset(self):
        self.count = 0
        self.seen = {}

    def after(self, *marks):
        for lane, value in marks:
            if self.seen.get(lane.sem.num, 0) < value:
                self.engine.wait_ge(lane.sem, value)
                self.seen[lane.sem.num] = value

    def mark(self, instruction):
        self.count += self.step
        instruction.then_inc(self.sem, self.step)
        return self, self.count


def over(ap, axis, shape):
    return ap.unsqueeze(axis).to_broadcast(shape)


def build(nc, t, out):
    ctx = ExitStack()
    with ctx:
        def sb(name, *shape):
            return ctx.enter_context(nc.sbuf_tensor(name, list(shape), F32))

        names = ["pe_done", "dve_done", "act_done", "pool_done", "load_done", "v_done", "halo_done"]
        sems = [ctx.enter_context(nc.semaphore(n)) for n in names]
        assert [s.num for s in sems] == list(range(sems[0].num, sems[0].num + len(sems)))
        T = Lane(nc.tensor, sems[0])
        V = Lane(nc.vector, sems[1])
        A = Lane(nc.scalar, sems[2])
        G = Lane(nc.gpsimd, sems[3])
        LOAD = Lane(nc.sync, sems[4], 16)
        VDMA = Lane(nc.sync, sems[5], 16)
        HALO = Lane(nc.sync, sems[6], 16)
        lanes = [T, V, A, G, LOAD, VDMA, HALO]
        te, ve, ac, gp, sp = nc.tensor, nc.vector, nc.scalar, nc.gpsimd, nc.sync

        def fence():
            nc.all_engine_barrier(sems_to_clear=range(sems[0].num, sems[-1].num + 1))
            for lane in lanes:
                lane.reset()

        PS = ctx.enter_context(nc.psum_tensor("PS", [P, 8, 512], F32))

        def flat(a, b):
            return PS[:, a:b, :].rearrange("p a b -> p (a b)")

        X = sb("X", P, NT, D)
        ident = sb("ident", P, P)
        mean_mat = sb("mean_mat", P, P)
        XNT = sb("XNT", P, A_WIN + NT * P)
        XN = sb("XN", P, NT, D)
        xn4 = sb("xn4", P, 4, D)
        xT4 = sb("xT4", P, 4 * P)
        stats = sb("stats", P, 4, 6)
        meanvar = sb("meanvar", P, 4, 2)
        rstd = sb("rstd", P, 4)
        minus_half = sb("minus_half", P, 2 * H)
        ones_mat = sb("ones_mat", P, P)

        def load(dst, src):
            return LOAD.mark(sp.dma_start(dst, src))

        def row(name, n):
            return t[name].rearrange("(a n) -> a n", a=1).to_broadcast([P, n])

        def column(name):
            return t[name].rearrange("(n a) -> n a", a=1)

        load(X[:, :, :], t["x"].rearrange("b (i p) d -> p (b i) d", p=P))
        load(ident[:, :], t["ident"])
        m = load(mean_mat[:, :], t["mean_mat"])
        G.mark(gp.memset(minus_half[:, :], -0.5))
        G.mark(gp.memset(ones_mat[:, :], 1.0))
        G.after(G.mark(gp.memset(XNT[:, 0:A_WIN], 0.0)))
        sp.wait_ge(LOAD.sem, LOAD.count)
        fence()

        def inverse_root(ap, n):
            return G.mark(gp.tensor_tensor(ap, ap, minus_half[:, 0:n], ALU.pow))

        def transpose4(src, bank, dst, before=()):
            T.after(*before)
            for j in range(4):
                m = T.mark(te.transpose(PS[:, bank, j * P:(j + 1) * P], src[:, j, :], ident[:, :]))
            A.after(m)
            return A.mark(ac.copy(dst, PS[:, bank, :]))

        def norm_loop(src, hook, gain=None, shift=None, keep=None, keep_t=True):
            with nc.Fori(0, NG) as g:
                for j in range(4):
                    m = V.mark(ve.bn_stats(stats[:, j, :], src[:, bass.ds(4 * g + j, 1), :].rearrange("p a d -> p (a d)")))
                V.after(m)
                for j in range(4):
                    m = V.mark(ve.bn_aggr(meanvar[:, j, :], stats[:, j, :]))
                V.after(m)
                G.after(V.mark(ve.tensor_scalar(rstd[:, :], meanvar[:, :, 1], EPS, None, ALU.add)))
                V.after(inverse_root(rstd[:, :], 4))
                for j in range(4):
                    m = V.mark(ve.tensor_scalar(xn4[:, j, :], src[:, bass.ds(4 * g + j, 1), :].rearrange("p a d -> p (a d)"),
                                                meanvar[:, j, 0:1], rstd[:, j:j + 1], ALU.subtract, ALU.mult))
                if gain is not None:
                    V.after(m)
                    m = V.mark(ve.tensor_tensor(xn4[:, :, :], xn4[:, :, :], over(gain[:, :], 1, [P, 4, D]), ALU.mult))
                    V.after(m)
                    m = V.mark(ve.tensor_tensor(xn4[:, :, :], xn4[:, :, :], over(shift[:, :], 1, [P, 4, D]), ALU.add))
                turned = transpose4(xn4, 0, xT4[:, :], [m])
                if keep is not None:
                    G.after(m)
                    G.mark(gp.tensor_copy(keep[:, bass.ds(4 * g, 4), :], xn4[:, :, :]))
                if keep_t:
                    G.after(turned)
                    G.mark(gp.tensor_copy(XNT[:, bass.ds(g * 512 + A_WIN, 512)], xT4[:, :]))
                hook(g, m, turned)
                fence()

        def project_loop(src, w, bias):
            with nc.Fori(0, NG) as g:
                m = G.mark(gp.tensor_copy(xn4[:, :, :], src[:, bass.ds(4 * g, 4), :]))
                b = G.mark(gp.tensor_tensor(X[:, bass.ds(4 * g, 4), :], X[:, bass.ds(4 * g, 4), :],
                                            over(bias, 1, [P, 4, D]), ALU.add))
                m = transpose4(xn4, 0, xT4[:, :], [m])
                T.after(m)
                for j in range(4):
                    m = T.mark(te.matmul(PS[:, 1, j * P:(j + 1) * P], xT4[:, j * P:(j + 1) * P], w, start=True, stop=True))
                V.after(m, b)
                xg = X[:, bass.ds(4 * g, 4), :]
                V.mark(ve.tensor_tensor(xg, PS[:, 1, :].rearrange("p (j d) -> p j d", j=4), xg, ALU.add))
                fence()

        def window_attention():
            with ExitStack() as own:
                def sl(name, *shape):
                    return own.enter_context(nc.sbuf_tensor("a_" + name, list(shape), F32))
                wq, wk, wv, wo = (sl(n, P, D) for n in ("wq", "wk", "wv", "wo"))
                bq, bk = sl("bq", P, 1), sl("bk", P, 1)
                bv, bo = sl("bv", P, D), sl("bo", P, D)
                headmask = sl("headmask", P, A_H)
                pad = sl("pad", P, NT)
                xw = sl("xw", P, A_WIN + P)
                qT = sl("qT", P, P)
                kT = sl("kT", P, A_WIN + P)
                kTm = sl("kTm", P, A_H, A_WIN + P)
                vc = sl("vc", P, 2, D)
                S = sl("S", P, A_H, P)
                pT = sl("pT", P, A_H, P)
                mx, sm, rs = sl("mx", P, A_H), sl("sm", P, A_H), sl("rs", P, A_H)
                o, oT = sl("o", P, D), sl("oT", P, P)
                for w, n in ((wq, "a_wqT"), (wk, "a_wkT"), (wv, "a_wvT"), (wo, "a_woT"),
                             (headmask, "a_headmask"), (pad, "a_pad")):
                    load(w[:, :], t[n])
                load(bq[:, :], column("a_bq"))
                load(bk[:, :], column("a_bk"))
                load(bv[:, :], row("a_bv", D))
                load(bo[:, :], row("a_bo", D))
                sp.wait_ge(LOAD.sem, LOAD.count)
                fence()
                norm_loop(X, lambda g, m, turned: None)
                with nc.Fori(0, NT) as i:
                    xin = G.mark(gp.tensor_copy(xw[:, :], XNT[:, bass.ds(i * P, A_WIN + P)]))
                    bias = G.mark(gp.tensor_tensor(X[:, bass.ds(i, 1), :], X[:, bass.ds(i, 1), :],
                                                   over(bo[:, :], 1, [P, 1, D]), ALU.add))
                    T.after(xin)
                    te.matmul(PS[:, 0, 0:P], wq[:, :], xw[:, A_WIN:], start=True, stop=True)
                    qk = T.mark(te.matmul(PS[:, 0, P:2 * P + A_WIN], wk[:, :], xw[:, :], start=True, stop=True))
                    for c in range(2):
                        v = T.mark(te.matmul(PS[:, 1, c * P:(c + 1) * P], xw[:, A_WIN * c:A_WIN * c + P], wv[:, :],
                                             start=True, stop=True))
                    A.after(qk)
                    k = A.mark(ac.activation(kT[:, :], PS[:, 0, P:2 * P + A_WIN], ACT.Identity, bias=bk[:, 0:1]))
                    q = A.mark(ac.activation(qT[:, :], PS[:, 0, 0:P], ACT.Identity, bias=bq[:, 0:1]))
                    V.after(k)
                    W_K = A_WIN + P
                    km = V.mark(ve.tensor_tensor(kTm[:, 0:10, :], over(kT[:, :], 1, [P, 10, W_K]),
                                                 over(headmask[:, 0:10], 2, [P, 10, W_K]), ALU.mult))
                    G.after(k)
                    km2 = G.mark(gp.tensor_tensor(kTm[:, 10:, :], over(kT[:, :], 1, [P, A_H - 10, W_K]),
                                                  over(headmask[:, 10:], 2, [P, A_H - 10, W_K]), ALU.mult))
                    V.after(v)
                    vc_in = V.mark(ve.tensor_tensor(vc[:, :, :], PS[:, 1, 0:2 * D].rearrange("p (c d) -> p c d", c=2),
                                                    over(bv[:, :], 1, [P, 2, D]), ALU.add))
                    T.after(q, km)
                    for n in range(4):
                        if n == 2:
                            T.after(km2)
                        for c in range(2):
                            s = T.mark(te.matmul(PS[A_WIN * c:A_WIN * (c + 1), 4 + n, :], qT[:, A_WIN * c:A_WIN * (c + 1)],
                                                 kTm[:, 4 * n:4 * n + 4, A_WIN * c:A_WIN * c + P], start=True, stop=True))
                    first = PS[0:A_WIN, 4:8, :].rearrange("p b (h k) -> p (b h) k", k=P)[:, :, 0:A_WIN]
                    V.after(s)
                    V.after(V.mark(ve.tensor_scalar(first, first, pad[0:A_WIN, bass.ds(i, 1)], None, ALU.add)))
                    scores = PS[:, 4:8, :].rearrange("p b (h k) -> p (b h) k", k=P)
                    V.after(V.mark(ve.tensor_reduce(mx[:, :], scores, AX, ALU.max)))
                    exps = []
                    for n in range(4):
                        sh = S[:, 4 * n:4 * n + 4, :]
                        m = V.mark(ve.tensor_tensor(sh, scores[:, 4 * n:4 * n + 4, :],
                                                    over(mx[:, 4 * n:4 * n + 4], 2, [P, 4, P]), ALU.subtract))
                        A.after(m)
                        exps.append(A.mark(ac.activation(sh, sh, ACT.Exp, scale=float(A_DH) ** -0.5)))
                    T.after(k, v, vc_in)
                    turned = []
                    for n in range(4):
                        T.after(exps[n])
                        for h in range(4 * n, 4 * n + 4):
                            m = T.mark(te.transpose(PS[:, n, (h % 4) * P:(h % 4 + 1) * P], S[:, h, :], ident[:, :]))
                        A.after(m)
                        turned.append(A.mark(ac.copy(pT[:, 4 * n:4 * n + 4, :].rearrange("p a b -> p (a b)"), PS[:, n, :])))
                    V.after(*exps)
                    V.after(V.mark(ve.tensor_reduce(sm[:, :], S[:, :, :], AX, ALU.add)))
                    rsm = V.mark(ve.reciprocal(rs[:, :], sm[:, :]))
                    for h in range(A_H):
                        T.after(turned[h // 4])
                        for c in range(2):
                            m = T.mark(te.matmul(PS[A_WIN * c:A_WIN * (c + 1), 4, h * A_DH:(h + 1) * A_DH],
                                                 pT[:, h, A_WIN * c:A_WIN * (c + 1)], vc[:, c, h * A_DH:(h + 1) * A_DH],
                                                 start=True, stop=True))
                    V.after(m, rsm)
                    m = V.mark(ve.tensor_tensor(o[:, :].rearrange("p (h d) -> p h d", h=A_H),
                                                PS[:, 4, 0:D].rearrange("p (h d) -> p h d", h=A_H),
                                                over(rs[:, :], 2, [P, A_H, A_DH]), ALU.mult))
                    T.after(m)
                    m = T.mark(te.transpose(PS[:, 5, 0:P], o[:, :], ident[:, :]))
                    A.after(m)
                    m = A.mark(ac.copy(oT[:, :], PS[:, 5, 0:P]))
                    T.after(m)
                    m = T.mark(te.matmul(PS[:, 6, 0:D], oT[:, :], wo[:, :], start=True, stop=True))
                    V.after(m, bias)
                    xi = X[:, bass.ds(i, 1), :].rearrange("p a d -> p (a d)")
                    V.mark(ve.tensor_tensor(xi, PS[:, 6, 0:D], xi, ALU.add))
                    fence()

        def mixture(tag):
            with ExitStack() as own:
                def sl(name, *shape):
                    return own.enter_context(nc.sbuf_tensor(tag + name, list(shape), F32))
                gate = sl("gate", P, E_N)
                w13 = sl("w13", P, E_N, 2, D)
                w2 = sl("w2", P, E_N, D)
                b1, b2, b3 = (sl(n, P, E_N, D) for n in ("b1", "b2", "b3"))
                sw12 = sl("sw12", P, 2 * I_SH)
                sw3 = sl("sw3", P, 2, D)
                lower = sl("lower", P, E_N, E_N)
                sc = sl("sc", P, NT, E_N)
                mask = sl("mask", P, NT, E_N)
                r1 = sl("r1", P, NT)
                gt, eq = sl("gt", P, NT, E_N * E_N), sl("eq", P, NT, E_N * E_N)
                xt = sl("xt", P, P)
                hin, x3, hT, y8 = (sl(n, P, E_N, D) for n in ("hin", "x3", "hT", "y8"))
                sg, sT, y1 = sl("sg", P, I_SH), sl("sT", P, I_SH), sl("y1", P, D)
                load(gate[:, :], t["f_gateT"])
                load(w13[:, :, 0, :], t["f_w1T"].rearrange("e d h -> d e h"))
                load(w13[:, :, 1, :], t["f_w3T"].rearrange("e d h -> d e h"))
                load(w2[:, :, :], t["f_w2T"].rearrange("e h d -> h e d"))
                for b, n in ((b1, "f_b1"), (b2, "f_b2"), (b3, "f_b3")):
                    load(b[:, :, :].rearrange("p e d -> p (e d)"),
                         t[n].rearrange("e d -> (e d)").rearrange("(a n) -> a n", a=1).to_broadcast([P, E_N * D]))
                load(sw12[:, :], t["f_sw12T"])
                load(sw3[:, :, :], t["f_sw3T"].rearrange("(c p) d -> p c d", p=P))
                load(lower[:, :, :].rearrange("p a b -> p (a b)"), row("f_lower", E_N * E_N))
                sp.wait_ge(LOAD.sem, LOAD.count)
                fence()

                def gates(g, m, turned):
                    T.after(turned)
                    for j in range(4):
                        m = T.mark(te.matmul(PS[:, 1, j * E_N:(j + 1) * E_N], xT4[:, j * P:(j + 1) * P], gate[:, :],
                                             start=True, stop=True))
                    V.after(m)
                    V.mark(ve.tensor_copy(sc[:, bass.ds(4 * g, 4), :],
                                          PS[:, 1, 0:4 * E_N].rearrange("p (j e) -> p j e", j=4)))

                norm_loop(X, gates)
                all3 = [P, NT, E_N]
                V.after(V.mark(ve.tensor_reduce(r1[:, :], sc[:, :, :], AX, ALU.max)))
                m = V.mark(ve.tensor_tensor(sc[:, :, :], sc[:, :, :], over(r1[:, :], 2, all3), ALU.subtract))
                A.after(m)
                m = A.mark(ac.activation(sc[:, :, :], sc[:, :, :], ACT.Exp))
                V.after(m)
                V.after(V.mark(ve.tensor_reduce(r1[:, :], sc[:, :, :], AX, ALU.add)))
                V.after(V.mark(ve.reciprocal(r1[:, :], r1[:, :])))
                V.after(V.mark(ve.tensor_tensor(sc[:, :, :], sc[:, :, :], over(r1[:, :], 2, all3), ALU.mult)))
                four = [P, NT, E_N, E_N]
                gt4 = gt[:, :, :].rearrange("p t (a b) -> p t a b", a=E_N)
                eq4 = eq[:, :, :].rearrange("p t (a b) -> p t a b", a=E_N)
                rival, own_s = over(sc[:, :, :], 2, four), over(sc[:, :, :], 3, four)
                V.mark(ve.tensor_tensor(gt4, rival, own_s, ALU.is_gt))
                V.after(V.mark(ve.tensor_tensor(eq4, rival, own_s, ALU.is_equal)))
                V.after(V.mark(ve.tensor_tensor(eq[:, :, :], eq[:, :, :],
                                                over(lower[:, :, :].rearrange("p a b -> p (a b)"), 1, [P, NT, E_N * E_N]),
                                                ALU.mult)))
                V.after(V.mark(ve.tensor_tensor(gt[:, :, :], gt[:, :, :], eq[:, :, :], ALU.add)))
                V.after(V.mark(ve.tensor_reduce(mask[:, :, :], gt4, AX, ALU.add)))
                V.mark(ve.tensor_scalar(mask[:, :, :], mask[:, :, :], 1.5, None, ALU.is_lt))
                fence()
                with nc.Fori(0, NT) as i:
                    xin = G.mark(gp.tensor_copy(xt[:, :], XNT[:, bass.ds(i * P + A_WIN, P)]))
                    T.after(xin)
                    z12 = T.mark(te.matmul(PS[:, 7, :], xt[:, :], sw12[:, :], start=True, stop=True))
                    u = [T.mark(te.matmul(PS[:, n, :], xt[:, :],
                                          w13[:, 2 * n:2 * n + 2, :, :].rearrange("p e k h -> p (e k h)"),
                                          start=True, stop=True)) for n in range(4)]
                    A.after(z12)
                    m = A.mark(ac.activation(sg[:, :], PS[:, 7, 0:I_SH], ACT.Silu))
                    V.after(m)
                    zs = V.mark(ve.tensor_tensor(sg[:, :], sg[:, :], PS[:, 7, I_SH:], ALU.mult))
                    hs, x3s = [], []
                    for e in range(E_N):
                        V.after(u[e // 2])
                        s = sc[:, bass.ds(i, 1), e:e + 1].rearrange("p a e -> p (a e)")
                        m = V.mark(ve.scalar_tensor_tensor(hin[:, e, :], PS[:, e // 2, (e % 2) * 256:(e % 2) * 256 + D],
                                                           s, b1[:, e, :], ALU.mult, ALU.add))
                        x3s.append(V.mark(ve.scalar_tensor_tensor(
                            x3[:, e, :], PS[:, e // 2, (e % 2) * 256 + D:(e % 2) * 256 + 2 * D],
                            s, b3[:, e, :], ALU.mult, ALU.add)))
                        if e % 2:
                            A.after(m)
                            hs.append(A.mark(ac.activation(hin[:, e - 1:e + 1, :], hin[:, e - 1:e + 1, :], ACT.Silu)))
                    G.after(x3s[-1])
                    x3m = G.mark(gp.tensor_tensor(x3[:, :, :], x3[:, :, :],
                                                  over(mask[:, bass.ds(i, 1), :].rearrange("p a e -> p (a e)"), 2, [P, E_N, D]),
                                                  ALU.mult))
                    T.after(zs)
                    for j in range(2):
                        m = T.mark(te.transpose(PS[:, 4, j * P:(j + 1) * P], sg[:, j * P:(j + 1) * P], ident[:, :]))
                    A.after(m)
                    sTm = A.mark(ac.copy(sT[:, :], PS[:, 4, 0:I_SH]))
                    T.after(sTm)
                    for j in range(2):
                        z = T.mark(te.matmul(PS[:, 7, 0:D], sT[:, j * P:(j + 1) * P], sw3[:, j, :], start=(j == 0), stop=(j == 1)))
                    xi = X[:, bass.ds(i, 1), :].rearrange("p a d -> p (a d)")
                    V.after(z)
                    xz = V.mark(ve.tensor_tensor(xi, PS[:, 7, 0:D], xi, ALU.add))
                    for n in range(2):
                        T.after(hs[2 * n + 1], sTm)
                        for e in range(4 * n, 4 * n + 4):
                            m = T.mark(te.transpose(PS[:, 4 + n, (e % 4) * P:(e % 4 + 1) * P], hin[:, e, :], ident[:, :]))
                        A.after(m)
                        m = A.mark(ac.copy(hT[:, 4 * n:4 * n + 4, :].rearrange("p a b -> p (a b)"), PS[:, 4 + n, :]))
                        T.after(m, xz)
                        for e in range(4 * n, 4 * n + 4):
                            m = T.mark(te.matmul(PS[:, 6 + n, (e % 4) * D:(e % 4 + 1) * D], hT[:, e, :], w2[:, e, :],
                                                 start=True, stop=True))
                        V.after(m)
                        half = y8[:, 4 * n:4 * n + 4, :]
                        V.after(V.mark(ve.tensor_tensor(half, PS[:, 6 + n, :].rearrange("p (e d) -> p e d", e=4),
                                                        b2[:, 4 * n:4 * n + 4, :], ALU.add)))
                        V.after(x3m)
                        m = V.mark(ve.tensor_tensor(half, half, x3[:, 4 * n:4 * n + 4, :], ALU.mult))
                    V.after(m)
                    V.after(V.mark(ve.tensor_reduce(y1[:, :], y8[:, :, :].rearrange("p e d -> p d e"), AX, ALU.add)))
                    V.mark(ve.tensor_tensor(xi, xi, y1[:, :], ALU.add))
                    fence()

        def causal_attention():
            with ExitStack() as own:
                def sl(name, *shape):
                    return own.enter_context(nc.sbuf_tensor("b_" + name, list(shape), F32))
                wqk, wov = sl("wqk", P, D), sl("wov", P, D)
                future = sl("future", P, 2 * L - P)
                QT = sl("QT", P, NT * P)
                XV = sl("XV", P, NT, D)
                q, S, pT = sl("q", P, P), sl("S", P, L), sl("pT", P, L)
                mx, nmx, sm, rs = (sl(n, P, 1) for n in ("mx", "nmx", "sm", "rs"))
                for w, n in ((wqk, "b_wqk"), (wov, "b_wov"), (future, "b_future")):
                    load(w[:, :], t[n])
                sp.wait_ge(LOAD.sem, LOAD.count)
                fence()

                def products(g, m, turned):
                    T.after(turned)
                    m = T.mark(te.matmul(PS[:, 1, :], wqk[:, :], xT4[:, :], start=True, stop=True))
                    V.after(m)
                    V.mark(ve.tensor_copy(QT[:, bass.ds(g * 512, 512)], PS[:, 1, :]))
                    for j in range(4):
                        m = T.mark(te.matmul(PS[:, 2, j * D:(j + 1) * D], xT4[:, j * P:(j + 1) * P], wov[:, :],
                                             start=True, stop=True))
                    V.after(m)
                    V.mark(ve.tensor_copy(XV[:, bass.ds(4 * g, 4), :], PS[:, 2, :].rearrange("p (j d) -> p j d", j=4)))

                norm_loop(X, products)
                with nc.Fori(0, B) as b:
                    with nc.Fori(0, TB) as i:
                        m = G.mark(gp.tensor_copy(q[:, :], QT[:, bass.ds(b * L + i * P, P)]))
                        T.after(m)
                        for n in range(2):
                            m = T.mark(te.matmul(PS[:, n, :], q[:, :], XNT[:, bass.ds(b * L + A_WIN + n * 512, 512)],
                                                 start=True, stop=True))
                        V.after(m)
                        V.after(V.mark(ve.tensor_tensor(S[:, :], flat(0, 2), future[:, bass.ds(L - P - i * P, L)], ALU.add)))
                        V.after(V.mark(ve.tensor_reduce(mx[:, :], S[:, :], AX, ALU.max)))
                        m = V.mark(ve.tensor_scalar(nmx[:, :], mx[:, :], -1.0, None, ALU.mult))
                        A.after(m)
                        m = A.mark(ac.activation(S[:, :], S[:, :], ACT.Exp, bias=nmx[:, 0:1], accum_out=sm[:, 0:1]))
                        V.after(m)
                        rsm = V.mark(ve.reciprocal(rs[:, :], sm[:, :]))
                        T.after(m)
                        for n in range(2):
                            for j in range(4):
                                c = 4 * n + j
                                m = T.mark(te.transpose(PS[:, 2 + n, j * P:(j + 1) * P], S[:, c * P:(c + 1) * P], ident[:, :]))
                            A.after(m)
                            m = A.mark(ac.copy(pT[:, n * 512:(n + 1) * 512], PS[:, 2 + n, :]))
                            T.after(m)
                            for c in range(4 * n, 4 * n + 4):
                                m = T.mark(te.matmul(PS[:, 4, 0:D], pT[:, c * P:(c + 1) * P],
                                                     XV[:, bass.ds(b * TB + c, 1), :].rearrange("p a d -> p (a d)"),
                                                     start=(c == 0), stop=(c == TB - 1)))
                        V.after(m, rsm)
                        xi = X[:, bass.ds(b * TB + i, 1), :].rearrange("p a d -> p (a d)")
                        V.mark(ve.scalar_tensor_tensor(xi, PS[:, 4, 0:D], rs[:, 0:1], xi, ALU.mult, ALU.add))
                        fence()

        full = [P, TB, H, DH]

        def split(ap):
            return ap.rearrange("p i (h d) -> p i h d", h=H)

        def cope_attention():
            with ExitStack() as own:
                def sl(name, *shape):
                    return own.enter_context(nc.sbuf_tensor("c_" + name, list(shape), F32))
                w = sl("w", P, 3 * D)
                bqkv = sl("bqkv", P, 3 * D)
                wo, bo = sl("wo", P, D), sl("bo", P, D)
                pos_rows = sl("pos_rows", P, DH, 3)
                qkv = sl("qkv", P, NT, 3 * D)
                prod, prod2 = sl("prod", P, TB, D), sl("prod2", P, TB, D)
                dots = sl("dots", P, 2, 2, P)
                tab = sl("tab", P, 2, 3, P)
                gates = sl("gates", P, 2, 2, P)
                w1, w2 = sl("w1", P, 2, 2, P), sl("w2", P, 2, 2, P)
                d1, d2 = sl("d1", P, 2, P), sl("d2", P, 2, P)
                mx = sl("mx", P, 2, P)
                att = sl("att", P, NT, D)
                for n in range(3):
                    load(w[:, n * D:(n + 1) * D], t[("c_wq", "c_wk", "c_wv")[n]])
                    load(bqkv[:, n * D:(n + 1) * D], row(("c_bq", "c_bk", "c_bv")[n], D))
                load(wo[:, :], t["c_wo"])
                load(bo[:, :], row("c_bo", D))
                for d in range(DH):
                    load(pos_rows[:, d, :], t["c_pos"][0, d:d + 1, 0:3].to_broadcast([P, 3]))
                sp.wait_ge(LOAD.sem, LOAD.count)
                fence()

                def products(g, m, turned):
                    T.after(turned)
                    for j in range(4):
                        m = T.mark(te.matmul(PS[:, 1 + j, 0:3 * D], xT4[:, j * P:(j + 1) * P], w[:, :], start=True, stop=True))
                    V.after(m)
                    V.mark(ve.tensor_tensor(qkv[:, bass.ds(4 * g, 4), :], PS[:, 1:5, 0:3 * D],
                                            over(bqkv[:, :], 1, [P, 4, 3 * D]), ALU.add))

                norm_loop(X, products)

                def part(s, n):
                    return qkv[:, TB * s:TB * (s + 1), n * D:(n + 1) * D]

                for s in range(2):
                    for k in range(2):
                        V.after(V.mark(ve.tensor_tensor(prod[:, :, :], part(s, 0), part(k, 1), ALU.mult)))
                        V.after(V.mark(ve.tensor_reduce(dots[:, s, k, :].rearrange("p (i h) -> p i h", h=H), split(prod[:, :, :]), AX, ALU.add)))
                    for n in range(3):
                        pe = pos_rows[:, :, n].unsqueeze(1).unsqueeze(1).to_broadcast(full)
                        V.after(V.mark(ve.tensor_tensor(split(prod[:, :, :]), split(part(s, 0)), pe, ALU.mult)))
                        m = V.mark(ve.tensor_reduce(tab[:, s, n, :].rearrange("p (i h) -> p i h", h=H), split(prod[:, :, :]), AX, ALU.add))
                        V.after(m)
                scale = float(DH) ** -0.5
                A.after(m)
                m = A.mark(ac.activation(gates[:, :, :, :], dots[:, :, :, :], ACT.Tanh, scale=scale / 2))
                V.after(m)
                V.after(V.mark(ve.tensor_scalar(gates[:, :, :, :], gates[:, :, :, :], 0.5, 0.5, ALU.mult, ALU.add)))
                V.after(V.mark(ve.tensor_tensor(gates[:, :, 0, :], gates[:, :, 0, :], gates[:, :, 1, :], ALU.add)))
                V.after(V.mark(ve.tensor_scalar(gates[:, :, :, :], gates[:, :, :, :], 124.0, None, ALU.min)))
                V.mark(ve.tensor_scalar(w1[:, :, :, :], gates[:, :, :, :], 1.0, None, ALU.min))
                V.mark(ve.tensor_scalar(w2[:, :, :, :], gates[:, :, :, :], 1.0, 0.0, ALU.subtract, ALU.max))
                V.mark(ve.tensor_tensor(d1[:, :, :], tab[:, :, 1, :], tab[:, :, 0, :], ALU.subtract))
                V.after(V.mark(ve.tensor_tensor(d2[:, :, :], tab[:, :, 2, :], tab[:, :, 1, :], ALU.subtract)))
                two = [P, 2, 2, P]
                V.mark(ve.tensor_tensor(w1[:, :, :, :], w1[:, :, :, :], over(d1[:, :, :], 2, two), ALU.mult))
                V.after(V.mark(ve.tensor_tensor(w2[:, :, :, :], w2[:, :, :, :], over(d2[:, :, :], 2, two), ALU.mult)))
                V.after(V.mark(ve.tensor_tensor(w1[:, :, :, :], w1[:, :, :, :], w2[:, :, :, :], ALU.add)))
                V.after(V.mark(ve.tensor_tensor(w1[:, :, :, :], w1[:, :, :, :], over(tab[:, :, 0, :], 2, two), ALU.add)))
                V.after(V.mark(ve.scalar_tensor_tensor(dots[:, :, :, :].rearrange("p a b c -> p (a b c)"),
                                                       dots[:, :, :, :].rearrange("p a b c -> p (a b c)"), scale,
                                                       w1[:, :, :, :].rearrange("p a b c -> p (a b c)"), ALU.mult, ALU.add)))
                V.after(V.mark(ve.tensor_tensor(mx[:, :, :], dots[:, :, 0, :], dots[:, :, 1, :], ALU.max)))
                m = V.mark(ve.tensor_tensor(dots[:, :, :, :], dots[:, :, :, :], over(mx[:, :, :], 2, two), ALU.subtract))
                A.after(m)
                m = A.mark(ac.activation(dots[:, :, :, :], dots[:, :, :, :], ACT.Exp))
                V.after(m)
                V.after(V.mark(ve.tensor_tensor(mx[:, :, :], dots[:, :, 0, :], dots[:, :, 1, :], ALU.add)))
                V.after(V.mark(ve.reciprocal(mx[:, :, :], mx[:, :, :])))
                V.after(V.mark(ve.tensor_tensor(dots[:, :, :, :], dots[:, :, :, :], over(mx[:, :, :], 2, two), ALU.mult)))
                for s in range(2):
                    for k, to in ((0, prod), (1, prod2)):
                        a = over(dots[:, s, k, :].rearrange("p (i h) -> p i h", h=H), 3, full)
                        m = V.mark(ve.tensor_tensor(split(to[:, :, :]), split(part(k, 2)), a, ALU.mult))
                    V.after(m)
                    V.after(V.mark(ve.tensor_tensor(att[:, TB * s:TB * (s + 1), :], prod[:, :, :], prod2[:, :, :], ALU.add)))
                fence()
                project_loop(att, wo[:, :], bo[:, :])

        def linear_attention():
            f, S4 = 4, D // 4
            with ExitStack() as own:
                def sl(name, *shape):
                    return own.enter_context(nc.sbuf_tensor("d_" + name, list(shape), F32))
                ws = {n: sl("w" + n, P, D) for n in "qkvo"}
                bs = {n: sl("b" + n, P, D) for n in "qkvo"}
                fact = sl("fact", P, 4, f, f)
                blocks = sl("blocks", P, 4, f, S4)
                g1, b1, g2, b2 = (sl(n, P, D) for n in ("g1", "b1", "g2", "b2"))
                tmp = sl("tmp", P, D)
                q, kv = sl("q", P, NT, D), sl("kv", P, NT, 2 * D)
                QN = sl("QN", P, NT, D)
                prod, prod2 = sl("prod", P, TB, D), sl("prod2", P, TB, D)
                dots = sl("dots", P, 2, 2, P)
                den = sl("den", P, 2, P)
                att = sl("att", P, NT, D)
                for m4, n in enumerate("qkvo"):
                    for i in range(f):
                        lo = i * S4
                        load(blocks[lo:lo + S4, m4, :, :], t[f"d_{n}S"].rearrange("n k l -> k n l"))
                        load(fact[lo:lo + S4, m4, :, :], t[f"d_{n}A"][:, i:i + 1, :].rearrange("n i j -> i n j").to_broadcast([S4, f, f]))
                    load(bs[n][:, :], row(f"d_{n}b", D))
                for b, n in ((g1, "d_g1"), (b1, "d_b1"), (g2, "d_g2"), (b2, "d_b2")):
                    load(b[:, :], row(n, D))
                V.after((LOAD, LOAD.count))
                for m4, n in enumerate("qkvo"):
                    shape = [P, f, S4]
                    for k in range(f):
                        to = (ws[n] if k == 0 else tmp)[:, :].rearrange("p (j l) -> p j l", j=f)
                        m = V.mark(ve.tensor_tensor(to, over(fact[:, m4, k, :], 2, shape), over(blocks[:, m4, k, :], 1, shape), ALU.mult))
                        V.after(m)
                        if k:
                            V.after(V.mark(ve.tensor_tensor(ws[n][:, :], ws[n][:, :], tmp[:, :], ALU.add)))
                fence()

                def keys_values(g, m, turned):
                    T.after(turned)
                    for j in range(4):
                        for c, n in enumerate("kv"):
                            m = T.mark(te.matmul(PS[:, 1 + j, c * D:(c + 1) * D], xT4[:, j * P:(j + 1) * P], ws[n][:, :],
                                                 start=True, stop=True))
                    V.after(m)
                    for c, n in enumerate("kv"):
                        to = kv[:, bass.ds(4 * g, 4), c * D:(c + 1) * D]
                        m = V.mark(ve.tensor_tensor(to, PS[:, 1:5, c * D:(c + 1) * D], over(bs[n][:, :], 1, [P, 4, D]), ALU.add))
                        if n == "k":
                            V.after(m)
                            V.mark(ve.tensor_scalar(to, to, 0.0, None, ALU.max))

                def queries(g, m, turned):
                    T.after(turned)
                    for j in range(4):
                        m = T.mark(te.matmul(PS[:, 1 + j, 0:D], xT4[:, j * P:(j + 1) * P], ws["q"][:, :], start=True, stop=True))
                    V.after(m)
                    to = q[:, bass.ds(4 * g, 4), :]
                    V.after(V.mark(ve.tensor_tensor(to, PS[:, 1:5, 0:D], over(bs["q"][:, :], 1, [P, 4, D]), ALU.add)))
                    V.mark(ve.tensor_scalar(to, to, 0.0, None, ALU.max))

                norm_loop(X, keys_values, keep=XN, keep_t=False)
                norm_loop(XN, queries, gain=g1, shift=b1, keep=QN, keep_t=False)
                at = np.float32(np.pi / 2) * np.arange(1, B + 1, dtype=np.float32) / np.float32(B)
                sin, cos = np.sin(at).astype(np.float32), np.cos(at).astype(np.float32)
                for s in range(2):
                    for k in range(2):
                        V.after(V.mark(ve.tensor_tensor(prod[:, :, :], q[:, TB * s:TB * (s + 1), :],
                                                        kv[:, TB * k:TB * (k + 1), 0:D], ALU.mult)))
                        to = dots[:, s, k, :].rearrange("p (i h) -> p i h", h=H)
                        V.after(V.mark(ve.tensor_reduce(to, split(prod[:, :, :]), AX, ALU.add)))
                        V.after(V.mark(ve.tensor_scalar(to, to, float(sin[s] * sin[k] + cos[s] * cos[k]), None, ALU.mult)))
                V.after(V.mark(ve.tensor_tensor(den[:, :, :], dots[:, :, 0, :], dots[:, :, 1, :], ALU.add)))
                V.after(V.mark(ve.tensor_scalar(den[:, :, :], den[:, :, :], 1e-6, None, ALU.max)))
                V.after(V.mark(ve.reciprocal(den[:, :, :], den[:, :, :])))
                V.after(V.mark(ve.tensor_tensor(dots[:, :, :, :], dots[:, :, :, :], over(den[:, :, :], 2, [P, 2, 2, P]), ALU.mult)))
                for s in range(2):
                    for k, to in ((0, prod), (1, prod2)):
                        a = over(dots[:, s, k, :].rearrange("p (i h) -> p i h", h=H), 3, full)
                        m = V.mark(ve.tensor_tensor(split(to[:, :, :]), split(kv[:, TB * k:TB * (k + 1), D:]), a, ALU.mult))
                    V.after(m)
                    V.after(V.mark(ve.tensor_tensor(prod[:, :, :], prod[:, :, :], prod2[:, :, :], ALU.add)))
                    V.after(V.mark(ve.tensor_tensor(att[:, TB * s:TB * (s + 1), :], prod[:, :, :], QN[:, TB * s:TB * (s + 1), :], ALU.add)))
                fence()

                def add_out(g, m, turned):
                    T.after(turned)
                    for j in range(4):
                        w = T.mark(te.matmul(PS[:, 1, j * P:(j + 1) * P], xT4[:, j * P:(j + 1) * P], ws["o"][:, :], start=True, stop=True))
                    xg = X[:, bass.ds(4 * g, 4), :]
                    V.after(m)
                    V.after(V.mark(ve.tensor_tensor(xg, xg, xn4[:, :, :], ALU.add)))
                    V.after(V.mark(ve.tensor_tensor(xg, xg, over(bs["o"][:, :], 1, [P, 4, D]), ALU.add)))
                    V.after(w)
                    V.mark(ve.tensor_tensor(xg, PS[:, 1, :].rearrange("p (j d) -> p j d", j=4), xg, ALU.add))

                norm_loop(att, add_out, gain=g2, shift=b2, keep_t=False)

        def local_stack(tag, load_first):
            with ExitStack() as own:
                def sl(name, *shape):
                    return own.enter_context(nc.sbuf_tensor(tag + name, list(shape), F32))
                wqkv = sl("wqkv", P, 3 * INNER)
                wo = sl("wo", P, LH // 2, D)
                w1 = sl("w1", P, 2 * HID)
                w2 = sl("w2", P, 3, D)
                b1 = sl("b1", P, 2, 3)
                lng, lnb = sl("lng", P, 1), sl("lnb", P, 1)
                qs, ks = sl("qs", P, LD), sl("ks", P, LD)
                base = sl("base", P, 4, TB, LD)
                rot = sl("rot", P, 4, NT, LD)
                mask = sl("mask", P, NT, 2 * LW)
                keep = sl("keep", P, NT)
                XST = sl("XST", P, NT * P)
                X0 = sl("X0", P, NT, D)
                xs = sl("xs", P, P)
                sq = sl("sq", P, INNER)
                ssq = sl("ssq", P, 2, LH)
                QN, QR, T2 = sl("QN", P, LH, LD), sl("QR", P, LH, LD), sl("T2", P, LH, LD)
                KN, KR, T3 = sl("KN", P, LH, LD), sl("KR", P, LH, LD), sl("T3", P, LH, LD)
                qT = sl("qT", P, 8, P)
                kT = sl("kT", P, 8, LW + P)
                Vt = sl("Vt", P, INNER)
                V2 = sl("V2", P, 4, 8, LD)
                S = sl("S", P, 2, 8, 2 * LW)
                Pm = sl("Pm", P, 8, 2, 2 * LW)
                pT = sl("pT", P, 8, P)
                mx, sm, rs = (sl(n, P, 2, 8) for n in ("mx", "sm", "rs"))
                O, oT = sl("O", P, 8, 2, LD), sl("oT", P, 8, P)
                xc = sl("xc", P, NT * P)
                xsq, rst = sl("xsq", P, 2, 512), sl("rst", P, 2, 512)
                vrt = sl("vrt", P, 2, 4)
                gl, hT = sl("gl", P, 2, 512), sl("hT", P, 3, 512)

                def load_attention(l):
                    load(wqkv[:, :], t["l_wqkv"][bass.ds(l, 1), :, :].rearrange("a d n -> (a d) n"))
                    load(wo[:, :, :], t["l_wo"][bass.ds(l, 1), :, :].rearrange("a (c p) d -> p (a c) d", p=P))
                    load(qs[:, :], t["l_qs"][bass.ds(l, 1), :].to_broadcast([P, LD]))
                    return load(ks[:, :], t["l_ks"][bass.ds(l, 1), :].to_broadcast([P, LD]))

                def load_ffn(l):
                    load(w1[:, :], t["l_w1"][bass.ds(l, 1), :, :].rearrange("a d n -> (a d) n"))
                    for c, n in enumerate(HCH):
                        load(w2[0:n, c, :], t["l_w2"][bass.ds(l, 1), c * P:c * P + n, :].rearrange("a p d -> (a p) d"))
                        for k in range(2):
                            load(b1[0:n, k, c:c + 1], t["l_b1"][bass.ds(l, 1), k * HID + c * P:k * HID + c * P + n].rearrange("a (p c) -> p (a c)", c=1))
                    load(w2[HCH[2]:HCH[2] + 1, 2, :], t["l_b2"][bass.ds(l, 1), :])
                    load(lng[:, :], t["l_g"][bass.ds(l, 1), :].rearrange("a (p c) -> p (a c)", c=1))
                    return load(lnb[:, :], t["l_b"][bass.ds(l, 1), :].rearrange("a (p c) -> p (a c)", c=1))

                for r in range(4):
                    load(base[:, r, :, :], t["l_rot"][r].rearrange("(i p) d -> p i d", p=P))
                load(mask[:, :, :], t["l_mask"])
                load(keep[:, :], t["l_keep"])
                load_attention(0)
                G.after(G.mark(gp.memset(XST[64:, :], 0.0)))
                G.after(G.mark(gp.memset(hT[64:, 2, :], 1.0)))
                G.after(G.mark(gp.memset(kT[:, :, :], 0.0)))
                G.after(G.mark(gp.memset(V2[:, :, :, :], 0.0)))
                sp.wait_ge(LOAD.sem, LOAD.count)
                fence()

                def shifted_transpose():
                    for g in range(NG):
                        for j in range(4):
                            m = T.mark(te.transpose(PS[:, g, j * P:(j + 1) * P], X[:, 4 * g + j, :], ident[:, :]))
                        n = 511 if g % 2 else 512
                        A.after(m)
                        A.mark(ac.copy(XST[0:64, g * 512:(g + 1) * 512], PS[0:64, g, :]))
                        A.mark(ac.copy(XST[64:, g * 512 + 1:g * 512 + 1 + n], PS[64:, g, 0:n]))

                def attention_step(i, first, last):
                    n = i + 1
                    project, attend = not last, not first
                    if project:
                        xin = G.mark(gp.tensor_copy(xs[:, :], XST[:, bass.ds(n * P, P)]))
                    if attend:
                        sdone, mdone, pdone = [], [], []
                        for r in range(2):
                            for c in range(8):
                                for w in range(4):
                                    m = te.matmul(PS[LW * w:LW * (w + 1), 6 + r, c * 64:(c + 1) * 64],
                                                  qT[64 * r:64 * r + 64, c, LW * w:LW * (w + 1)],
                                                  kT[64 * r:64 * r + 64, c, LW * w:LW * w + 64], start=True, stop=True,
                                                  skip_group_check=True)
                            sdone.append(T.mark(m))
                        for r in range(2):
                            V.after(sdone[r])
                            s3 = [P, 8, 2 * LW]
                            mdone.append(V.mark(ve.tensor_tensor(
                                S[:, r, :, :], PS[:, 6 + r, :].rearrange("p (c k) -> p c k", c=8),
                                mask[:, bass.ds(i, 1), :].to_broadcast(s3), ALU.add)))
                            V.after(mdone[r])
                            V.after(V.mark(ve.tensor_reduce(mx[:, r, :], S[:, r, :, :], AX, ALU.max)))
                            m = V.mark(ve.tensor_tensor(S[:, r, :, :], S[:, r, :, :], over(mx[:, r, :], 2, s3), ALU.subtract))
                            A.after(m)
                            pdone.append(A.mark(ac.activation(Pm[:, :, r, :], S[:, r, :, :], ACT.Exp)))
                    if project:
                        T.after(xin)
                        qk_done = []
                        for c in range(4):
                            m = T.mark(te.matmul(PS[:, c, :], xs[:, :], wqkv[:, c * 512:(c + 1) * 512], start=True, stop=True))
                            qk_done.append(m)
                        normed = []
                        for c, (N, R, U) in enumerate(((QN, QR, T2), (KN, KR, T3))):
                            src = PS[:, 2 * c:2 * c + 2, :].rearrange("p b (h d) -> p (b h) d", d=LD)
                            A.after(qk_done[2 * c + 1])
                            if c:
                                A.after(red)
                            m = A.mark(ac.activation(sq[:, :], flat(2 * c, 2 * c + 2), ACT.Square))
                            V.after(m)
                            red = V.mark(ve.tensor_reduce(ssq[:, c, :], sq[:, :].rearrange("p (h d) -> p h d", d=LD), AX, ALU.add))
                            V.after(red)
                            G.after(V.mark(ve.tensor_scalar(ssq[:, c, :], ssq[:, c, :], 1e-24, None, ALU.max)))
                            V.after(inverse_root(ssq[:, c, :], LH))
                            m = V.mark(ve.tensor_tensor(N[:, :, :], src, over(ssq[:, c, :], 2, [P, LH, LD]), ALU.mult))
                            normed.append(m)
                            V.after(m)
                            G.after(m)
                            half = LD // 2
                            for k in range(2):
                                lo, hi = k * half, (1 - k) * half
                                m = G.mark(gp.tensor_tensor(U[:, :, lo:lo + half], N[:, :, hi:hi + half],
                                                            rot[:, 2 * c + 1, bass.ds(n, 1), lo:lo + half].to_broadcast([P, LH, half]), ALU.mult))
                            m2 = V.mark(ve.tensor_tensor(R[:, :, :], N[:, :, :], rot[:, 2 * c, bass.ds(n, 1), :].to_broadcast([P, LH, LD]), ALU.mult))
                            G.after(m, m2)
                            m = G.mark(gp.tensor_tensor(R[:, :, :], R[:, :, :], U[:, :, :], ALU.add))
                            normed.append(m)
                        T.after(normed[0])
                        for r in range(2):
                            wv = wqkv[:, 2 * INNER:].rearrange("p (c r d) -> p r c d", r=2, d=LD)[:, r, :, :]
                            m = T.mark(te.matmul(PS[:, r, :], xs[:, :], wv, start=True, stop=True))
                        A.after(m)
                        vin = A.mark(ac.copy(Vt[:, :], flat(0, 2)))
                    if attend:
                        V.after(*pdone)
                        for r in range(2):
                            m = V.mark(ve.tensor_reduce(sm[:, r, :], Pm[:, :, r, :], AX, ALU.add))
                        V.after(m)
                        rsm = V.mark(ve.reciprocal(rs[:, :, :], sm[:, :, :]))
                        T.after(*pdone)
                        for b in range(2):
                            for c in range(4 * b, 4 * b + 4):
                                m = T.mark(te.transpose(PS[:, 4 + b, (c % 4) * P:(c % 4 + 1) * P],
                                                        Pm[:, c, :, :].rearrange("p r k -> p (r k)"), ident[:, :]))
                            A.after(m)
                            pt = A.mark(ac.copy(pT[:, 4 * b:4 * b + 4, :].rearrange("p c q -> p (c q)"), PS[:, 4 + b, :]))
                        T.after(pt, *mdone)
                        for r in range(2):
                            for c in range(8):
                                for w in range(4):
                                    m = te.matmul(PS[LW * w:LW * (w + 1), 6 + r, c * LD:(c + 1) * LD],
                                                  pT[64 * r:64 * r + 64, c, LW * w:LW * (w + 1)],
                                                  V2[64 * r:64 * r + 64, w, c, :], start=True, stop=True, skip_group_check=True)
                            pv = T.mark(m)
                            V.after(pv, rsm)
                            odone = V.mark(ve.tensor_tensor(O[:, :, r, :], PS[:, 6 + r, :].rearrange("p (c d) -> p c d", d=LD),
                                                            over(rs[:, r, :], 2, [P, 8, LD]), ALU.mult))
                    if project:
                        if attend:
                            HALO.after(pv)
                        for r in range(2):
                            halo = HALO.mark(sp.dma_start(V2[64 * r:64 * r + LW, 0, :, :], V2[64 * r + LW:64 * r + 64, 3, :, :]))
                        VDMA.after(vin)
                        for r in range(2):
                            cols = Vt[:, r * 512:(r + 1) * 512].rearrange("p (c d) -> p c d", d=LD)
                            VDMA.mark(sp.dma_start(V2[64 * r + LW:64 * r + 64, 0, :, :], cols[0:LW]))
                            for w in (1, 2):
                                VDMA.mark(sp.dma_start(V2[64 * r:64 * r + 64, w, :, :], cols[LW * (w - 1):LW * (w + 1)]))
                        VDMA.after(halo)
                        for r in range(2):
                            cols = Vt[:, r * 512:(r + 1) * 512].rearrange("p (c d) -> p c d", d=LD)
                            vdma = VDMA.mark(sp.dma_start(V2[64 * r:64 * r + 64, 3, :, :], cols[2 * LW:4 * LW]))
                    if attend:
                        T.after(odone)
                        for b in range(2):
                            for c in range(4 * b, 4 * b + 4):
                                m = T.mark(te.transpose(PS[:, 4 + b, (c % 4) * P:(c % 4 + 1) * P],
                                                        O[:, c, :, :].rearrange("p r d -> p (r d)"), ident[:, :]))
                            A.after(m)
                            ot = A.mark(ac.copy(oT[:, 4 * b:4 * b + 4, :].rearrange("p c q -> p (c q)"), PS[:, 4 + b, :]))
                        T.after(ot)
                        for c in range(8):
                            m = te.matmul(PS[:, 4, 0:D], oT[:, c, :], wo[:, c, :], start=(c == 0), stop=(c == 7))
                        m = T.mark(m)
                        V.after(m)
                        xi = X[:, bass.ds(i, 1), :].rearrange("p a d -> p (a d)")
                        xadd = V.mark(ve.tensor_tensor(xi, PS[:, 4, 0:D], xi, ALU.add))
                    if project:
                        if attend:
                            G.after(sdone[1])
                        halo_k = G.mark(gp.tensor_tensor(kT[:, :, 0:LW], kT[:, :, P:], over(keep[:, bass.ds(n, 1)], 1, [P, 8, LW]), ALU.mult))
                        bank = 0
                        evac = [None, None]
                        if attend:
                            T.after(ot, xadd)
                        for R, dst, lo, need in ((QR, qT, 0, normed[1]), (KR, kT, LW, normed[3])):
                            T.after(need)
                            for b in range(2):
                                if evac[b]:
                                    T.after(evac[b])
                                for c in range(4 * b, 4 * b + 4):
                                    m = T.mark(te.transpose(PS[:, 4 + b, (c % 4) * P:(c % 4 + 1) * P],
                                                            R[:, 2 * c:2 * c + 2, :].rearrange("p r d -> p (r d)"), ident[:, :]))
                                A.after(m)
                                if dst is kT:
                                    A.after(halo_k)
                                evac[b] = A.mark(ac.copy(dst[:, 4 * b:4 * b + 4, lo:lo + P],
                                                         PS[:, 4 + b, :].rearrange("p (c q) -> p c q", c=4)))
                        sp.wait_ge(HALO.sem, HALO.count)
                        sp.wait_ge(VDMA.sem, VDMA.count)

                def attention():
                    attention_step(-1, True, False)
                    fence()
                    with nc.Fori(0, NT - 1) as i:
                        attention_step(i, False, False)
                        fence()
                    attention_step(NT - 1, False, True)
                    fence()

                norm_loop(X, lambda g, m, turned: None, keep=XN, keep_t=False)
                m = V.mark(ve.tensor_copy(X0[:, :, :], X[:, :, :]))
                V.after(m)
                V.mark(ve.tensor_copy(X[:, :, :], XN[:, :, :]))
                fence()
                with nc.Fori(0, DEPTH) as l:
                    half = LD // 2
                    for r, scale in ((0, qs), (2, ks)):
                        for b in range(B):
                            V.mark(ve.tensor_tensor(rot[:, r, b * TB:(b + 1) * TB, :], base[:, r, :, :],
                                                    over(scale[:, :], 1, [P, TB, LD]), ALU.mult))
                            for k in range(2):
                                lo, hi = k * half, (1 - k) * half
                                V.mark(ve.tensor_tensor(rot[:, r + 1, b * TB:(b + 1) * TB, lo:lo + half],
                                                        base[:, r + 1, :, lo:lo + half],
                                                        over(scale[:, hi:hi + half], 1, [P, TB, half]), ALU.mult))
                    shifted_transpose()
                    ffn_in = load_ffn(l)
                    sp.wait_ge(LOAD.sem, LOAD.count)
                    fence()
                    attention()
                    load_attention(l + 1)
                    shifted_transpose()
                    fence_mark = (A, A.count)
                    for g in range(NG):
                        cols = slice(g * 512, (g + 1) * 512)
                        p2 = g % 2
                        T.after(fence_mark)
                        if g >= 2:
                            T.after(sub[g - 2], powd[g - 2])
                        if g == 0:
                            sub, powd, muld = [], [], []
                        m = T.mark(te.matmul(PS[:, 4 + 2 * p2, :], mean_mat[:, :], XST[:, cols], start=True, stop=True))
                        V.after(m)
                        sub.append(V.mark(ve.tensor_tensor(xc[:, cols], XST[:, cols], PS[:, 4 + 2 * p2, :], ALU.subtract)))
                        A.after(sub[g])
                        m = A.mark(ac.activation(xsq[:, p2, :], xc[:, cols], ACT.Square))
                        T.after(m)
                        for j in range(4):
                            m = T.mark(te.matmul(PS[:, 2 + p2, j:j + 1], xsq[:, p2, j * P:(j + 1) * P], mean_mat[:, 0:1],
                                                 start=True, stop=True))
                        V.after(m)
                        m = V.mark(ve.tensor_scalar(vrt[:, p2, :], PS[:, 2 + p2, 0:4], EPS, None, ALU.add))
                        G.after(m)
                        m = inverse_root(vrt[:, p2, :], 4)
                        V.after(m)
                        for j in range(4):
                            m = V.mark(ve.tensor_scalar(rst[:, p2, j * P:(j + 1) * P], ident[:, :], vrt[:, p2, j:j + 1], None, ALU.mult))
                        T.after(m)
                        m = T.mark(te.matmul(PS[:, 5 + 2 * p2, :], ones_mat[:, :], rst[:, p2, :], start=True, stop=True))
                        V.after(m)
                        powd.append(V.mark(ve.tensor_tensor(xc[:, cols], xc[:, cols], PS[:, 5 + 2 * p2, :], ALU.mult)))
                        muld.append(powd[g])
                        A.after(muld[g])
                        A.mark(ac.activation(xc[:, cols], xc[:, cols], ACT.Identity, scale=lng[:, 0:1], bias=lnb[:, 0:1]))
                    sp.wait_ge(LOAD.sem, LOAD.count)
                    fence()
                    with nc.Fori(0, NG) as g:
                        xn = xc[:, bass.ds(g * 512, 512)]
                        ups, gelus, hs = [], [], []
                        for c, n in enumerate(HCH):
                            te.matmul(PS[0:n, 2 * c, :], w1[:, HID + c * P:HID + c * P + n], xn, start=True, stop=True)
                            m = T.mark(te.matmul(PS[0:n, 2 * c + 1, :], w1[:, c * P:c * P + n], xn, start=True, stop=True))
                            ups.append(m)
                        for c, n in enumerate(HCH):
                            A.after(ups[c])
                            if c == 2:
                                A.after(hs[0])
                            m = A.mark(ac.activation(gl[0:n, c % 2, :], PS[0:n, 2 * c, :], ACT.Gelu, bias=b1[0:n, 1, c:c + 1]))
                            V.after(m)
                            hs.append(V.mark(ve.scalar_tensor_tensor(hT[0:n, c, :], PS[0:n, 2 * c + 1, :], b1[0:n, 0, c:c + 1],
                                                                     gl[0:n, c % 2, :], ALU.add, ALU.mult)))
                        T.after(hs[2])
                        for j in range(4):
                            for c, n in enumerate((P, P, HCH[2] + 1)):
                                m = te.matmul(PS[:, 6, j * D:(j + 1) * D], hT[0:n, c, j * P:(j + 1) * P], w2[0:n, c, :],
                                              start=(c == 0), stop=(c == 2))
                        m = T.mark(m)
                        V.after(m)
                        xg = X[:, bass.ds(4 * g, 4), :]
                        V.mark(ve.tensor_tensor(xg, PS[:, 6, :].rearrange("p (j d) -> p j d", j=4), xg, ALU.add))
                        fence()

                V.mark(ve.tensor_tensor(X[:, :, :], X[:, :, :], X0[:, :, :], ALU.add))
                fence()

        window_attention()
        mixture("f_")
        causal_attention()
        mixture("g_")
        cope_attention()
        local_stack("l_", True)
        linear_attention()
        local_stack("m_", True)
        done = LOAD.mark(sp.dma_start(out.rearrange("b (i p) d -> p (b i) d", p=P), X[:, :, :]))
        sp.wait_ge(LOAD.sem, LOAD.count)


def tables():
    f = np.float32
    c = {"ident": np.eye(P, dtype=f), "mean_mat": np.full((P, P), 1.0 / D, f)}
    c["a_headmask"] = (np.arange(P)[:, None] // A_DH == np.arange(A_H)[None, :]).astype(f)
    c["a_pad"] = np.tile(np.where(np.arange(NT) % TB == 0, NEG, 0.0).astype(f), (P, 1))
    c["f_lower"] = (np.arange(E_N)[None, :] < np.arange(E_N)[:, None]).astype(f).reshape(-1)
    ahead = np.arange(2 * L - P)[None, :] - (L - P) - np.arange(P)[:, None]
    c["b_future"] = np.where(ahead > 0, NEG, 0.0).astype(f)
    half = np.arange(0, LD, 2, dtype=f)
    freqs = np.arange(L, dtype=f)[:, None] * (f(1) / f(10000) ** (half / f(LD)))[None, :]
    freqs = np.concatenate([freqs, freqs], -1)
    power = (np.arange(L, dtype=f) - L // 2) / f(LW // 2)
    scale = ((half + f(0.4 * LD)) / f(1.4 * LD))[None, :] ** power[:, None]
    scale = np.concatenate([scale, scale], -1)
    cos, sin = np.cos(freqs), np.sin(freqs)
    sin = np.concatenate([-sin[:, :LD // 2], sin[:, LD // 2:]], -1)
    c["l_rot"] = np.stack([8 * cos * scale, 8 * sin * scale, cos / scale, sin / scale]).astype(f)
    a, k = np.arange(P)[:, None] % LW, np.arange(2 * LW)[None, :]
    allowed = (a <= k) & (k <= a + LW)
    first = allowed & ((np.arange(P)[:, None] >= LW) | (k >= LW))
    m = np.stack([first if i % TB == 0 else allowed for i in range(NT)], 1)
    c["l_mask"] = np.where(m, 0.0, NEG).astype(f)
    c["l_keep"] = np.tile((np.arange(NT) % TB != 0).astype(f), (P, 1))
    return c


def kernel(**inputs):
    from concourse import bacc
    from concourse.bass_utils import run_bass_kernel_spmd

    a = {k: np.asarray(v) for k, v in inputs.items()}
    arrays = {"x": a["L0_attn_a_x"]}
    for n in "qkvo":
        arrays[f"a_w{n}T"] = a[f"L0_attn_a_W{n}"].T
        arrays[f"a_b{n}"] = a[f"L0_attn_a_b{n}"]
        arrays[f"c_w{n}"] = a[f"L1_attn_a_W{n}"]
        arrays[f"c_b{n}"] = a[f"L1_attn_a_b{n}"]
        for part in "ASb":
            arrays[f"d_{n}{part}"] = a[f"L1_attn_b_{n}{part}"]
    arrays["b_wqk"], arrays["b_wov"] = a["L0_attn_b_wqk"], a["L0_attn_b_wov"]
    arrays["f_gateT"] = a["L0_ffn_gate_w"].T
    for n in "123":
        arrays[f"f_w{n}T"] = a[f"L0_ffn_w{n}"].transpose(0, 2, 1)
        arrays[f"f_b{n}"] = a[f"L0_ffn_b{n}"]
    arrays["f_sw12T"] = np.concatenate([a["L0_ffn_sw1"].T, a["L0_ffn_sw2"].T], 1)
    arrays["f_sw3T"] = a["L0_ffn_sw3"].T
    arrays["c_pos"] = a["L1_attn_a_pos_emb"]
    for n in ("g1", "b1", "g2", "b2"):
        arrays[f"d_{n}"] = a[f"L1_attn_b_{n}"]
    for n, src in (("wqkv", "Wqkv"), ("wo", "Wo"), ("qs", "q_scale"), ("ks", "k_scale")):
        w = a[f"L1_ffn_{src}"]
        arrays[f"l_{n}"] = np.concatenate([w, w[:1]])
    for n, src in (("w1", "W1"), ("b1", "b1"), ("w2", "W2"), ("b2", "b2"), ("g", "ln_g"), ("b", "ln_b")):
        arrays[f"l_{n}"] = a[f"L1_ffn_{src}"]
    arrays.update(tables())

    nc = bacc.Bacc("TRN2", target_bir_lowering=False, num_devices=1)
    arrays = {k + "_dram": np.ascontiguousarray(v) for k, v in arrays.items()}
    t = {k[:-5]: nc.dram_tensor(k, v.shape, F32, kind="ExternalInput").ap() for k, v in arrays.items()}
    out = nc.dram_tensor("out_dram", (B, L, D), F32, kind="ExternalOutput").ap()
    build(nc, t, out)
    r = run_bass_kernel_spmd(nc, [arrays], core_ids=[0])
    return r.results[0]["out_dram"]
```

```python
from contextlib import ExitStack

import numpy as np

import concourse.bass as bass
from concourse import mybir

F32 = mybir.dt.float32
BF16 = mybir.dt.bfloat16
ALU = mybir.AluOpType
ACT = mybir.ActivationFunctionType
AX = mybir.AxisListType.X

P = 128
B, L, D = 2, 1024, 128
NT = B * L // P
TB = L // P
NG = NT // 4
EPS = 1e-5
NEG = -3.0e38

A_WIN, A_H, A_DH = 64, 16, 8
E_N, I_SH = 8, 256
H, DH = 16, 8
DEPTH, LH, LD, LW = 6, 16, 64, 32
INNER = LH * LD
HID = int(D * 4 * 2 / 3)
HCH = [128, 128, HID - 256]


class Lane:

    def __init__(self, engine, sem, step=1):
        self.engine, self.sem, self.step = engine, sem, step
        self.reset()

    def reset(self):
        self.count = 0
        self.seen = {}

    def after(self, *marks):
        for lane, value in marks:
            if self.seen.get(lane.sem.num, 0) < value:
                self.engine.wait_ge(lane.sem, value)
                self.seen[lane.sem.num] = value

    def mark(self, instruction):
        self.count += self.step
        instruction.then_inc(self.sem, self.step)
        return self, self.count


def over(ap, axis, shape):
    return ap.unsqueeze(axis).to_broadcast(shape)


def build(nc, t, out):
    ctx = ExitStack()
    with ctx:
        def sb(name, *shape):
            return ctx.enter_context(nc.sbuf_tensor(name, list(shape), F32))

        names = ["pe_done", "dve_done", "act_done", "pool_done", "load_done", "v_done", "halo_done"]
        sems = [ctx.enter_context(nc.semaphore(n)) for n in names]
        assert [s.num for s in sems] == list(range(sems[0].num, sems[0].num + len(sems)))
        T = Lane(nc.tensor, sems[0])
        V = Lane(nc.vector, sems[1])
        A = Lane(nc.scalar, sems[2])
        G = Lane(nc.gpsimd, sems[3])
        LOAD = Lane(nc.sync, sems[4], 16)
        VDMA = Lane(nc.sync, sems[5], 16)
        HALO = Lane(nc.sync, sems[6], 16)
        lanes = [T, V, A, G, LOAD, VDMA, HALO]
        te, ve, ac, gp, sp = nc.tensor, nc.vector, nc.scalar, nc.gpsimd, nc.sync

        def fence():
            nc.all_engine_barrier(sems_to_clear=range(sems[0].num, sems[-1].num + 1))
            for lane in lanes:
                lane.reset()

        PS = ctx.enter_context(nc.psum_tensor("PS", [P, 8, 512], F32))

        def flat(a, b):
            return PS[:, a:b, :].rearrange("p a b -> p (a b)")

        X = sb("X", P, NT, D)
        ident = sb("ident", P, P)
        mean_mat = sb("mean_mat", P, P)
        XNT = sb("XNT", P, A_WIN + NT * P)
        XN = sb("XN", P, NT, D)
        xn4 = sb("xn4", P, 4, D)
        xT4 = sb("xT4", P, 4 * P)
        stats = sb("stats", P, 4, 6)
        meanvar = sb("meanvar", P, 4, 2)
        rstd = sb("rstd", P, 4)
        minus_half = sb("minus_half", P, 2 * H)
        ones_mat = sb("ones_mat", P, P)

        def load(dst, src):
            return LOAD.mark(sp.dma_start(dst, src))

        def row(name, n):
            return t[name].rearrange("(a n) -> a n", a=1).to_broadcast([P, n])

        def column(name):
            return t[name].rearrange("(n a) -> n a", a=1)

        load(X[:, :, :], t["x"].rearrange("b (i p) d -> p (b i) d", p=P))
        load(ident[:, :], t["ident"])
        m = load(mean_mat[:, :], t["mean_mat"])
        G.mark(gp.memset(minus_half[:, :], -0.5))
        G.mark(gp.memset(ones_mat[:, :], 1.0))
        G.after(G.mark(gp.memset(XNT[:, 0:A_WIN], 0.0)))
        sp.wait_ge(LOAD.sem, LOAD.count)
        fence()

        def inverse_root(ap, n):
            return G.mark(gp.tensor_tensor(ap, ap, minus_half[:, 0:n], ALU.pow))

        def transpose4(src, bank, dst, before=()):
            T.after(*before)
            for j in range(4):
                m = T.mark(te.transpose(PS[:, bank, j * P:(j + 1) * P], src[:, j, :], ident[:, :]))
            A.after(m)
            return A.mark(ac.copy(dst, PS[:, bank, :]))

        def norm_loop(src, hook, gain=None, shift=None, keep=None, keep_t=True):
            with nc.Fori(0, NG) as g:
                for j in range(4):
                    m = V.mark(ve.bn_stats(stats[:, j, :], src[:, bass.ds(4 * g + j, 1), :].rearrange("p a d -> p (a d)")))
                V.after(m)
                for j in range(4):
                    m = V.mark(ve.bn_aggr(meanvar[:, j, :], stats[:, j, :]))
                V.after(m)
                G.after(V.mark(ve.tensor_scalar(rstd[:, :], meanvar[:, :, 1], EPS, None, ALU.add)))
                V.after(inverse_root(rstd[:, :], 4))
                for j in range(4):
                    m = V.mark(ve.tensor_scalar(xn4[:, j, :], src[:, bass.ds(4 * g + j, 1), :].rearrange("p a d -> p (a d)"),
                                                meanvar[:, j, 0:1], rstd[:, j:j + 1], ALU.subtract, ALU.mult))
                if gain is not None:
                    V.after(m)
                    m = V.mark(ve.tensor_tensor(xn4[:, :, :], xn4[:, :, :], over(gain[:, :], 1, [P, 4, D]), ALU.mult))
                    V.after(m)
                    m = V.mark(ve.tensor_tensor(xn4[:, :, :], xn4[:, :, :], over(shift[:, :], 1, [P, 4, D]), ALU.add))
                turned = transpose4(xn4, 0, xT4[:, :], [m])
                if keep is not None:
                    G.after(m)
                    G.mark(gp.tensor_copy(keep[:, bass.ds(4 * g, 4), :], xn4[:, :, :]))
                if keep_t:
                    G.after(turned)
                    G.mark(gp.tensor_copy(XNT[:, bass.ds(g * 512 + A_WIN, 512)], xT4[:, :]))
                hook(g, m, turned)
                fence()

        def project_loop(src, w, bias):
            with nc.Fori(0, NG) as g:
                m = G.mark(gp.tensor_copy(xn4[:, :, :], src[:, bass.ds(4 * g, 4), :]))
                b = G.mark(gp.tensor_tensor(X[:, bass.ds(4 * g, 4), :], X[:, bass.ds(4 * g, 4), :],
                                            over(bias, 1, [P, 4, D]), ALU.add))
                m = transpose4(xn4, 0, xT4[:, :], [m])
                T.after(m)
                for j in range(4):
                    m = T.mark(te.matmul(PS[:, 1, j * P:(j + 1) * P], xT4[:, j * P:(j + 1) * P], w, start=True, stop=True))
                V.after(m, b)
                xg = X[:, bass.ds(4 * g, 4), :]
                V.mark(ve.tensor_tensor(xg, PS[:, 1, :].rearrange("p (j d) -> p j d", j=4), xg, ALU.add))
                fence()

        def window_attention():
            with ExitStack() as own:
                def sl(name, *shape):
                    return own.enter_context(nc.sbuf_tensor("a_" + name, list(shape), F32))
                wq, wk, wv, wo = (sl(n, P, D) for n in ("wq", "wk", "wv", "wo"))
                bq, bk = sl("bq", P, 1), sl("bk", P, 1)
                bv, bo = sl("bv", P, D), sl("bo", P, D)
                headmask = sl("headmask", P, A_H)
                pad = sl("pad", P, NT)
                xw = sl("xw", P, A_WIN + P)
                qT = sl("qT", P, P)
                kT = sl("kT", P, A_WIN + P)
                kTm = sl("kTm", P, A_H, A_WIN + P)
                vc = sl("vc", P, 2, D)
                S = sl("S", P, A_H, P)
                pT = sl("pT", P, A_H, P)
                mx, sm, rs = sl("mx", P, A_H), sl("sm", P, A_H), sl("rs", P, A_H)
                o, oT = sl("o", P, D), sl("oT", P, P)
                for w, n in ((wq, "a_wqT"), (wk, "a_wkT"), (wv, "a_wvT"), (wo, "a_woT"),
                             (headmask, "a_headmask"), (pad, "a_pad")):
                    load(w[:, :], t[n])
                load(bq[:, :], column("a_bq"))
                load(bk[:, :], column("a_bk"))
                load(bv[:, :], row("a_bv", D))
                load(bo[:, :], row("a_bo", D))
                sp.wait_ge(LOAD.sem, LOAD.count)
                fence()
                norm_loop(X, lambda g, m, turned: None)
                with nc.Fori(0, NT) as i:
                    xin = G.mark(gp.tensor_copy(xw[:, :], XNT[:, bass.ds(i * P, A_WIN + P)]))
                    bias = G.mark(gp.tensor_tensor(X[:, bass.ds(i, 1), :], X[:, bass.ds(i, 1), :],
                                                   over(bo[:, :], 1, [P, 1, D]), ALU.add))
                    T.after(xin)
                    te.matmul(PS[:, 0, 0:P], wq[:, :], xw[:, A_WIN:], start=True, stop=True)
                    qk = T.mark(te.matmul(PS[:, 0, P:2 * P + A_WIN], wk[:, :], xw[:, :], start=True, stop=True))
                    for c in range(2):
                        v = T.mark(te.matmul(PS[:, 1, c * P:(c + 1) * P], xw[:, A_WIN * c:A_WIN * c + P], wv[:, :],
                                             start=True, stop=True))
                    A.after(qk)
                    k = A.mark(ac.activation(kT[:, :], PS[:, 0, P:2 * P + A_WIN], ACT.Identity, bias=bk[:, 0:1]))
                    q = A.mark(ac.activation(qT[:, :], PS[:, 0, 0:P], ACT.Identity, bias=bq[:, 0:1]))
                    V.after(k)
                    W_K = A_WIN + P
                    km = V.mark(ve.tensor_tensor(kTm[:, 0:10, :], over(kT[:, :], 1, [P, 10, W_K]),
                                                 over(headmask[:, 0:10], 2, [P, 10, W_K]), ALU.mult))
                    G.after(k)
                    km2 = G.mark(gp.tensor_tensor(kTm[:, 10:, :], over(kT[:, :], 1, [P, A_H - 10, W_K]),
                                                  over(headmask[:, 10:], 2, [P, A_H - 10, W_K]), ALU.mult))
                    V.after(v)
                    vc_in = V.mark(ve.tensor_tensor(vc[:, :, :], PS[:, 1, 0:2 * D].rearrange("p (c d) -> p c d", c=2),
                                                    over(bv[:, :], 1, [P, 2, D]), ALU.add))
                    T.after(q, km)
                    for n in range(4):
                        if n == 2:
                            T.after(km2)
                        for c in range(2):
                            s = T.mark(te.matmul(PS[A_WIN * c:A_WIN * (c + 1), 4 + n, :], qT[:, A_WIN * c:A_WIN * (c + 1)],
                                                 kTm[:, 4 * n:4 * n + 4, A_WIN * c:A_WIN * c + P], start=True, stop=True))
                    first = PS[0:A_WIN, 4:8, :].rearrange("p b (h k) -> p (b h) k", k=P)[:, :, 0:A_WIN]
                    V.after(s)
                    V.after(V.mark(ve.tensor_scalar(first, first, pad[0:A_WIN, bass.ds(i, 1)], None, ALU.add)))
                    scores = PS[:, 4:8, :].rearrange("p b (h k) -> p (b h) k", k=P)
                    V.after(V.mark(ve.tensor_reduce(mx[:, :], scores, AX, ALU.max)))
                    exps = []
                    for n in range(4):
                        sh = S[:, 4 * n:4 * n + 4, :]
                        m = V.mark(ve.tensor_tensor(sh, scores[:, 4 * n:4 * n + 4, :],
                                                    over(mx[:, 4 * n:4 * n + 4], 2, [P, 4, P]), ALU.subtract))
                        A.after(m)
                        exps.append(A.mark(ac.activation(sh, sh, ACT.Exp, scale=float(A_DH) ** -0.5)))
                    T.after(k, v, vc_in)
                    turned = []
                    for n in range(4):
                        T.after(exps[n])
                        for h in range(4 * n, 4 * n + 4):
                            m = T.mark(te.transpose(PS[:, n, (h % 4) * P:(h % 4 + 1) * P], S[:, h, :], ident[:, :]))
                        A.after(m)
                        turned.append(A.mark(ac.copy(pT[:, 4 * n:4 * n + 4, :].rearrange("p a b -> p (a b)"), PS[:, n, :])))
                    V.after(*exps)
                    V.after(V.mark(ve.tensor_reduce(sm[:, :], S[:, :, :], AX, ALU.add)))
                    rsm = V.mark(ve.reciprocal(rs[:, :], sm[:, :]))
                    for h in range(A_H):
                        T.after(turned[h // 4])
                        for c in range(2):
                            m = T.mark(te.matmul(PS[A_WIN * c:A_WIN * (c + 1), 4, h * A_DH:(h + 1) * A_DH],
                                                 pT[:, h, A_WIN * c:A_WIN * (c + 1)], vc[:, c, h * A_DH:(h + 1) * A_DH],
                                                 start=True, stop=True))
                    V.after(m, rsm)
                    m = V.mark(ve.tensor_tensor(o[:, :].rearrange("p (h d) -> p h d", h=A_H),
                                                PS[:, 4, 0:D].rearrange("p (h d) -> p h d", h=A_H),
                                                over(rs[:, :], 2, [P, A_H, A_DH]), ALU.mult))
                    T.after(m)
                    m = T.mark(te.transpose(PS[:, 5, 0:P], o[:, :], ident[:, :]))
                    A.after(m)
                    m = A.mark(ac.copy(oT[:, :], PS[:, 5, 0:P]))
                    T.after(m)
                    m = T.mark(te.matmul(PS[:, 6, 0:D], oT[:, :], wo[:, :], start=True, stop=True))
                    V.after(m, bias)
                    xi = X[:, bass.ds(i, 1), :].rearrange("p a d -> p (a d)")
                    V.mark(ve.tensor_tensor(xi, PS[:, 6, 0:D], xi, ALU.add))
                    fence()

        def mixture(tag):
            with ExitStack() as own:
                def sl(name, *shape):
                    return own.enter_context(nc.sbuf_tensor(tag + name, list(shape), F32))
                gate = sl("gate", P, E_N)
                w13 = sl("w13", P, E_N, 2, D)
                w2 = sl("w2", P, E_N, D)
                b1, b2, b3 = (sl(n, P, E_N, D) for n in ("b1", "b2", "b3"))
                sw12 = sl("sw12", P, 2 * I_SH)
                sw3 = sl("sw3", P, 2, D)
                lower = sl("lower", P, E_N, E_N)
                sc = sl("sc", P, NT, E_N)
                mask = sl("mask", P, NT, E_N)
                r1 = sl("r1", P, NT)
                gt, eq = sl("gt", P, NT, E_N * E_N), sl("eq", P, NT, E_N * E_N)
                xt = sl("xt", P, P)
                hin, x3, hT, y8 = (sl(n, P, E_N, D) for n in ("hin", "x3", "hT", "y8"))
                sg, sT, y1 = sl("sg", P, I_SH), sl("sT", P, I_SH), sl("y1", P, D)
                load(gate[:, :], t["f_gateT"])
                load(w13[:, :, 0, :], t["f_w1T"].rearrange("e d h -> d e h"))
                load(w13[:, :, 1, :], t["f_w3T"].rearrange("e d h -> d e h"))
                load(w2[:, :, :], t["f_w2T"].rearrange("e h d -> h e d"))
                for b, n in ((b1, "f_b1"), (b2, "f_b2"), (b3, "f_b3")):
                    load(b[:, :, :].rearrange("p e d -> p (e d)"),
                         t[n].rearrange("e d -> (e d)").rearrange("(a n) -> a n", a=1).to_broadcast([P, E_N * D]))
                load(sw12[:, :], t["f_sw12T"])
                load(sw3[:, :, :], t["f_sw3T"].rearrange("(c p) d -> p c d", p=P))
                load(lower[:, :, :].rearrange("p a b -> p (a b)"), row("f_lower", E_N * E_N))
                sp.wait_ge(LOAD.sem, LOAD.count)
                fence()

                def gates(g, m, turned):
                    T.after(turned)
                    for j in range(4):
                        m = T.mark(te.matmul(PS[:, 1, j * E_N:(j + 1) * E_N], xT4[:, j * P:(j + 1) * P], gate[:, :],
                                             start=True, stop=True))
                    V.after(m)
                    V.mark(ve.tensor_copy(sc[:, bass.ds(4 * g, 4), :],
                                          PS[:, 1, 0:4 * E_N].rearrange("p (j e) -> p j e", j=4)))

                norm_loop(X, gates)
                all3 = [P, NT, E_N]
                V.after(V.mark(ve.tensor_reduce(r1[:, :], sc[:, :, :], AX, ALU.max)))
                m = V.mark(ve.tensor_tensor(sc[:, :, :], sc[:, :, :], over(r1[:, :], 2, all3), ALU.subtract))
                A.after(m)
                m = A.mark(ac.activation(sc[:, :, :], sc[:, :, :], ACT.Exp))
                V.after(m)
                V.after(V.mark(ve.tensor_reduce(r1[:, :], sc[:, :, :], AX, ALU.add)))
                V.after(V.mark(ve.reciprocal(r1[:, :], r1[:, :])))
                V.after(V.mark(ve.tensor_tensor(sc[:, :, :], sc[:, :, :], over(r1[:, :], 2, all3), ALU.mult)))
                four = [P, NT, E_N, E_N]
                gt4 = gt[:, :, :].rearrange("p t (a b) -> p t a b", a=E_N)
                eq4 = eq[:, :, :].rearrange("p t (a b) -> p t a b", a=E_N)
                rival, own_s = over(sc[:, :, :], 2, four), over(sc[:, :, :], 3, four)
                V.mark(ve.tensor_tensor(gt4, rival, own_s, ALU.is_gt))
                V.after(V.mark(ve.tensor_tensor(eq4, rival, own_s, ALU.is_equal)))
                V.after(V.mark(ve.tensor_tensor(eq[:, :, :], eq[:, :, :],
                                                over(lower[:, :, :].rearrange("p a b -> p (a b)"), 1, [P, NT, E_N * E_N]),
                                                ALU.mult)))
                V.after(V.mark(ve.tensor_tensor(gt[:, :, :], gt[:, :, :], eq[:, :, :], ALU.add)))
                V.after(V.mark(ve.tensor_reduce(mask[:, :, :], gt4, AX, ALU.add)))
                V.mark(ve.tensor_scalar(mask[:, :, :], mask[:, :, :], 1.5, None, ALU.is_lt))
                fence()
                with nc.Fori(0, NT) as i:
                    xin = G.mark(gp.tensor_copy(xt[:, :], XNT[:, bass.ds(i * P + A_WIN, P)]))
                    T.after(xin)
                    z12 = T.mark(te.matmul(PS[:, 7, :], xt[:, :], sw12[:, :], start=True, stop=True))
                    u = [T.mark(te.matmul(PS[:, n, :], xt[:, :],
                                          w13[:, 2 * n:2 * n + 2, :, :].rearrange("p e k h -> p (e k h)"),
                                          start=True, stop=True)) for n in range(4)]
                    A.after(z12)
                    m = A.mark(ac.activation(sg[:, :], PS[:, 7, 0:I_SH], ACT.Silu))
                    V.after(m)
                    zs = V.mark(ve.tensor_tensor(sg[:, :], sg[:, :], PS[:, 7, I_SH:], ALU.mult))
                    hs, x3s = [], []
                    for e in range(E_N):
                        V.after(u[e // 2])
                        s = sc[:, bass.ds(i, 1), e:e + 1].rearrange("p a e -> p (a e)")
                        m = V.mark(ve.scalar_tensor_tensor(hin[:, e, :], PS[:, e // 2, (e % 2) * 256:(e % 2) * 256 + D],
                                                           s, b1[:, e, :], ALU.mult, ALU.add))
                        x3s.append(V.mark(ve.scalar_tensor_tensor(
                            x3[:, e, :], PS[:, e // 2, (e % 2) * 256 + D:(e % 2) * 256 + 2 * D],
                            s, b3[:, e, :], ALU.mult, ALU.add)))
                        if e % 2:
                            A.after(m)
                            hs.append(A.mark(ac.activation(hin[:, e - 1:e + 1, :], hin[:, e - 1:e + 1, :], ACT.Silu)))
                    G.after(x3s[-1])
                    x3m = G.mark(gp.tensor_tensor(x3[:, :, :], x3[:, :, :],
                                                  over(mask[:, bass.ds(i, 1), :].rearrange("p a e -> p (a e)"), 2, [P, E_N, D]),
                                                  ALU.mult))
                    T.after(zs)
                    for j in range(2):
                        m = T.mark(te.transpose(PS[:, 4, j * P:(j + 1) * P], sg[:, j * P:(j + 1) * P], ident[:, :]))
                    A.after(m)
                    sTm = A.mark(ac.copy(sT[:, :], PS[:, 4, 0:I_SH]))
                    T.after(sTm)
                    for j in range(2):
                        z = T.mark(te.matmul(PS[:, 7, 0:D], sT[:, j * P:(j + 1) * P], sw3[:, j, :], start=(j == 0), stop=(j == 1)))
                    xi = X[:, bass.ds(i, 1), :].rearrange("p a d -> p (a d)")
                    V.after(z)
                    xz = V.mark(ve.tensor_tensor(xi, PS[:, 7, 0:D], xi, ALU.add))
                    for n in range(2):
                        T.after(hs[2 * n + 1], sTm)
                        for e in range(4 * n, 4 * n + 4):
                            m = T.mark(te.transpose(PS[:, 4 + n, (e % 4) * P:(e % 4 + 1) * P], hin[:, e, :], ident[:, :]))
                        A.after(m)
                        m = A.mark(ac.copy(hT[:, 4 * n:4 * n + 4, :].rearrange("p a b -> p (a b)"), PS[:, 4 + n, :]))
                        T.after(m, xz)
                        for e in range(4 * n, 4 * n + 4):
                            m = T.mark(te.matmul(PS[:, 6 + n, (e % 4) * D:(e % 4 + 1) * D], hT[:, e, :], w2[:, e, :],
                                                 start=True, stop=True))
                        V.after(m)
                        half = y8[:, 4 * n:4 * n + 4, :]
                        V.after(V.mark(ve.tensor_tensor(half, PS[:, 6 + n, :].rearrange("p (e d) -> p e d", e=4),
                                                        b2[:, 4 * n:4 * n + 4, :], ALU.add)))
                        V.after(x3m)
                        m = V.mark(ve.tensor_tensor(half, half, x3[:, 4 * n:4 * n + 4, :], ALU.mult))
                    V.after(m)
                    V.after(V.mark(ve.tensor_reduce(y1[:, :], y8[:, :, :].rearrange("p e d -> p d e"), AX, ALU.add)))
                    V.mark(ve.tensor_tensor(xi, xi, y1[:, :], ALU.add))
                    fence()

        def causal_attention():
            with ExitStack() as own:
                def sl(name, *shape):
                    return own.enter_context(nc.sbuf_tensor("b_" + name, list(shape), F32))
                wqk, wov = sl("wqk", P, D), sl("wov", P, D)
                future = sl("future", P, 2 * L - P)
                QT = sl("QT", P, NT * P)
                XV = sl("XV", P, NT, D)
                q, S, pT = sl("q", P, P), sl("S", P, L), sl("pT", P, L)
                mx, nmx, sm, rs = (sl(n, P, 1) for n in ("mx", "nmx", "sm", "rs"))
                for w, n in ((wqk, "b_wqk"), (wov, "b_wov"), (future, "b_future")):
                    load(w[:, :], t[n])
                sp.wait_ge(LOAD.sem, LOAD.count)
                fence()

                def products(g, m, turned):
                    T.after(turned)
                    m = T.mark(te.matmul(PS[:, 1, :], wqk[:, :], xT4[:, :], start=True, stop=True))
                    V.after(m)
                    V.mark(ve.tensor_copy(QT[:, bass.ds(g * 512, 512)], PS[:, 1, :]))
                    for j in range(4):
                        m = T.mark(te.matmul(PS[:, 2, j * D:(j + 1) * D], xT4[:, j * P:(j + 1) * P], wov[:, :],
                                             start=True, stop=True))
                    V.after(m)
                    V.mark(ve.tensor_copy(XV[:, bass.ds(4 * g, 4), :], PS[:, 2, :].rearrange("p (j d) -> p j d", j=4)))

                norm_loop(X, products)
                with nc.Fori(0, B) as b:
                    with nc.Fori(0, TB) as i:
                        m = G.mark(gp.tensor_copy(q[:, :], QT[:, bass.ds(b * L + i * P, P)]))
                        T.after(m)
                        for n in range(2):
                            m = T.mark(te.matmul(PS[:, n, :], q[:, :], XNT[:, bass.ds(b * L + A_WIN + n * 512, 512)],
                                                 start=True, stop=True))
                        V.after(m)
                        V.after(V.mark(ve.tensor_tensor(S[:, :], flat(0, 2), future[:, bass.ds(L - P - i * P, L)], ALU.add)))
                        V.after(V.mark(ve.tensor_reduce(mx[:, :], S[:, :], AX, ALU.max)))
                        m = V.mark(ve.tensor_scalar(nmx[:, :], mx[:, :], -1.0, None, ALU.mult))
                        A.after(m)
                        m = A.mark(ac.activation(S[:, :], S[:, :], ACT.Exp, bias=nmx[:, 0:1], accum_out=sm[:, 0:1]))
                        V.after(m)
                        rsm = V.mark(ve.reciprocal(rs[:, :], sm[:, :]))
                        T.after(m)
                        for n in range(2):
                            for j in range(4):
                                c = 4 * n + j
                                m = T.mark(te.transpose(PS[:, 2 + n, j * P:(j + 1) * P], S[:, c * P:(c + 1) * P], ident[:, :]))
                            A.after(m)
                            m = A.mark(ac.copy(pT[:, n * 512:(n + 1) * 512], PS[:, 2 + n, :]))
                            T.after(m)
                            for c in range(4 * n, 4 * n + 4):
                                m = T.mark(te.matmul(PS[:, 4, 0:D], pT[:, c * P:(c + 1) * P],
                                                     XV[:, bass.ds(b * TB + c, 1), :].rearrange("p a d -> p (a d)"),
                                                     start=(c == 0), stop=(c == TB - 1)))
                        V.after(m, rsm)
                        xi = X[:, bass.ds(b * TB + i, 1), :].rearrange("p a d -> p (a d)")
                        V.mark(ve.scalar_tensor_tensor(xi, PS[:, 4, 0:D], rs[:, 0:1], xi, ALU.mult, ALU.add))
                        fence()

        full = [P, TB, H, DH]

        def split(ap):
            return ap.rearrange("p i (h d) -> p i h d", h=H)

        def cope_attention():
            with ExitStack() as own:
                def sl(name, *shape):
                    return own.enter_context(nc.sbuf_tensor("c_" + name, list(shape), F32))
                w = sl("w", P, 3 * D)
                bqkv = sl("bqkv", P, 3 * D)
                wo, bo = sl("wo", P, D), sl("bo", P, D)
                pos_rows = sl("pos_rows", P, DH, 3)
                qkv = sl("qkv", P, NT, 3 * D)
                prod, prod2 = sl("prod", P, TB, D), sl("prod2", P, TB, D)
                dots = sl("dots", P, 2, 2, P)
                tab = sl("tab", P, 2, 3, P)
                gates = sl("gates", P, 2, 2, P)
                w1, w2 = sl("w1", P, 2, 2, P), sl("w2", P, 2, 2, P)
                d1, d2 = sl("d1", P, 2, P), sl("d2", P, 2, P)
                mx = sl("mx", P, 2, P)
                att = sl("att", P, NT, D)
                for n in range(3):
                    load(w[:, n * D:(n + 1) * D], t[("c_wq", "c_wk", "c_wv")[n]])
                    load(bqkv[:, n * D:(n + 1) * D], row(("c_bq", "c_bk", "c_bv")[n], D))
                load(wo[:, :], t["c_wo"])
                load(bo[:, :], row("c_bo", D))
                for d in range(DH):
                    load(pos_rows[:, d, :], t["c_pos"][0, d:d + 1, 0:3].to_broadcast([P, 3]))
                sp.wait_ge(LOAD.sem, LOAD.count)
                fence()

                def products(g, m, turned):
                    T.after(turned)
                    for j in range(4):
                        m = T.mark(te.matmul(PS[:, 1 + j, 0:3 * D], xT4[:, j * P:(j + 1) * P], w[:, :], start=True, stop=True))
                    V.after(m)
                    V.mark(ve.tensor_tensor(qkv[:, bass.ds(4 * g, 4), :], PS[:, 1:5, 0:3 * D],
                                            over(bqkv[:, :], 1, [P, 4, 3 * D]), ALU.add))

                norm_loop(X, products)

                def part(s, n):
                    return qkv[:, TB * s:TB * (s + 1), n * D:(n + 1) * D]

                for s in range(2):
                    for k in range(2):
                        V.after(V.mark(ve.tensor_tensor(prod[:, :, :], part(s, 0), part(k, 1), ALU.mult)))
                        V.after(V.mark(ve.tensor_reduce(dots[:, s, k, :].rearrange("p (i h) -> p i h", h=H), split(prod[:, :, :]), AX, ALU.add)))
                    for n in range(3):
                        pe = pos_rows[:, :, n].unsqueeze(1).unsqueeze(1).to_broadcast(full)
                        V.after(V.mark(ve.tensor_tensor(split(prod[:, :, :]), split(part(s, 0)), pe, ALU.mult)))
                        m = V.mark(ve.tensor_reduce(tab[:, s, n, :].rearrange("p (i h) -> p i h", h=H), split(prod[:, :, :]), AX, ALU.add))
                        V.after(m)
                scale = float(DH) ** -0.5
                A.after(m)
                m = A.mark(ac.activation(gates[:, :, :, :], dots[:, :, :, :], ACT.Tanh, scale=scale / 2))
                V.after(m)
                V.after(V.mark(ve.tensor_scalar(gates[:, :, :, :], gates[:, :, :, :], 0.5, 0.5, ALU.mult, ALU.add)))
                V.after(V.mark(ve.tensor_tensor(gates[:, :, 0, :], gates[:, :, 0, :], gates[:, :, 1, :], ALU.add)))
                V.after(V.mark(ve.tensor_scalar(gates[:, :, :, :], gates[:, :, :, :], 124.0, None, ALU.min)))
                V.mark(ve.tensor_scalar(w1[:, :, :, :], gates[:, :, :, :], 1.0, None, ALU.min))
                V.mark(ve.tensor_scalar(w2[:, :, :, :], gates[:, :, :, :], 1.0, 0.0, ALU.subtract, ALU.max))
                V.mark(ve.tensor_tensor(d1[:, :, :], tab[:, :, 1, :], tab[:, :, 0, :], ALU.subtract))
                V.after(V.mark(ve.tensor_tensor(d2[:, :, :], tab[:, :, 2, :], tab[:, :, 1, :], ALU.subtract)))
                two = [P, 2, 2, P]
                V.mark(ve.tensor_tensor(w1[:, :, :, :], w1[:, :, :, :], over(d1[:, :, :], 2, two), ALU.mult))
                V.after(V.mark(ve.tensor_tensor(w2[:, :, :, :], w2[:, :, :, :], over(d2[:, :, :], 2, two), ALU.mult)))
                V.after(V.mark(ve.tensor_tensor(w1[:, :, :, :], w1[:, :, :, :], w2[:, :, :, :], ALU.add)))
                V.after(V.mark(ve.tensor_tensor(w1[:, :, :, :], w1[:, :, :, :], over(tab[:, :, 0, :], 2, two), ALU.add)))
                V.after(V.mark(ve.scalar_tensor_tensor(dots[:, :, :, :].rearrange("p a b c -> p (a b c)"),
                                                       dots[:, :, :, :].rearrange("p a b c -> p (a b c)"), scale,
                                                       w1[:, :, :, :].rearrange("p a b c -> p (a b c)"), ALU.mult, ALU.add)))
                V.after(V.mark(ve.tensor_tensor(mx[:, :, :], dots[:, :, 0, :], dots[:, :, 1, :], ALU.max)))
                m = V.mark(ve.tensor_tensor(dots[:, :, :, :], dots[:, :, :, :], over(mx[:, :, :], 2, two), ALU.subtract))
                A.after(m)
                m = A.mark(ac.activation(dots[:, :, :, :], dots[:, :, :, :], ACT.Exp))
                V.after(m)
                V.after(V.mark(ve.tensor_tensor(mx[:, :, :], dots[:, :, 0, :], dots[:, :, 1, :], ALU.add)))
                V.after(V.mark(ve.reciprocal(mx[:, :, :], mx[:, :, :])))
                V.after(V.mark(ve.tensor_tensor(dots[:, :, :, :], dots[:, :, :, :], over(mx[:, :, :], 2, two), ALU.mult)))
                for s in range(2):
                    for k, to in ((0, prod), (1, prod2)):
                        a = over(dots[:, s, k, :].rearrange("p (i h) -> p i h", h=H), 3, full)
                        m = V.mark(ve.tensor_tensor(split(to[:, :, :]), split(part(k, 2)), a, ALU.mult))
                    V.after(m)
                    V.after(V.mark(ve.tensor_tensor(att[:, TB * s:TB * (s + 1), :], prod[:, :, :], prod2[:, :, :], ALU.add)))
                fence()
                project_loop(att, wo[:, :], bo[:, :])

        def linear_attention():
            f, S4 = 4, D // 4
            with ExitStack() as own:
                def sl(name, *shape):
                    return own.enter_context(nc.sbuf_tensor("d_" + name, list(shape), F32))
                ws = {n: sl("w" + n, P, D) for n in "qkvo"}
                bs = {n: sl("b" + n, P, D) for n in "qkvo"}
                fact = sl("fact", P, 4, f, f)
                blocks = sl("blocks", P, 4, f, S4)
                g1, b1, g2, b2 = (sl(n, P, D) for n in ("g1", "b1", "g2", "b2"))
                tmp = sl("tmp", P, D)
                q, kv = sl("q", P, NT, D), sl("kv", P, NT, 2 * D)
                QN = sl("QN", P, NT, D)
                prod, prod2 = sl("prod", P, TB, D), sl("prod2", P, TB, D)
                dots = sl("dots", P, 2, 2, P)
                den = sl("den", P, 2, P)
                att = sl("att", P, NT, D)
                for m4, n in enumerate("qkvo"):
                    for i in range(f):
                        lo = i * S4
                        load(blocks[lo:lo + S4, m4, :, :], t[f"d_{n}S"].rearrange("n k l -> k n l"))
                        load(fact[lo:lo + S4, m4, :, :], t[f"d_{n}A"][:, i:i + 1, :].rearrange("n i j -> i n j").to_broadcast([S4, f, f]))
                    load(bs[n][:, :], row(f"d_{n}b", D))
                for b, n in ((g1, "d_g1"), (b1, "d_b1"), (g2, "d_g2"), (b2, "d_b2")):
                    load(b[:, :], row(n, D))
                V.after((LOAD, LOAD.count))
                for m4, n in enumerate("qkvo"):
                    shape = [P, f, S4]
                    for k in range(f):
                        to = (ws[n] if k == 0 else tmp)[:, :].rearrange("p (j l) -> p j l", j=f)
                        m = V.mark(ve.tensor_tensor(to, over(fact[:, m4, k, :], 2, shape), over(blocks[:, m4, k, :], 1, shape), ALU.mult))
                        V.after(m)
                        if k:
                            V.after(V.mark(ve.tensor_tensor(ws[n][:, :], ws[n][:, :], tmp[:, :], ALU.add)))
                fence()

                def keys_values(g, m, turned):
                    T.after(turned)
                    for j in range(4):
                        for c, n in enumerate("kv"):
                            m = T.mark(te.matmul(PS[:, 1 + j, c * D:(c + 1) * D], xT4[:, j * P:(j + 1) * P], ws[n][:, :],
                                                 start=True, stop=True))
                    V.after(m)
                    for c, n in enumerate("kv"):
                        to = kv[:, bass.ds(4 * g, 4), c * D:(c + 1) * D]
                        m = V.mark(ve.tensor_tensor(to, PS[:, 1:5, c * D:(c + 1) * D], over(bs[n][:, :], 1, [P, 4, D]), ALU.add))
                        if n == "k":
                            V.after(m)
                            V.mark(ve.tensor_scalar(to, to, 0.0, None, ALU.max))

                def queries(g, m, turned):
                    T.after(turned)
                    for j in range(4):
                        m = T.mark(te.matmul(PS[:, 1 + j, 0:D], xT4[:, j * P:(j + 1) * P], ws["q"][:, :], start=True, stop=True))
                    V.after(m)
                    to = q[:, bass.ds(4 * g, 4), :]
                    V.after(V.mark(ve.tensor_tensor(to, PS[:, 1:5, 0:D], over(bs["q"][:, :], 1, [P, 4, D]), ALU.add)))
                    V.mark(ve.tensor_scalar(to, to, 0.0, None, ALU.max))

                norm_loop(X, keys_values, keep=XN, keep_t=False)
                norm_loop(XN, queries, gain=g1, shift=b1, keep=QN, keep_t=False)
                at = np.float32(np.pi / 2) * np.arange(1, B + 1, dtype=np.float32) / np.float32(B)
                sin, cos = np.sin(at).astype(np.float32), np.cos(at).astype(np.float32)
                for s in range(2):
                    for k in range(2):
                        V.after(V.mark(ve.tensor_tensor(prod[:, :, :], q[:, TB * s:TB * (s + 1), :],
                                                        kv[:, TB * k:TB * (k + 1), 0:D], ALU.mult)))
                        to = dots[:, s, k, :].rearrange("p (i h) -> p i h", h=H)
                        V.after(V.mark(ve.tensor_reduce(to, split(prod[:, :, :]), AX, ALU.add)))
                        V.after(V.mark(ve.tensor_scalar(to, to, float(sin[s] * sin[k] + cos[s] * cos[k]), None, ALU.mult)))
                V.after(V.mark(ve.tensor_tensor(den[:, :, :], dots[:, :, 0, :], dots[:, :, 1, :], ALU.add)))
                V.after(V.mark(ve.tensor_scalar(den[:, :, :], den[:, :, :], 1e-6, None, ALU.max)))
                V.after(V.mark(ve.reciprocal(den[:, :, :], den[:, :, :])))
                V.after(V.mark(ve.tensor_tensor(dots[:, :, :, :], dots[:, :, :, :], over(den[:, :, :], 2, [P, 2, 2, P]), ALU.mult)))
                for s in range(2):
                    for k, to in ((0, prod), (1, prod2)):
                        a = over(dots[:, s, k, :].rearrange("p (i h) -> p i h", h=H), 3, full)
                        m = V.mark(ve.tensor_tensor(split(to[:, :, :]), split(kv[:, TB * k:TB * (k + 1), D:]), a, ALU.mult))
                    V.after(m)
                    V.after(V.mark(ve.tensor_tensor(prod[:, :, :], prod[:, :, :], prod2[:, :, :], ALU.add)))
                    V.after(V.mark(ve.tensor_tensor(att[:, TB * s:TB * (s + 1), :], prod[:, :, :], QN[:, TB * s:TB * (s + 1), :], ALU.add)))
                fence()

                def add_out(g, m, turned):
                    T.after(turned)
                    for j in range(4):
                        w = T.mark(te.matmul(PS[:, 1, j * P:(j + 1) * P], xT4[:, j * P:(j + 1) * P], ws["o"][:, :], start=True, stop=True))
                    xg = X[:, bass.ds(4 * g, 4), :]
                    V.after(m)
                    V.after(V.mark(ve.tensor_tensor(xg, xg, xn4[:, :, :], ALU.add)))
                    V.after(V.mark(ve.tensor_tensor(xg, xg, over(bs["o"][:, :], 1, [P, 4, D]), ALU.add)))
                    V.after(w)
                    V.mark(ve.tensor_tensor(xg, PS[:, 1, :].rearrange("p (j d) -> p j d", j=4), xg, ALU.add))

                norm_loop(att, add_out, gain=g2, shift=b2, keep_t=False)

        def local_stack(tag):
            with ExitStack() as own:
                def sl(name, *shape, dtype=F32):
                    return own.enter_context(nc.sbuf_tensor(tag + name, list(shape), dtype))
                Y = XN
                wqkv = sl("wqkv", P, 3 * INNER)
                wo = sl("wo", P, LH // 2, D)
                w1 = sl("w1", P, 2 * HID)
                w2 = sl("w2", P, 3, D)
                b1 = sl("b1", P, 2, 3)
                lng, lnb = sl("lng", P, 1), sl("lnb", P, 1)
                qs, ks = sl("qs", P, LD), sl("ks", P, LD)
                base = sl("base", P, 4, TB, LD)
                rot = sl("rot", P, 4, NT, LD)
                mask = sl("mask", P, NT, 2 * LW, dtype=BF16)
                ident_b = sl("ident_b", P, P, dtype=BF16)
                keep = sl("keep", P, NT)
                XST = sl("XST", P, NT * P)
                sq = sl("sq", P, 2, INNER)
                ssq, irt, itm = (sl(n, P, 2 * LH) for n in ("ssq", "irt", "itm"))
                QN, QR, T2 = sl("QN", P, LH, LD), sl("QR", P, LH, LD), sl("T2", P, LH, LD)
                KN, KR, T3 = sl("KN", P, LH, LD), sl("KR", P, LH, LD), sl("T3", P, LH, LD)
                qT = sl("qT", P, 8, P)
                kT = sl("kT", P, 8, LW + P)
                Vt = sl("Vt", P, 2, INNER)
                V2 = sl("V2", P, 4, 8, LD)
                S = sl("S", P, 2, 8, 2 * LW)
                Pm = sl("Pm", P, 8, 2, 2 * LW)
                pT = sl("pT", P, 8, P)
                mx, sm, rs = (sl(n, P, 2, 8) for n in ("mx", "sm", "rs"))
                O, oT = sl("O", P, 8, 2, LD), sl("oT", P, 8, P)
                xc = sl("xc", P, NT * P)
                xsq, rst = sl("xsq", P, NG, 512), sl("rst", P, NG, 512)
                vrt = sl("vrt", P, NG, 4)
                gl, hT = sl("gl", P, 2, 512), sl("hT", P, 2, 3, 512)

                def load_attention(l):
                    load(wqkv[:, :], t["l_wqkv"][bass.ds(l, 1), :, :].rearrange("a d n -> (a d) n"))
                    load(wo[:, :, :], t["l_wo"][bass.ds(l, 1), :, :].rearrange("a (c p) d -> p (a c) d", p=P))
                    load(qs[:, :], t["l_qs"][bass.ds(l, 1), :].to_broadcast([P, LD]))
                    load(ks[:, :], t["l_ks"][bass.ds(l, 1), :].to_broadcast([P, LD]))

                def load_ffn(l):
                    load(w1[:, :], t["l_w1"][bass.ds(l, 1), :, :].rearrange("a d n -> (a d) n"))
                    for c, n in enumerate(HCH):
                        load(w2[0:n, c, :], t["l_w2"][bass.ds(l, 1), c * P:c * P + n, :].rearrange("a p d -> (a p) d"))
                        for k in range(2):
                            load(b1[0:n, k, c:c + 1], t["l_b1"][bass.ds(l, 1), k * HID + c * P:k * HID + c * P + n].rearrange("a (p c) -> p (a c)", c=1))
                    load(w2[HCH[2]:HCH[2] + 1, 2, :], t["l_b2"][bass.ds(l, 1), :])
                    load(lng[:, :], t["l_g"][bass.ds(l, 1), :].rearrange("a (p c) -> p (a c)", c=1))
                    load(lnb[:, :], t["l_b"][bass.ds(l, 1), :].rearrange("a (p c) -> p (a c)", c=1))

                for r in range(4):
                    load(base[:, r, :, :], t["l_rot"][r].rearrange("(i p) d -> p i d", p=P))
                load(mask[:, :, :], t["l_mask"])
                load(ident_b[:, :], t["ident_b"])
                load(keep[:, :], t["l_keep"])
                load_attention(0)
                G.after(G.mark(gp.memset(XST[64:, :], 0.0)))
                G.after(G.mark(gp.memset(hT[64:, :, 2, :], 1.0)))
                G.after(G.mark(gp.memset(kT[:, :, :], 0.0)))
                G.after(G.mark(gp.memset(V2[:, :, :, :], 0.0)))
                sp.wait_ge(LOAD.sem, LOAD.count)
                fence()

                def shifted_transpose():
                    done = []
                    for g in range(NG):
                        for j in range(4):
                            m = T.mark(te.transpose(PS[:, g, j * P:(j + 1) * P], Y[:, 4 * g + j, :], ident[:, :]))
                        n = 511 if g % 2 else 512
                        A.after(m)
                        A.mark(ac.copy(XST[0:64, g * 512:(g + 1) * 512], PS[0:64, g, :]))
                        done.append(A.mark(ac.copy(XST[64:, g * 512 + 1:g * 512 + 1 + n], PS[64:, g, 0:n])))
                    return done

                last = {}

                def used(*names):
                    return [last[n] for n in names if n in last]

                def project_qk(n, c):
                    T.after(*used(f"banks {2 * c}-{2 * c + 1} read"))
                    for b in range(2 * c, 2 * c + 2):
                        m = te.matmul(PS[:, b, :], XST[:, n * P:(n + 1) * P], wqkv[:, b * 512:(b + 1) * 512], start=True, stop=True)
                    A.after(T.mark(m), *used(f"sq{c} read"))
                    last[f"sq{c}"] = A.mark(ac.activation(sq[:, c, :], flat(2 * c, 2 * c + 2), ACT.Square))

                def project_norms():
                    for c in range(2):
                        V.after(last[f"sq{c}"])
                        m = last[f"sq{c} read"] = V.mark(ve.tensor_reduce(
                            ssq[:, c * LH:(c + 1) * LH], sq[:, c, :].rearrange("p (h d) -> p h d", d=LD), AX, ALU.add))
                    V.after(m)
                    V.after(V.mark(ve.tensor_scalar(ssq[:, :], ssq[:, :], 1e-24, None, ALU.max)))
                    i32 = mybir.dt.int32
                    V.after(V.mark(ve.tensor_scalar(itm[:, :].bitcast(i32), ssq[:, :].bitcast(i32), 1, None, ALU.logical_shift_right)))
                    V.after(V.mark(ve.tensor_scalar(irt[:, :].bitcast(i32), itm[:, :].bitcast(i32), -1.0, float(0x5F3759DF), ALU.mult, ALU.add)))
                    for _ in range(3):
                        V.after(V.mark(ve.scalar_tensor_tensor(itm[:, :], irt[:, :], -0.5, irt[:, :], ALU.mult, ALU.mult)))
                        V.after(V.mark(ve.tensor_tensor(itm[:, :], itm[:, :], ssq[:, :], ALU.mult)))
                        V.after(V.mark(ve.scalar_tensor_tensor(irt[:, :], itm[:, :], 1.5, irt[:, :], ALU.add, ALU.mult)))

                def project_norm(c):
                    N = (QN, KN)[c]
                    src = PS[:, 2 * c:2 * c + 2, :].rearrange("p b (h d) -> p (b h) d", d=LD)
                    V.after(*used(f"N{c} read"))
                    last[f"N{c}"] = last[f"banks {2 * c}-{2 * c + 1} read"] = V.mark(ve.tensor_tensor(
                        N[:, :, :], src, over(irt[:, c * LH:(c + 1) * LH], 2, [P, LH, LD]), ALU.mult))

                def project_sine(n, c):
                    N, U = ((QN, T2), (KN, T3))[c]
                    G.after(last[f"N{c}"])
                    half = LD // 2
                    for k in range(2):
                        lo, hi = k * half, (1 - k) * half
                        last[f"U{c}"] = G.mark(gp.tensor_tensor(U[:, :, lo:lo + half], N[:, :, hi:hi + half],
                                                                over(rot[:, 2 * c + 1, n, lo:lo + half], 1, [P, LH, half]), ALU.mult))

                def project_cosine(n, c):
                    N, R = ((QN, QR), (KN, KR))[c]
                    V.after(last[f"N{c}"], *used(f"R{c} read"))
                    last[f"C{c}"] = V.mark(ve.tensor_tensor(R[:, :, :], N[:, :, :], over(rot[:, 2 * c, n, :], 1, [P, LH, LD]), ALU.mult))

                def project_sum(c):
                    R, U = ((QR, T2), (KR, T3))[c]
                    last[f"N{c} read"] = last[f"U{c}"]
                    G.after(last[f"U{c}"], last[f"C{c}"])
                    last[f"R{c}"] = G.mark(gp.tensor_tensor(R[:, :, :], R[:, :, :], U[:, :, :], ALU.add))

                def project_v(n):
                    par = n % 2
                    T.after(*used("banks 0-1 read"))
                    for r in range(2):
                        wv = wqkv[:, 2 * INNER:].rearrange("p (c r d) -> p r c d", r=2, d=LD)[:, r, :, :]
                        m = te.matmul(PS[:, r, :], XST[:, n * P:(n + 1) * P], wv, start=True, stop=True)
                    A.after(T.mark(m), *used(f"V{par} read"))
                    last["banks 0-1 read"] = last[f"V{par}"] = A.mark(ac.copy(Vt[:, par, :], flat(0, 2)))

                def to_bank(bank, blocks):
                    T.after(*used(f"bank {bank} read"))
                    for k, block in enumerate(blocks):
                        m = te.transpose(PS[:, bank, k * P:(k + 1) * P], block, ident[:, :])
                    return T.mark(m)

                def keep_halo(n):
                    G.after(*used("scores", "kT"))
                    last["kT halo"] = G.mark(gp.tensor_tensor(kT[:, :, 0:LW], kT[:, :, P:], over(keep[:, n:n + 1], 1, [P, 8, LW]), ALU.mult))

                def turn(c, b):
                    R, dst, lo = ((QR, qT, 0), (KR, kT, LW))[c]
                    bank = 4 + b
                    T.after(*used(f"R{c}"))
                    m = last[f"R{c} read"] = to_bank(bank, [R[:, 2 * k:2 * k + 2, :].rearrange("p r d -> p (r d)") for k in range(4 * b, 4 * b + 4)])
                    A.after(m, *used("scores", *(["kT halo"] if c else [])))
                    last["kT" if c else "qT"] = last[f"bank {bank} read"] = A.mark(
                        ac.copy(dst[:, 4 * b:4 * b + 4, lo:lo + P], PS[:, bank, :].rearrange("p (c q) -> p c q", c=4)))

                def spread_v(n):
                    par = n % 2
                    HALO.after(*used("pv"), *used("V2"))
                    for r in range(2):
                        halo = HALO.mark(sp.dma_start(V2[64 * r:64 * r + LW, 0, :, :], V2[64 * r + LW:64 * r + 64, 3, :, :]))
                    VDMA.after(*used(f"V{par}"))
                    for w in range(4):
                        if w == 3:
                            VDMA.after(halo)
                        for r in range(2):
                            cols = Vt[:, par, r * 512:(r + 1) * 512].rearrange("p (c d) -> p c d", d=LD)
                            if w == 0:
                                m = VDMA.mark(sp.dma_start(V2[64 * r + LW:64 * r + 64, 0, :, :], cols[0:LW]))
                            else:
                                m = VDMA.mark(sp.dma_start(V2[64 * r:64 * r + 64, w, :, :], cols[LW * (w - 1):LW * (w + 1)]))
                    last["V2"] = last[f"V{par} read"] = m

                def scores(i, r):
                    T.after(*used("qT", "kT", "kT halo", f"bank {6 + r} read"))
                    te.matmul(PS[:, 6 + r, :], ident_b[:, :], over(mask[:, i, :], 1, [P, 8, 2 * LW]),
                              start=True, stop=False, skip_group_check=True)
                    for c in range(8):
                        for w in range(4):
                            m = te.matmul(PS[LW * w:LW * (w + 1), 6 + r, c * 64:(c + 1) * 64],
                                          qT[64 * r:64 * r + 64, c, LW * w:LW * (w + 1)],
                                          kT[64 * r:64 * r + 64, c, LW * w:LW * w + 64], start=False, stop=True,
                                          skip_group_check=True)
                    last["scores"] = T.mark(m)
                    s = PS[:, 6 + r, :].rearrange("p (c k) -> p c k", c=8)
                    V.after(last["scores"], *used(f"mx{r} read"))
                    m = V.mark(ve.tensor_reduce(mx[:, r, :], s, AX, ALU.max))
                    V.after(m, *used(f"P{r}"))
                    m = V.mark(ve.tensor_tensor(S[:, r, :, :], s, over(mx[:, r, :], 2, [P, 8, 2 * LW]), ALU.subtract))
                    last[f"mx{r} read"] = last[f"bank {6 + r} read"] = m
                    A.after(m, *used("Pm read", "Pm summed"))
                    last[f"P{r}"] = A.mark(ac.activation(Pm[:, :, r, :], S[:, r, :, :], ACT.Exp))

                def sums():
                    V.after(last["P0"], last["P1"], *used("rs read"))
                    for r in range(2):
                        m = V.mark(ve.tensor_reduce(sm[:, r, :], Pm[:, :, r, :], AX, ALU.add))
                    last["Pm summed"] = m
                    V.after(m)
                    last["rs"] = V.mark(ve.reciprocal(rs[:, :, :], sm[:, :, :]))

                def weights_turn(b):
                    T.after(last["P0"], last["P1"])
                    m = last["Pm read"] = to_bank(6 + b, [Pm[:, c, :, :].rearrange("p r k -> p (r k)") for c in range(4 * b, 4 * b + 4)])
                    A.after(m, *used("pv"))
                    last["pT"] = last[f"bank {6 + b} read"] = A.mark(
                        ac.copy(pT[:, 4 * b:4 * b + 4, :].rearrange("p c q -> p (c q)"), PS[:, 6 + b, :]))

                def values():
                    T.after(last["pT"], *used("V2"))
                    pvs = []
                    for r in range(2):
                        T.after(*used(f"bank {6 + r} read"))
                        for c in range(8):
                            for w in range(4):
                                m = te.matmul(PS[LW * w:LW * (w + 1), 6 + r, c * LD:(c + 1) * LD],
                                              pT[64 * r:64 * r + 64, c, LW * w:LW * (w + 1)],
                                              V2[64 * r:64 * r + 64, w, c, :], start=True, stop=True, skip_group_check=True)
                        pvs.append(T.mark(m))
                    last["pv"] = pvs[1]
                    return pvs

                def divide(pvs):
                    for r in range(2):
                        V.after(pvs[r], last["rs"], *used("O read"))
                        last[f"bank {6 + r} read"] = last["O"] = last["rs read"] = V.mark(ve.tensor_tensor(
                            O[:, :, r, :], PS[:, 6 + r, :].rearrange("p (c d) -> p c d", d=LD),
                            over(rs[:, r, :], 2, [P, 8, LD]), ALU.mult))

                def output_turn():
                    T.after(last["O"])
                    for b in range(2):
                        m = last["O read"] = to_bank(4 + b, [O[:, c, :, :].rearrange("p r d -> p (r d)") for c in range(4 * b, 4 * b + 4)])
                        A.after(m, *used("oT read"))
                        last["oT"] = last[f"bank {4 + b} read"] = A.mark(
                            ac.copy(oT[:, 4 * b:4 * b + 4, :].rearrange("p c q -> p (c q)"), PS[:, 4 + b, :]))

                def output_add(i):
                    T.after(last["oT"])
                    for c in range(8):
                        m = te.matmul(PS[:, 5, 0:D], oT[:, c, :], wo[:, c, :], start=(c == 0), stop=(c == 7))
                    last["oT read"] = m = T.mark(m)
                    V.after(m)
                    yi = Y[:, i, :]
                    last["bank 5 read"] = V.mark(ve.tensor_tensor(yi, PS[:, 5, 0:D], yi, ALU.add))

                def step(i):
                    attends, outputs = 0 <= i < NT, 0 < i <= NT
                    turns, projects = 0 <= i + 1 < NT, i + 2 < NT
                    if attends:
                        scores(i, 0)
                    if outputs:
                        output_turn()
                    if attends:
                        scores(i, 1)
                    if turns:
                        project_cosine(i + 1, 1)
                        project_sum(1)
                        keep_halo(i + 1)
                    if projects:
                        project_qk(i + 2, 0)
                    if outputs:
                        output_add(i - 1)
                    if projects:
                        project_qk(i + 2, 1)
                    if turns:
                        turn(0, 0)
                        turn(0, 1)
                    if attends:
                        sums()
                        weights_turn(0)
                        weights_turn(1)
                    if turns:
                        turn(1, 0)
                        turn(1, 1)
                    if projects:
                        project_norms()
                        project_norm(0)
                        project_sine(i + 2, 0)
                        project_norm(1)
                        project_cosine(i + 2, 0)
                        project_sum(0)
                        project_sine(i + 2, 1)
                    if attends:
                        divide(values())
                    if turns:
                        spread_v(i + 1)
                    if projects:
                        project_v(i + 2)

                def attention():
                    for i in range(-2, NT + 1):
                        step(i)
                    for lane in (HALO, VDMA):
                        sp.wait_ge(lane.sem, lane.count)

                def feed_forward():
                    shifted = shifted_transpose()
                    cols = [slice(g * 512, (g + 1) * 512) for g in range(NG)]
                    marks = []
                    for g in range(NG):
                        T.after(shifted[min(g + 1, NG - 1)])
                        marks.append(T.mark(te.matmul(PS[:, g, :], mean_mat[:, :], XST[:, cols[g]], start=True, stop=True)))
                    for g in range(NG):
                        V.after(marks[g])
                        m = V.mark(ve.tensor_tensor(xc[:, cols[g]], XST[:, cols[g]], PS[:, g, :], ALU.subtract))
                        A.after(m)
                        marks[g] = A.mark(ac.activation(xsq[:, g, :], xc[:, cols[g]], ACT.Square))
                    for g in range(NG):
                        T.after(marks[g])
                        for j in range(4):
                            m = T.mark(te.matmul(PS[:, g, j:j + 1], xsq[:, g, j * P:(j + 1) * P], mean_mat[:, 0:1],
                                                 start=True, stop=True))
                        V.after(m)
                        m = V.mark(ve.tensor_scalar(vrt[:, g, :], PS[:, g, 0:4], EPS, None, ALU.add))
                        G.after(m)
                        marks[g] = inverse_root(vrt[:, g, :], 4)
                    for g in range(NG):
                        V.after(marks[g])
                        for j in range(4):
                            m = V.mark(ve.tensor_scalar(rst[:, g, j * P:(j + 1) * P], ident[:, :], vrt[:, g, j:j + 1], None, ALU.mult))
                        T.after(m)
                        marks[g] = T.mark(te.matmul(PS[:, 4 + g, :], ones_mat[:, :], rst[:, g, :], start=True, stop=True))
                    for g in range(NG):
                        V.after(marks[g])
                        m = V.mark(ve.tensor_tensor(xc[:, cols[g]], xc[:, cols[g]], PS[:, 4 + g, :], ALU.mult))
                        A.after(m)
                        A.mark(ac.activation(xc[:, cols[g]], xc[:, cols[g]], ACT.Identity, scale=lng[:, 0:1], bias=lnb[:, 0:1]))
                    ac.preload_act_table(ACT.Gelu)
                    fence()
                    with nc.Fori(0, NG // 2) as g2:
                        up = {}
                        read = {}
                        hs = {}

                        def ups(u, c):
                            n, pair = HCH[c], (3 * u + c) % 3
                            xn = xc[:, bass.ds(g2 * 1024 + u * 512, 512)]
                            T.after(*([read[u - 1, c]] if u else []))
                            te.matmul(PS[0:n, 2 * pair, :], w1[:, HID + c * P:HID + c * P + n], xn, start=True, stop=True)
                            up[u, c] = T.mark(te.matmul(PS[0:n, 2 * pair + 1, :], w1[:, c * P:c * P + n], xn, start=True, stop=True))
                            A.after(up[u, c])
                            if (u, c) > (0, 1):
                                A.after(hs[(u, c - 2) if c == 2 else (u - 1, c + 1)])
                            slot = (3 * u + c) % 2
                            m = A.mark(ac.activation(gl[0:n, slot, :], PS[0:n, 2 * pair, :], ACT.Gelu, bias=b1[0:n, 1, c:c + 1]))
                            V.after(m)
                            hs[u, c] = read[u, c] = V.mark(ve.scalar_tensor_tensor(
                                hT[0:n, u, c, :], PS[0:n, 2 * pair + 1, :], b1[0:n, 0, c:c + 1], gl[0:n, slot, :], ALU.add, ALU.mult))

                        def down(u):
                            T.after(hs[u, 2])
                            for j in range(4):
                                for c, n in enumerate((P, P, HCH[2] + 1)):
                                    m = te.matmul(PS[:, 6 + u, j * D:(j + 1) * D], hT[0:n, u, c, j * P:(j + 1) * P], w2[0:n, c, :],
                                                  start=(c == 0), stop=(c == 2))
                            m = T.mark(m)
                            V.after(m)
                            yg = Y[:, bass.ds(8 * g2 + 4 * u, 4), :]
                            V.mark(ve.tensor_tensor(yg, PS[:, 6 + u, :].rearrange("p (j d) -> p j d", j=4), yg, ALU.add))

                        for c in range(3):
                            ups(0, c)
                        ups(1, 0)
                        ups(1, 1)
                        down(0)
                        ups(1, 2)
                        down(1)
                        fence()

                norm_loop(X, lambda g, m, turned: None, keep=Y, keep_t=False)
                with nc.Fori(0, DEPTH) as l:
                    half = LD // 2
                    for r, scale in ((0, qs), (2, ks)):
                        for b in range(B):
                            V.mark(ve.tensor_tensor(rot[:, r, b * TB:(b + 1) * TB, :], base[:, r, :, :],
                                                    over(scale[:, :], 1, [P, TB, LD]), ALU.mult))
                            for k in range(2):
                                lo, hi = k * half, (1 - k) * half
                                G.mark(gp.tensor_tensor(rot[:, r + 1, b * TB:(b + 1) * TB, lo:lo + half],
                                                        base[:, r + 1, :, lo:lo + half],
                                                        over(scale[:, hi:hi + half], 1, [P, TB, half]), ALU.mult))
                    shifted_transpose()
                    load_ffn(l)
                    sp.wait_ge(LOAD.sem, LOAD.count)
                    fence()
                    attention()
                    fence()
                    last.clear()
                    load_attention(l + 1)
                    sp.wait_ge(LOAD.sem, LOAD.count)
                    feed_forward()
                V.mark(ve.tensor_tensor(X[:, :, :], X[:, :, :], Y[:, :, :], ALU.add))
                fence()

        window_attention()
        mixture("f_")
        causal_attention()
        mixture("g_")
        cope_attention()
        local_stack("l_")
        linear_attention()
        local_stack("m_")
        done = LOAD.mark(sp.dma_start(out.rearrange("b (i p) d -> p (b i) d", p=P), X[:, :, :]))
        sp.wait_ge(LOAD.sem, LOAD.count)


def tables():
    f = np.float32
    c = {"ident": np.eye(P, dtype=f), "mean_mat": np.full((P, P), 1.0 / D, f)}
    c["a_headmask"] = (np.arange(P)[:, None] // A_DH == np.arange(A_H)[None, :]).astype(f)
    c["a_pad"] = np.tile(np.where(np.arange(NT) % TB == 0, NEG, 0.0).astype(f), (P, 1))
    c["f_lower"] = (np.arange(E_N)[None, :] < np.arange(E_N)[:, None]).astype(f).reshape(-1)
    ahead = np.arange(2 * L - P)[None, :] - (L - P) - np.arange(P)[:, None]
    c["b_future"] = np.where(ahead > 0, NEG, 0.0).astype(f)
    half = np.arange(0, LD, 2, dtype=f)
    freqs = np.arange(L, dtype=f)[:, None] * (f(1) / f(10000) ** (half / f(LD)))[None, :]
    freqs = np.concatenate([freqs, freqs], -1)
    power = (np.arange(L, dtype=f) - L // 2) / f(LW // 2)
    scale = ((half + f(0.4 * LD)) / f(1.4 * LD))[None, :] ** power[:, None]
    scale = np.concatenate([scale, scale], -1)
    cos, sin = np.cos(freqs), np.sin(freqs)
    sin = np.concatenate([-sin[:, :LD // 2], sin[:, LD // 2:]], -1)
    c["l_rot"] = np.stack([8 * cos * scale, 8 * sin * scale, cos / scale, sin / scale]).astype(f)
    a, k = np.arange(P)[:, None] % LW, np.arange(2 * LW)[None, :]
    allowed = (a <= k) & (k <= a + LW)
    first = allowed & ((np.arange(P)[:, None] >= LW) | (k >= LW))
    m = np.stack([first if i % TB == 0 else allowed for i in range(NT)], 1)
    bf16 = mybir.dt.np(BF16)
    c["l_mask"] = np.where(m, 0.0, NEG).astype(bf16)
    c["ident_b"] = np.eye(P, dtype=bf16)
    c["l_keep"] = np.tile((np.arange(NT) % TB != 0).astype(f), (P, 1))
    return c


def kernel(**inputs):
    from concourse import bacc
    from concourse.bass_utils import run_bass_kernel_spmd

    a = {k: np.asarray(v) for k, v in inputs.items()}
    arrays = {"x": a["L0_attn_a_x"]}
    for n in "qkvo":
        arrays[f"a_w{n}T"] = a[f"L0_attn_a_W{n}"].T
        arrays[f"a_b{n}"] = a[f"L0_attn_a_b{n}"]
        arrays[f"c_w{n}"] = a[f"L1_attn_a_W{n}"]
        arrays[f"c_b{n}"] = a[f"L1_attn_a_b{n}"]
        for part in "ASb":
            arrays[f"d_{n}{part}"] = a[f"L1_attn_b_{n}{part}"]
    arrays["b_wqk"], arrays["b_wov"] = a["L0_attn_b_wqk"], a["L0_attn_b_wov"]
    arrays["f_gateT"] = a["L0_ffn_gate_w"].T
    for n in "123":
        arrays[f"f_w{n}T"] = a[f"L0_ffn_w{n}"].transpose(0, 2, 1)
        arrays[f"f_b{n}"] = a[f"L0_ffn_b{n}"]
    arrays["f_sw12T"] = np.concatenate([a["L0_ffn_sw1"].T, a["L0_ffn_sw2"].T], 1)
    arrays["f_sw3T"] = a["L0_ffn_sw3"].T
    arrays["c_pos"] = a["L1_attn_a_pos_emb"]
    for n in ("g1", "b1", "g2", "b2"):
        arrays[f"d_{n}"] = a[f"L1_attn_b_{n}"]
    for n, src in (("wqkv", "Wqkv"), ("wo", "Wo"), ("qs", "q_scale"), ("ks", "k_scale")):
        w = a[f"L1_ffn_{src}"]
        arrays[f"l_{n}"] = np.concatenate([w, w[:1]])
    for n, src in (("w1", "W1"), ("b1", "b1"), ("w2", "W2"), ("b2", "b2"), ("g", "ln_g"), ("b", "ln_b")):
        arrays[f"l_{n}"] = a[f"L1_ffn_{src}"]
    arrays.update(tables())

    nc = bacc.Bacc("TRN2", target_bir_lowering=False, num_devices=1)
    arrays = {k + "_dram": np.ascontiguousarray(v) for k, v in arrays.items()}
    t = {k[:-5]: nc.dram_tensor(k, v.shape, mybir.dt.from_np(v.dtype), kind="ExternalInput").ap() for k, v in arrays.items()}
    out = nc.dram_tensor("out_dram", (B, L, D), F32, kind="ExternalOutput").ap()
    build(nc, t, out)
    r = run_bass_kernel_spmd(nc, [arrays], core_ids=[0])
    return r.results[0]["out_dram"]
```

```python
from contextlib import ExitStack

import numpy as np

import concourse.bass as bass
from concourse import mybir

F32 = mybir.dt.float32
BF16 = mybir.dt.bfloat16
ALU = mybir.AluOpType
ACT = mybir.ActivationFunctionType
AX = mybir.AxisListType.X

P = 128
B, L, D = 2, 1024, 128
NT = B * L // P
TB = L // P
NG = NT // 4
EPS = 1e-5
NEG = -3.0e38

A_WIN, A_H, A_DH = 64, 16, 8
E_N, I_SH = 8, 256
H, DH = 16, 8
DEPTH, LH, LD, LW = 6, 16, 64, 32
INNER = LH * LD
HID = int(D * 4 * 2 / 3)
HCH = [128, 128, HID - 256]


class Lane:

    def __init__(self, engine, sem, step=1):
        self.engine, self.sem, self.step = engine, sem, step
        self.reset()

    def reset(self):
        self.count = 0
        self.seen = {}

    def after(self, *marks):
        for lane, value in marks:
            if self.seen.get(lane.sem.num, 0) < value:
                self.engine.wait_ge(lane.sem, value)
                self.seen[lane.sem.num] = value

    def mark(self, instruction):
        self.count += self.step
        instruction.then_inc(self.sem, self.step)
        return self, self.count


def over(ap, axis, shape):
    return ap.unsqueeze(axis).to_broadcast(shape)


def build(nc, t, out):
    ctx = ExitStack()
    with ctx:
        def sb(name, *shape):
            return ctx.enter_context(nc.sbuf_tensor(name, list(shape), F32))

        names = ["pe_done", "dve_done", "act_done", "pool_done", "load_done", "v_done", "halo_done", "weights_done", "shift_done"]
        sems = [ctx.enter_context(nc.semaphore(n)) for n in names]
        assert [s.num for s in sems] == list(range(sems[0].num, sems[0].num + len(sems)))
        T = Lane(nc.tensor, sems[0])
        V = Lane(nc.vector, sems[1])
        A = Lane(nc.scalar, sems[2])
        G = Lane(nc.gpsimd, sems[3])
        LOAD = Lane(nc.sync, sems[4], 16)
        VDMA = Lane(nc.sync, sems[5], 16)
        HALO = Lane(nc.sync, sems[6], 16)
        WLOAD = Lane(nc.sync, sems[7], 16)
        SHIFT = Lane(nc.sync, sems[8], 16)
        lanes = [T, V, A, G, LOAD, VDMA, HALO, WLOAD, SHIFT]
        te, ve, ac, gp, sp = nc.tensor, nc.vector, nc.scalar, nc.gpsimd, nc.sync

        last = {}

        def used(*names):
            return [last[n] for n in names if n in last]

        def fence():
            nc.all_engine_barrier(sems_to_clear=range(sems[0].num, sems[-1].num + 1))
            for lane in lanes:
                lane.reset()
            last.clear()

        PS = ctx.enter_context(nc.psum_tensor("PS", [P, 8, 512], F32))

        def flat(a, b):
            return PS[:, a:b, :].rearrange("p a b -> p (a b)")

        X = sb("X", P, NT, D)
        ident = sb("ident", P, P)
        XNT = sb("XNT", P, A_WIN + NT * P)
        XN = sb("XN", P, NT, D)
        xn4 = sb("xn4", P, 2, 4, D)
        xT4 = sb("xT4", P, 2, 4 * P)
        stats = sb("stats", P, 2, 4, 6)
        meanvar = sb("meanvar", P, 2, 4, 2)
        rstd = sb("rstd", P, 2, 4)
        minus_half = sb("minus_half", P, 2 * H)

        def load(dst, src):
            return LOAD.mark(sp.dma_start(dst, src))

        def row(name, n):
            return t[name].rearrange("(a n) -> a n", a=1).to_broadcast([P, n])

        def column(name):
            return t[name].rearrange("(n a) -> n a", a=1)

        load(X[:, :, :], t["x"].rearrange("b (i p) d -> p (b i) d", p=P))
        load(ident[:, :], t["ident"])
        G.mark(gp.memset(minus_half[:, :], -0.5))
        G.after(G.mark(gp.memset(XNT[:, 0:A_WIN], 0.0)))
        sp.wait_ge(LOAD.sem, LOAD.count)
        fence()

        def inverse_root(ap, n):
            return G.mark(gp.tensor_tensor(ap, ap, minus_half[:, 0:n], ALU.pow))

        def turn4(src, dst, par, *before):
            T.after(*before, *used(f"bank {7 * par} read"))
            for j in range(4):
                m = te.transpose(PS[:, 7 * par, j * P:(j + 1) * P], src[:, j, :], ident[:, :])
            m = last[f"xn{par} turned"] = T.mark(m)
            A.after(m, *used(f"xT{par} read"))
            last[f"bank {7 * par} read"] = A.mark(ac.copy(dst, PS[:, 7 * par, :]))
            return last[f"bank {7 * par} read"]

        def norm_groups(src, hook, gain=None, shift=None, keep=None, keep_t=False):
            def statistics(g):
                par = g % 2
                V.after(*used(f"xn{par}"))
                for j in range(4):
                    m = V.mark(ve.bn_stats(stats[:, par, j, :], src[:, 4 * g + j, :]))
                V.after(m)
                for j in range(4):
                    m = V.mark(ve.bn_aggr(meanvar[:, par, j, :], stats[:, par, j, :]))
                V.after(m)
                G.after(V.mark(ve.tensor_scalar(rstd[:, par, :], meanvar[:, par, :, 1], EPS, None, ALU.add)))
                last[f"rstd{par}"] = inverse_root(rstd[:, par, :], 4)

            statistics(0)
            for g in range(NG):
                par = g % 2
                if g < NG - 1:
                    statistics(g + 1)
                xn = xn4[:, par, :, :] if keep is None else keep[:, 4 * g:4 * g + 4, :]
                xT = XNT[:, A_WIN + 512 * g:A_WIN + 512 * (g + 1)] if keep_t else xT4[:, par, :]
                V.after(last[f"rstd{par}"], *used(f"xn{par} turned", f"xn{par} read"))
                for j in range(4):
                    m = V.mark(ve.tensor_scalar(xn[:, j, :], src[:, 4 * g + j, :],
                                                meanvar[:, par, j, 0:1], rstd[:, par, j:j + 1], ALU.subtract, ALU.mult))
                if gain is not None:
                    V.after(m)
                    m = V.mark(ve.tensor_tensor(xn, xn, over(gain[:, :], 1, [P, 4, D]), ALU.mult))
                    V.after(m)
                    m = V.mark(ve.tensor_tensor(xn, xn, over(shift[:, :], 1, [P, 4, D]), ALU.add))
                last[f"xn{par}"] = m
                turned = turn4(xn, xT, par, m) if hook or keep_t else None
                if hook:
                    hook(g, xn, m, xT, turned)
            fence()

        def project_groups(src, w, bias):
            for g in range(NG):
                par = g % 2
                xg = X[:, 4 * g:4 * g + 4, :]
                b = G.mark(gp.tensor_tensor(xg, xg, over(bias, 1, [P, 4, D]), ALU.add))
                T.after(turn4(src[:, 4 * g:4 * g + 4, :], xT4[:, par, :], par), *used(f"bank {1 + par} read"))
                for j in range(4):
                    m = te.matmul(PS[:, 1 + par, j * P:(j + 1) * P], xT4[:, par, j * P:(j + 1) * P], w, start=True, stop=True)
                last[f"xT{par} read"] = m = T.mark(m)
                V.after(m, b)
                last[f"bank {1 + par} read"] = V.mark(ve.tensor_tensor(xg, PS[:, 1 + par, :].rearrange("p (j d) -> p j d", j=4), xg, ALU.add))
            fence()

        def window_attention():
            with ExitStack() as own:
                def sl(name, *shape):
                    return own.enter_context(nc.sbuf_tensor("a_" + name, list(shape), F32))
                wq, wk, wv, wo = (sl(n, P, D) for n in ("wq", "wk", "wv", "wo"))
                bq, bk = sl("bq", P, 1), sl("bk", P, 1)
                bv, bo = sl("bv", P, D), sl("bo", P, D)
                headmask = sl("headmask", P, A_H)
                xw = sl("xw", P, TB, A_WIN + P)
                qT = sl("qT", P, 2, P)
                kT = sl("kT", P, A_WIN + P)
                kTm = sl("kTm", P, 2, A_H, A_WIN + P)
                vc = sl("vc", P, 3, 2, D)
                S = sl("S", P, 2, A_H, P)
                pT = sl("pT", P, A_H, P)
                mx, sm, rs = sl("mx", P, A_H), sl("sm", P, A_H), sl("rs", P, A_H)
                o, oT = sl("o", P, D), sl("oT", P, P)
                for w, n in ((wq, "a_wqT"), (wk, "a_wkT"), (wv, "a_wvT"), (wo, "a_woT"),
                             (headmask, "a_headmask")):
                    load(w[:, :], t[n])
                load(bq[:, :], column("a_bq"))
                load(bk[:, :], column("a_bk"))
                load(bv[:, :], row("a_bv", D))
                load(bo[:, :], row("a_bo", D))
                sp.wait_ge(LOAD.sem, LOAD.count)
                fence()
                norm_groups(X, None, keep_t=True)
                with nc.Fori(0, B) as batch:
                    def project(i):
                        par, W_K = i % 2, A_WIN + P
                        T.after(last[f"xw{i}"], *used("bank 0 read", "bank 1 read"))
                        te.matmul(PS[:, 0, 0:P], wq[:, :], xw[:, i, A_WIN:], start=True, stop=True)
                        m = T.mark(te.matmul(PS[:, 0, P:2 * P + A_WIN], wk[:, :], xw[:, i, :], start=True, stop=True))
                        for c in range(2):
                            v = te.matmul(PS[:, 1, c * P:(c + 1) * P], xw[:, i, A_WIN * c:A_WIN * c + P], wv[:, :],
                                          start=True, stop=True)
                        v = T.mark(v)
                        A.after(m, *used("kT read by DVE", "kT read by GpSimd"))
                        k = A.mark(ac.activation(kT[:, :], PS[:, 0, P:2 * P + A_WIN], ACT.Identity, bias=bk[:, 0:1]))
                        A.after(*used(f"scores{par}"))
                        last[f"q{par}"] = last["bank 0 read"] = A.mark(ac.activation(qT[:, par, :], PS[:, 0, 0:P], ACT.Identity, bias=bq[:, 0:1]))
                        V.after(k, *used(f"scores{par}"))
                        last["kT read by DVE"] = last[f"km{par}"] = V.mark(ve.tensor_tensor(
                            kTm[:, par, 0:10, :], over(kT[:, :], 1, [P, 10, W_K]), over(headmask[:, 0:10], 2, [P, 10, W_K]), ALU.mult))
                        G.after(k, *used(f"scores{par}"))
                        last["kT read by GpSimd"] = last[f"km2{par}"] = G.mark(gp.tensor_tensor(
                            kTm[:, par, 10:, :], over(kT[:, :], 1, [P, A_H - 10, W_K]), over(headmask[:, 10:], 2, [P, A_H - 10, W_K]), ALU.mult))
                        V.after(v, *used(f"pv{i % 3}"))
                        last[f"v{i % 3}"] = last["bank 1 read"] = V.mark(ve.tensor_tensor(
                            vc[:, i % 3, :, :], PS[:, 1, 0:2 * D].rearrange("p (c d) -> p c d", c=2), over(bv[:, :], 1, [P, 2, D]), ALU.add))

                    def scores(i, n):
                        par = i % 2
                        T.after(last[f"q{par}"], last[f"km{par}"], *([last[f"km2{par}"]] if n > 1 else []), *used(f"bank {4 + n} read"))
                        for c in range(2):
                            m = te.matmul(PS[A_WIN * c:A_WIN * (c + 1), 4 + n, :], qT[:, par, A_WIN * c:A_WIN * (c + 1)],
                                          kTm[:, par, 4 * n:4 * n + 4, A_WIN * c:A_WIN * c + P], start=True, stop=True)
                        last[f"scores{par}"] = T.mark(m)
                        bank = PS[:, 4 + n, :].rearrange("p (h k) -> p h k", k=P)
                        V.after(last[f"scores{par}"], *used(f"mx{n} read"))
                        if i == 0:
                            V.after(V.mark(ve.tensor_scalar(bank[0:A_WIN, :, 0:A_WIN], bank[0:A_WIN, :, 0:A_WIN], NEG, None, ALU.add)))
                        V.after(V.mark(ve.tensor_reduce(mx[:, 4 * n:4 * n + 4], bank, AX, ALU.max)))
                        sh = S[:, par, 4 * n:4 * n + 4, :]
                        V.after(*used(f"S{par} turned", f"S{par} summed"))
                        last[f"mx{n} read"] = last[f"bank {4 + n} read"] = m = V.mark(ve.tensor_tensor(
                            sh, bank, over(mx[:, 4 * n:4 * n + 4], 2, [P, 4, P]), ALU.subtract))
                        A.after(m)
                        last[f"exp{par}{n}"] = A.mark(ac.activation(sh, sh, ACT.Exp, scale=float(A_DH) ** -0.5))

                    def turn(i, n):
                        par, bank = i % 2, 2 + n % 2
                        T.after(last[f"exp{par}{n}"], *used(f"bank {bank} read"))
                        for h in range(4):
                            m = te.transpose(PS[:, bank, h * P:(h + 1) * P], S[:, par, 4 * n + h, :], ident[:, :])
                        m = last[f"turned{par}"] = T.mark(m)
                        A.after(m, *used("pT read"))
                        last[f"pT{n}"] = last[f"bank {bank} read"] = A.mark(
                            ac.copy(pT[:, 4 * n:4 * n + 4, :].rearrange("p a b -> p (a b)"), PS[:, bank, :]))

                    def sums(i):
                        par = i % 2
                        V.after(*[last[f"exp{par}{n}"] for n in range(4)])
                        m = last[f"S{par} summed"] = V.mark(ve.tensor_reduce(sm[:, :], S[:, par, :, :], AX, ALU.add))
                        V.after(m, *used("rs read"))
                        last["rs"] = V.mark(ve.reciprocal(rs[:, :], sm[:, :]))

                    def values(i):
                        par = i % 2
                        last[f"S{par} turned"] = last[f"turned{par}"]
                        T.after(last[f"v{i % 3}"], *[last[f"pT{n}"] for n in range(4)])
                        for h in range(A_H):
                            for c in range(2):
                                m = te.matmul(PS[A_WIN * c:A_WIN * (c + 1), 2, h * A_DH:(h + 1) * A_DH],
                                              pT[:, h, A_WIN * c:A_WIN * (c + 1)], vc[:, i % 3, c, h * A_DH:(h + 1) * A_DH],
                                              start=True, stop=True)
                        m = last["pT read"] = last[f"pv{i % 3}"] = T.mark(m)
                        V.after(m, last["rs"], *used("o turned"))
                        last["o"] = last["rs read"] = last["bank 2 read"] = V.mark(ve.tensor_tensor(
                            o[:, :].rearrange("p (h d) -> p h d", h=A_H), PS[:, 2, 0:D].rearrange("p (h d) -> p h d", h=A_H),
                            over(rs[:, :], 2, [P, A_H, A_DH]), ALU.mult))

                    def output(i):
                        T.after(last["o"])
                        m = last["o turned"] = T.mark(te.transpose(PS[:, 3, 0:P], o[:, :], ident[:, :]))
                        A.after(m)
                        T.after(A.mark(ac.copy(oT[:, :], PS[:, 3, 0:P])))
                        m = T.mark(te.matmul(PS[:, 3, P:P + D], oT[:, :], wo[:, :], start=True, stop=True))
                        V.after(m, last["bias"])
                        xi = X[:, bass.ds(batch * TB + i, 1), :].rearrange("p a d -> p (a d)")
                        last["bank 3 read"] = V.mark(ve.tensor_tensor(xi, PS[:, 3, P:P + D], xi, ALU.add))

                    for i in range(TB):
                        last[f"xw{i}"] = G.mark(gp.tensor_copy(xw[:, i, :], XNT[:, bass.ds(batch * L + i * P, A_WIN + P)]))
                        if i == 0:
                            project(0)
                    xb = X[:, bass.ds(batch * TB, TB), :]
                    last["bias"] = G.mark(gp.tensor_tensor(xb, xb, over(bo[:, :], 1, [P, TB, D]), ALU.add))
                    for i in range(TB + 1):
                        if i:
                            sums(i - 1)
                        for n in range(4):
                            if i < TB:
                                scores(i, n)
                            if i:
                                turn(i - 1, n)
                        if i + 1 < TB:
                            project(i + 1)
                        if i:
                            values(i - 1)
                            output(i - 1)
                    fence()

        def mixture(tag):
            with ExitStack() as own:
                def sl(name, *shape):
                    return own.enter_context(nc.sbuf_tensor(tag + name, list(shape), F32))
                gate = sl("gate", P, E_N)
                w13 = sl("w13", P, E_N, 2, D)
                w2 = sl("w2", P, E_N, D)
                b1, b2, b3 = (sl(n, P, E_N, D) for n in ("b1", "b2", "b3"))
                sw12 = sl("sw12", P, 2 * I_SH)
                sw3 = sl("sw3", P, 2, D)
                lower = sl("lower", P, E_N, E_N)
                sc = sl("sc", P, NT, E_N)
                mask = sl("mask", P, NT, E_N)
                r1 = sl("r1", P, NT)
                gt, eq = sl("gt", P, NT, E_N * E_N), sl("eq", P, NT, E_N * E_N)
                xt = sl("xt", P, TB, P)
                hin, x3 = sl("hin", P, 2, E_N, D), sl("x3", P, 2, E_N, D)
                hT, y8 = sl("hT", P, E_N, D), sl("y8", P, E_N, D)
                sg, sT, y1 = sl("sg", P, I_SH), sl("sT", P, I_SH), sl("y1", P, D)
                load(gate[:, :], t["f_gateT"])
                load(w13[:, :, 0, :], t["f_w1T"].rearrange("e d h -> d e h"))
                load(w13[:, :, 1, :], t["f_w3T"].rearrange("e d h -> d e h"))
                load(w2[:, :, :], t["f_w2T"].rearrange("e h d -> h e d"))
                for b, n in ((b1, "f_b1"), (b2, "f_b2"), (b3, "f_b3")):
                    load(b[:, :, :].rearrange("p e d -> p (e d)"),
                         t[n].rearrange("e d -> (e d)").rearrange("(a n) -> a n", a=1).to_broadcast([P, E_N * D]))
                load(sw12[:, :], t["f_sw12T"])
                load(sw3[:, :, :], t["f_sw3T"].rearrange("(c p) d -> p c d", p=P))
                load(lower[:, :, :].rearrange("p a b -> p (a b)"), row("f_lower", E_N * E_N))
                sp.wait_ge(LOAD.sem, LOAD.count)
                fence()

                def gates(g, xn, m, xT, turned):
                    par = g % 2
                    T.after(turned, *used(f"bank {1 + par} read"))
                    for j in range(4):
                        m = te.matmul(PS[:, 1 + par, j * E_N:(j + 1) * E_N], xT[:, j * P:(j + 1) * P], gate[:, :],
                                      start=True, stop=True)
                    m = last[f"xT{par} read"] = T.mark(m)
                    V.after(m)
                    last[f"bank {1 + par} read"] = V.mark(ve.tensor_copy(
                        sc[:, 4 * g:4 * g + 4, :], PS[:, 1 + par, 0:4 * E_N].rearrange("p (j e) -> p j e", j=4)))

                norm_groups(X, gates, keep_t=True)
                all3 = [P, NT, E_N]
                V.after(V.mark(ve.tensor_reduce(r1[:, :], sc[:, :, :], AX, ALU.max)))
                m = V.mark(ve.tensor_tensor(sc[:, :, :], sc[:, :, :], over(r1[:, :], 2, all3), ALU.subtract))
                A.after(m)
                m = A.mark(ac.activation(sc[:, :, :], sc[:, :, :], ACT.Exp))
                V.after(m)
                V.after(V.mark(ve.tensor_reduce(r1[:, :], sc[:, :, :], AX, ALU.add)))
                V.after(V.mark(ve.reciprocal(r1[:, :], r1[:, :])))
                V.after(V.mark(ve.tensor_tensor(sc[:, :, :], sc[:, :, :], over(r1[:, :], 2, all3), ALU.mult)))
                four = [P, NT, E_N, E_N]
                gt4 = gt[:, :, :].rearrange("p t (a b) -> p t a b", a=E_N)
                eq4 = eq[:, :, :].rearrange("p t (a b) -> p t a b", a=E_N)
                rival, own_s = over(sc[:, :, :], 2, four), over(sc[:, :, :], 3, four)
                V.mark(ve.tensor_tensor(gt4, rival, own_s, ALU.is_gt))
                V.after(V.mark(ve.tensor_tensor(eq4, rival, own_s, ALU.is_equal)))
                V.after(V.mark(ve.tensor_tensor(eq[:, :, :], eq[:, :, :],
                                                over(lower[:, :, :].rearrange("p a b -> p (a b)"), 1, [P, NT, E_N * E_N]),
                                                ALU.mult)))
                V.after(V.mark(ve.tensor_tensor(gt[:, :, :], gt[:, :, :], eq[:, :, :], ALU.add)))
                V.after(V.mark(ve.tensor_reduce(mask[:, :, :], gt4, AX, ALU.add)))
                V.mark(ve.tensor_scalar(mask[:, :, :], mask[:, :, :], 1.5, None, ALU.is_lt))
                fence()
                with nc.Fori(0, B) as batch:
                    def tile(i):
                        return bass.ds(batch * TB + i, 1)

                    def experts_up(i):
                        T.after(last[f"xt{i}"])
                        for n in range(4):
                            T.after(*used(f"bank {n} read"))
                            last[f"u{n}"] = T.mark(te.matmul(PS[:, n, :], xt[:, i, :],
                                                             w13[:, 2 * n:2 * n + 2, :, :].rearrange("p e k h -> p (e k h)"),
                                                             start=True, stop=True))
                        T.after(*used("bank 4 read"))
                        last["z12"] = T.mark(te.matmul(PS[:, 4, :], xt[:, i, :], sw12[:, :], start=True, stop=True))

                    def experts_gate(i):
                        par = i % 2
                        for e in range(E_N):
                            V.after(last[f"u{e // 2}"], *used(f"hin{par} turned", f"x3{par} read"))
                            s = sc[:, tile(i), e:e + 1].rearrange("p a e -> p (a e)")
                            m = V.mark(ve.scalar_tensor_tensor(hin[:, par, e, :], PS[:, e // 2, (e % 2) * 256:(e % 2) * 256 + D],
                                                               s, b1[:, e, :], ALU.mult, ALU.add))
                            x = V.mark(ve.scalar_tensor_tensor(x3[:, par, e, :], PS[:, e // 2, (e % 2) * 256 + D:(e % 2) * 256 + 2 * D],
                                                               s, b3[:, e, :], ALU.mult, ALU.add))
                            if e % 2:
                                last[f"bank {e // 2} read"] = x
                                A.after(m)
                                last[f"h{par}{e // 4}"] = A.mark(ac.activation(hin[:, par, e - 1:e + 1, :], hin[:, par, e - 1:e + 1, :], ACT.Silu))
                        A.after(last["z12"], *used("sg turned"))
                        m = A.mark(ac.activation(sg[:, :], PS[:, 4, 0:I_SH], ACT.Silu))
                        V.after(m)
                        last["sg"] = V.mark(ve.tensor_tensor(sg[:, :], sg[:, :], PS[:, 4, I_SH:], ALU.mult))
                        G.after(x)
                        last[f"x3{par}"] = G.mark(gp.tensor_tensor(x3[:, par, :, :], x3[:, par, :, :],
                                                                   over(mask[:, tile(i), :].rearrange("p a e -> p (a e)"), 2, [P, E_N, D]),
                                                                   ALU.mult))

                    def shared_down(i):
                        T.after(last["sg"])
                        for j in range(2):
                            m = te.transpose(PS[:, 4, j * P:(j + 1) * P], sg[:, j * P:(j + 1) * P], ident[:, :])
                        m = last["sg turned"] = T.mark(m)
                        A.after(m, *used("sT read"))
                        T.after(A.mark(ac.copy(sT[:, :], PS[:, 4, 0:I_SH])))
                        for j in range(2):
                            m = te.matmul(PS[:, 4, I_SH:I_SH + D], sT[:, j * P:(j + 1) * P], sw3[:, j, :], start=(j == 0), stop=(j == 1))
                        last["sT read"] = last["z"] = T.mark(m)

                    def experts_turn(i):
                        par = i % 2
                        for n in range(2):
                            T.after(last[f"h{par}{n}"], *used(f"bank {5 + n} read"))
                            for e in range(4 * n, 4 * n + 4):
                                m = te.transpose(PS[:, 5 + n, (e % 4) * P:(e % 4 + 1) * P], hin[:, par, e, :], ident[:, :])
                            m = last[f"hin{par} turned"] = T.mark(m)
                            A.after(m, *used("hT read"))
                            last[f"hT{n}"] = last[f"bank {5 + n} read"] = A.mark(
                                ac.copy(hT[:, 4 * n:4 * n + 4, :].rearrange("p a b -> p (a b)"), PS[:, 5 + n, :]))

                    def experts_down(i):
                        par = i % 2
                        for n, bank in ((0, 7), (1, 5)):
                            T.after(last[f"hT{n}"], *used(f"bank {bank} read"))
                            for e in range(4 * n, 4 * n + 4):
                                m = te.matmul(PS[:, bank, (e % 4) * D:(e % 4 + 1) * D], hT[:, e, :], w2[:, e, :],
                                              start=True, stop=True)
                            last[f"y{n}"] = T.mark(m)
                        last["hT read"] = last["y1"]
                        halves = [y8[:, 4 * n:4 * n + 4, :] for n in range(2)]
                        for n, bank in ((0, 7), (1, 5)):
                            V.after(last[f"y{n}"], *used("y8 read"))
                            last[f"bank {bank} read"] = m = V.mark(ve.tensor_tensor(
                                halves[n], PS[:, bank, :].rearrange("p (e d) -> p e d", e=4), b2[:, 4 * n:4 * n + 4, :], ALU.add))
                        V.after(last[f"x3{par}"], m)
                        m = last[f"x3{par} read"] = V.mark(ve.tensor_tensor(y8[:, :, :], y8[:, :, :], x3[:, par, :, :], ALU.mult))
                        V.after(m)
                        m = last["y8 read"] = V.mark(ve.tensor_reduce(y1[:, :], y8[:, :, :].rearrange("p e d -> p d e"), AX, ALU.add))
                        xi = X[:, tile(i), :].rearrange("p a d -> p (a d)")
                        V.after(m)
                        last["x"] = V.mark(ve.tensor_tensor(xi, xi, y1[:, :], ALU.add))

                    def shared_add(i):
                        xi = X[:, tile(i), :].rearrange("p a d -> p (a d)")
                        V.after(last["z"])
                        last["bank 4 read"] = V.mark(ve.tensor_tensor(xi, PS[:, 4, I_SH:I_SH + D], xi, ALU.add))

                    for i in range(TB):
                        last[f"xt{i}"] = G.mark(gp.tensor_copy(xt[:, i, :], XNT[:, bass.ds(batch * L + i * P + A_WIN, P)]))
                    for i in range(TB + 1):
                        if i:
                            experts_turn(i - 1)
                        if i < TB:
                            experts_up(i)
                            experts_gate(i)
                        if i:
                            experts_down(i - 1)
                        if i < TB:
                            shared_down(i)
                            V.after(*used("x"))
                            shared_add(i)
                    fence()

        def causal_attention():
            with ExitStack() as own:
                def sl(name, *shape):
                    return own.enter_context(nc.sbuf_tensor("b_" + name, list(shape), F32))
                wqk, wov = sl("wqk", P, D), sl("wov", P, D)
                future = sl("future", P, 2 * L - P)
                QT = sl("QT", P, NT * P)
                XV = sl("XV", P, NT, D)
                q, S, pT = sl("q", P, TB, P), sl("S", P, 2, L), sl("pT", P, L)
                mx, nmx, sm, rs = (sl(n, P, 2) for n in ("mx", "nmx", "sm", "rs"))
                for w, n in ((wqk, "b_wqk"), (wov, "b_wov"), (future, "b_future")):
                    load(w[:, :], t[n])
                sp.wait_ge(LOAD.sem, LOAD.count)
                fence()

                def products(g, xn, m, xT, turned):
                    par = g % 2
                    T.after(turned, *used(f"bank {1 + par} read", f"bank {3 + par} read"))
                    m = T.mark(te.matmul(PS[:, 1 + par, :], wqk[:, :], xT, start=True, stop=True))
                    V.after(m)
                    last[f"bank {1 + par} read"] = V.mark(ve.tensor_copy(QT[:, g * 512:(g + 1) * 512], PS[:, 1 + par, :]))
                    for j in range(4):
                        m = te.matmul(PS[:, 3 + par, j * D:(j + 1) * D], xT[:, j * P:(j + 1) * P], wov[:, :], start=True, stop=True)
                    m = last[f"xT{par} read"] = T.mark(m)
                    V.after(m)
                    last[f"bank {3 + par} read"] = V.mark(ve.tensor_copy(
                        XV[:, 4 * g:4 * g + 4, :], PS[:, 3 + par, :].rearrange("p (j d) -> p j d", j=4)))

                norm_groups(X, products, keep_t=True)
                with nc.Fori(0, B) as batch:
                    def scores(i):
                        par = i % 2
                        bank = 2 * par
                        T.after(last[f"q{i}"], *used(f"bank {bank} read"))
                        for n in range(2):
                            m = te.matmul(PS[:, bank + n, :], q[:, i, :], XNT[:, bass.ds(batch * L + A_WIN + n * 512, 512)],
                                          start=True, stop=True)
                        V.after(T.mark(m), *used(f"S{par} turned"))
                        m = last[f"bank {bank} read"] = V.mark(ve.tensor_tensor(
                            S[:, par, :], flat(bank, bank + 2), future[:, L - P - i * P:2 * L - P - i * P], ALU.add))
                        V.after(m)
                        V.after(V.mark(ve.tensor_reduce(mx[:, par:par + 1], S[:, par, :], AX, ALU.max)))
                        V.after(*used(f"exp{par}"))
                        m = V.mark(ve.tensor_scalar(nmx[:, par:par + 1], mx[:, par:par + 1], -1.0, None, ALU.mult))
                        A.after(m, *used(f"rs{par}"))
                        last[f"exp{par}"] = A.mark(ac.activation(S[:, par, :], S[:, par, :], ACT.Exp, bias=nmx[:, par:par + 1],
                                                                 accum_out=sm[:, par:par + 1]))

                    def values(i):
                        par = i % 2
                        V.after(last[f"exp{par}"])
                        last[f"rs{par}"] = V.mark(ve.reciprocal(rs[:, par:par + 1], sm[:, par:par + 1]))
                        for n in range(2):
                            T.after(last[f"exp{par}"], *used(f"bank {4 + n} read"))
                            for j in range(4):
                                c = 4 * n + j
                                m = te.transpose(PS[:, 4 + n, j * P:(j + 1) * P], S[:, par, c * P:(c + 1) * P], ident[:, :])
                            m = last[f"S{par} turned"] = T.mark(m)
                            A.after(m, *used(f"pT{n} read"))
                            last[f"pT{n}"] = last[f"bank {4 + n} read"] = A.mark(ac.copy(pT[:, n * 512:(n + 1) * 512], PS[:, 4 + n, :]))
                        for n in range(2):
                            T.after(last[f"pT{n}"], *used(f"bank {6 + par} read"))
                            for c in range(4 * n, 4 * n + 4):
                                m = te.matmul(PS[:, 6 + par, 0:D], pT[:, c * P:(c + 1) * P],
                                              XV[:, bass.ds(batch * TB + c, 1), :].rearrange("p a d -> p (a d)"),
                                              start=(c == 0), stop=(c == TB - 1))
                            m = last[f"pT{n} read"] = T.mark(m)
                        last["out"] = m

                    def add(i):
                        par = i % 2
                        V.after(last["out"], last[f"rs{par}"])
                        xi = X[:, bass.ds(batch * TB + i, 1), :].rearrange("p a d -> p (a d)")
                        last[f"bank {6 + par} read"] = V.mark(ve.scalar_tensor_tensor(
                            xi, PS[:, 6 + par, 0:D], rs[:, par:par + 1], xi, ALU.mult, ALU.add))

                    for i in range(TB):
                        last[f"q{i}"] = G.mark(gp.tensor_copy(q[:, i, :], QT[:, bass.ds(batch * L + i * P, P)]))
                    scores(0)
                    for i in range(TB):
                        if i + 1 < TB:
                            scores(i + 1)
                        values(i)
                        add(i)
                    fence()

        full = [P, TB, H, DH]

        def split(ap):
            return ap.rearrange("p i (h d) -> p i h d", h=H)

        def cope_attention():
            with ExitStack() as own:
                def sl(name, *shape):
                    return own.enter_context(nc.sbuf_tensor("c_" + name, list(shape), F32))
                w = sl("w", P, 3 * D)
                bqkv = sl("bqkv", P, 3 * D)
                wo, bo = sl("wo", P, D), sl("bo", P, D)
                pos_rows = sl("pos_rows", P, DH, 3)
                qkv = sl("qkv", P, NT, 3 * D)
                prod, prod2 = sl("prod", P, TB, D), sl("prod2", P, TB, D)
                dots = sl("dots", P, 2, 2, P)
                tab = sl("tab", P, 2, 3, P)
                gates = sl("gates", P, 2, 2, P)
                w1, w2 = sl("w1", P, 2, 2, P), sl("w2", P, 2, 2, P)
                d1, d2 = sl("d1", P, 2, P), sl("d2", P, 2, P)
                mx = sl("mx", P, 2, P)
                att = sl("att", P, NT, D)
                for n in range(3):
                    load(w[:, n * D:(n + 1) * D], t[("c_wq", "c_wk", "c_wv")[n]])
                    load(bqkv[:, n * D:(n + 1) * D], row(("c_bq", "c_bk", "c_bv")[n], D))
                load(wo[:, :], t["c_wo"])
                load(bo[:, :], row("c_bo", D))
                for d in range(DH):
                    load(pos_rows[:, d, :], t["c_pos"][0, d:d + 1, 0:3].to_broadcast([P, 3]))
                sp.wait_ge(LOAD.sem, LOAD.count)
                fence()

                def products(g, xn, m, xT, turned):
                    T.after(turned, *used("banks 1-4 read"))
                    for j in range(4):
                        m = te.matmul(PS[:, 1 + j, 0:3 * D], xT[:, j * P:(j + 1) * P], w[:, :], start=True, stop=True)
                    m = last[f"xT{g % 2} read"] = T.mark(m)
                    V.after(m)
                    last["banks 1-4 read"] = V.mark(ve.tensor_tensor(qkv[:, 4 * g:4 * g + 4, :], PS[:, 1:5, 0:3 * D],
                                                                     over(bqkv[:, :], 1, [P, 4, 3 * D]), ALU.add))

                norm_groups(X, products)

                def part(s, n):
                    return qkv[:, TB * s:TB * (s + 1), n * D:(n + 1) * D]

                for s in range(2):
                    for k in range(2):
                        V.after(V.mark(ve.tensor_tensor(prod[:, :, :], part(s, 0), part(k, 1), ALU.mult)))
                        V.after(V.mark(ve.tensor_reduce(dots[:, s, k, :].rearrange("p (i h) -> p i h", h=H), split(prod[:, :, :]), AX, ALU.add)))
                    for n in range(3):
                        pe = pos_rows[:, :, n].unsqueeze(1).unsqueeze(1).to_broadcast(full)
                        V.after(V.mark(ve.tensor_tensor(split(prod[:, :, :]), split(part(s, 0)), pe, ALU.mult)))
                        m = V.mark(ve.tensor_reduce(tab[:, s, n, :].rearrange("p (i h) -> p i h", h=H), split(prod[:, :, :]), AX, ALU.add))
                        V.after(m)
                scale = float(DH) ** -0.5
                A.after(m)
                m = A.mark(ac.activation(gates[:, :, :, :], dots[:, :, :, :], ACT.Tanh, scale=scale / 2))
                V.after(m)
                V.after(V.mark(ve.tensor_scalar(gates[:, :, :, :], gates[:, :, :, :], 0.5, 0.5, ALU.mult, ALU.add)))
                V.after(V.mark(ve.tensor_tensor(gates[:, :, 0, :], gates[:, :, 0, :], gates[:, :, 1, :], ALU.add)))
                V.after(V.mark(ve.tensor_scalar(gates[:, :, :, :], gates[:, :, :, :], 124.0, None, ALU.min)))
                V.mark(ve.tensor_scalar(w1[:, :, :, :], gates[:, :, :, :], 1.0, None, ALU.min))
                V.mark(ve.tensor_scalar(w2[:, :, :, :], gates[:, :, :, :], 1.0, 0.0, ALU.subtract, ALU.max))
                V.mark(ve.tensor_tensor(d1[:, :, :], tab[:, :, 1, :], tab[:, :, 0, :], ALU.subtract))
                V.after(V.mark(ve.tensor_tensor(d2[:, :, :], tab[:, :, 2, :], tab[:, :, 1, :], ALU.subtract)))
                two = [P, 2, 2, P]
                V.mark(ve.tensor_tensor(w1[:, :, :, :], w1[:, :, :, :], over(d1[:, :, :], 2, two), ALU.mult))
                V.after(V.mark(ve.tensor_tensor(w2[:, :, :, :], w2[:, :, :, :], over(d2[:, :, :], 2, two), ALU.mult)))
                V.after(V.mark(ve.tensor_tensor(w1[:, :, :, :], w1[:, :, :, :], w2[:, :, :, :], ALU.add)))
                V.after(V.mark(ve.tensor_tensor(w1[:, :, :, :], w1[:, :, :, :], over(tab[:, :, 0, :], 2, two), ALU.add)))
                V.after(V.mark(ve.scalar_tensor_tensor(dots[:, :, :, :].rearrange("p a b c -> p (a b c)"),
                                                       dots[:, :, :, :].rearrange("p a b c -> p (a b c)"), scale,
                                                       w1[:, :, :, :].rearrange("p a b c -> p (a b c)"), ALU.mult, ALU.add)))
                V.after(V.mark(ve.tensor_tensor(mx[:, :, :], dots[:, :, 0, :], dots[:, :, 1, :], ALU.max)))
                m = V.mark(ve.tensor_tensor(dots[:, :, :, :], dots[:, :, :, :], over(mx[:, :, :], 2, two), ALU.subtract))
                A.after(m)
                m = A.mark(ac.activation(dots[:, :, :, :], dots[:, :, :, :], ACT.Exp))
                V.after(m)
                V.after(V.mark(ve.tensor_tensor(mx[:, :, :], dots[:, :, 0, :], dots[:, :, 1, :], ALU.add)))
                V.after(V.mark(ve.reciprocal(mx[:, :, :], mx[:, :, :])))
                V.after(V.mark(ve.tensor_tensor(dots[:, :, :, :], dots[:, :, :, :], over(mx[:, :, :], 2, two), ALU.mult)))
                for s in range(2):
                    for k, to in ((0, prod), (1, prod2)):
                        a = over(dots[:, s, k, :].rearrange("p (i h) -> p i h", h=H), 3, full)
                        m = V.mark(ve.tensor_tensor(split(to[:, :, :]), split(part(k, 2)), a, ALU.mult))
                    V.after(m)
                    V.after(V.mark(ve.tensor_tensor(att[:, TB * s:TB * (s + 1), :], prod[:, :, :], prod2[:, :, :], ALU.add)))
                fence()
                project_groups(att, wo[:, :], bo[:, :])

        def linear_attention():
            f, S4 = 4, D // 4
            with ExitStack() as own:
                def sl(name, *shape):
                    return own.enter_context(nc.sbuf_tensor("d_" + name, list(shape), F32))
                ws = {n: sl("w" + n, P, D) for n in "qkvo"}
                bs = {n: sl("b" + n, P, D) for n in "qkvo"}
                fact = sl("fact", P, 4, f, f)
                blocks = sl("blocks", P, 4, f, S4)
                g1, b1, g2, b2 = (sl(n, P, D) for n in ("g1", "b1", "g2", "b2"))
                tmp = sl("tmp", P, D)
                q, kv = sl("q", P, NT, D), sl("kv", P, NT, 2 * D)
                QN = sl("QN", P, NT, D)
                prod, prod2 = sl("prod", P, TB, D), sl("prod2", P, TB, D)
                dots = sl("dots", P, 2, 2, P)
                den = sl("den", P, 2, P)
                att = sl("att", P, NT, D)
                for m4, n in enumerate("qkvo"):
                    for i in range(f):
                        lo = i * S4
                        load(blocks[lo:lo + S4, m4, :, :], t[f"d_{n}S"].rearrange("n k l -> k n l"))
                        load(fact[lo:lo + S4, m4, :, :], t[f"d_{n}A"][:, i:i + 1, :].rearrange("n i j -> i n j").to_broadcast([S4, f, f]))
                    load(bs[n][:, :], row(f"d_{n}b", D))
                for b, n in ((g1, "d_g1"), (b1, "d_b1"), (g2, "d_g2"), (b2, "d_b2")):
                    load(b[:, :], row(n, D))
                V.after((LOAD, LOAD.count))
                for m4, n in enumerate("qkvo"):
                    shape = [P, f, S4]
                    for k in range(f):
                        to = (ws[n] if k == 0 else tmp)[:, :].rearrange("p (j l) -> p j l", j=f)
                        m = V.mark(ve.tensor_tensor(to, over(fact[:, m4, k, :], 2, shape), over(blocks[:, m4, k, :], 1, shape), ALU.mult))
                        V.after(m)
                        if k:
                            V.after(V.mark(ve.tensor_tensor(ws[n][:, :], ws[n][:, :], tmp[:, :], ALU.add)))
                fence()

                def keys_values(g, xn, m, xT, turned):
                    T.after(turned, *used("banks 1-4 read"))
                    for j in range(4):
                        for c, n in enumerate("kv"):
                            m = te.matmul(PS[:, 1 + j, c * D:(c + 1) * D], xT[:, j * P:(j + 1) * P], ws[n][:, :],
                                          start=True, stop=True)
                    m = last[f"xT{g % 2} read"] = T.mark(m)
                    V.after(m)
                    for c, n in enumerate("kv"):
                        to = kv[:, 4 * g:4 * g + 4, c * D:(c + 1) * D]
                        m = V.mark(ve.tensor_tensor(to, PS[:, 1:5, c * D:(c + 1) * D], over(bs[n][:, :], 1, [P, 4, D]), ALU.add))
                        last["banks 1-4 read"] = m
                        if n == "k":
                            V.after(m)
                            V.mark(ve.tensor_scalar(to, to, 0.0, None, ALU.max))

                def queries(g, xn, m, xT, turned):
                    T.after(turned, *used("banks 1-4 read"))
                    for j in range(4):
                        m = te.matmul(PS[:, 1 + j, 0:D], xT[:, j * P:(j + 1) * P], ws["q"][:, :], start=True, stop=True)
                    m = last[f"xT{g % 2} read"] = T.mark(m)
                    V.after(m)
                    to = q[:, 4 * g:4 * g + 4, :]
                    m = last["banks 1-4 read"] = V.mark(ve.tensor_tensor(to, PS[:, 1:5, 0:D], over(bs["q"][:, :], 1, [P, 4, D]), ALU.add))
                    V.after(m)
                    V.mark(ve.tensor_scalar(to, to, 0.0, None, ALU.max))

                norm_groups(X, keys_values, keep=XN)
                norm_groups(XN, queries, gain=g1, shift=b1, keep=QN)
                at = np.float32(np.pi / 2) * np.arange(1, B + 1, dtype=np.float32) / np.float32(B)
                sin, cos = np.sin(at).astype(np.float32), np.cos(at).astype(np.float32)
                for s in range(2):
                    for k in range(2):
                        V.after(V.mark(ve.tensor_tensor(prod[:, :, :], q[:, TB * s:TB * (s + 1), :],
                                                        kv[:, TB * k:TB * (k + 1), 0:D], ALU.mult)))
                        to = dots[:, s, k, :].rearrange("p (i h) -> p i h", h=H)
                        V.after(V.mark(ve.tensor_reduce(to, split(prod[:, :, :]), AX, ALU.add)))
                        V.after(V.mark(ve.tensor_scalar(to, to, float(sin[s] * sin[k] + cos[s] * cos[k]), None, ALU.mult)))
                V.after(V.mark(ve.tensor_tensor(den[:, :, :], dots[:, :, 0, :], dots[:, :, 1, :], ALU.add)))
                V.after(V.mark(ve.tensor_scalar(den[:, :, :], den[:, :, :], 1e-6, None, ALU.max)))
                V.after(V.mark(ve.reciprocal(den[:, :, :], den[:, :, :])))
                V.after(V.mark(ve.tensor_tensor(dots[:, :, :, :], dots[:, :, :, :], over(den[:, :, :], 2, [P, 2, 2, P]), ALU.mult)))
                for s in range(2):
                    for k, to in ((0, prod), (1, prod2)):
                        a = over(dots[:, s, k, :].rearrange("p (i h) -> p i h", h=H), 3, full)
                        m = V.mark(ve.tensor_tensor(split(to[:, :, :]), split(kv[:, TB * k:TB * (k + 1), D:]), a, ALU.mult))
                    V.after(m)
                    V.after(V.mark(ve.tensor_tensor(prod[:, :, :], prod[:, :, :], prod2[:, :, :], ALU.add)))
                    V.after(V.mark(ve.tensor_tensor(att[:, TB * s:TB * (s + 1), :], prod[:, :, :], QN[:, TB * s:TB * (s + 1), :], ALU.add)))
                fence()

                def add_out(g, xn, m, xT, turned):
                    par = g % 2
                    T.after(turned, *used(f"bank {1 + par} read"))
                    for j in range(4):
                        w = te.matmul(PS[:, 1 + par, j * P:(j + 1) * P], xT[:, j * P:(j + 1) * P], ws["o"][:, :], start=True, stop=True)
                    w = last[f"xT{par} read"] = T.mark(w)
                    xg = X[:, 4 * g:4 * g + 4, :]
                    V.after(m)
                    m = last[f"xn{par} read"] = V.mark(ve.tensor_tensor(xg, xg, xn, ALU.add))
                    V.after(m)
                    V.after(V.mark(ve.tensor_tensor(xg, xg, over(bs["o"][:, :], 1, [P, 4, D]), ALU.add)))
                    V.after(w)
                    last[f"bank {1 + par} read"] = V.mark(ve.tensor_tensor(xg, PS[:, 1 + par, :].rearrange("p (j d) -> p j d", j=4), xg, ALU.add))

                norm_groups(att, add_out, gain=g2, shift=b2)

        def local_stack(tag):
            with ExitStack() as own:
                def sl(name, *shape, dtype=F32):
                    return own.enter_context(nc.sbuf_tensor(tag + name, list(shape), dtype))
                Y = XN
                wqkv = sl("wqkv", P, 3 * INNER)
                wo = sl("wo", P, LH // 2, D)
                w1 = sl("w1", P, 2 * HID)
                w2 = sl("w2", P, 3, D)
                b1 = sl("b1", P, 2, 3)
                lng, lnb = sl("lng", P, 1), sl("lnb", P, 1)
                qs, ks = sl("qs", P, LD), sl("ks", P, LD)
                base = sl("base", P, 4, TB, LD)
                rot = sl("rot", P, 4, TB, LD)
                mask = sl("mask", P, NT, 2 * LW, dtype=BF16)
                ident_b = sl("ident_b", P, P, dtype=BF16)
                keep = sl("keep", P, NT)
                XST = sl("XST", P, NT * P)
                sq = sl("sq", P, 2, INNER)
                ssq, irt, itm = (sl(n, P, 2 * LH) for n in ("ssq", "irt", "itm"))
                QN, QR, T2 = sl("QN", P, LH, LD), sl("QR", P, LH, LD), sl("T2", P, LH, LD)
                KN, KR, T3 = sl("KN", P, LH, LD), sl("KR", P, LH, LD), sl("T3", P, LH, LD)
                qT = sl("qT", P, 8, P)
                kT = sl("kT", P, 8, LW + P)
                Vt = sl("Vt", P, 2, INNER)
                V2 = sl("V2", P, 4, 8, LD)
                S = sl("S", P, 2, 8, 2 * LW)
                Pm = sl("Pm", P, 8, 2, 2 * LW)
                pT = sl("pT", P, 8, P)
                mx, sm, rs = (sl(n, P, 2, 8) for n in ("mx", "sm", "rs"))
                O, oT = sl("O", P, 8, 2, LD), sl("oT", P, 8, P)
                xsh = sl("xsh", P, NT, D)
                xnorm = sl("xnorm", P, NT, D)
                xnT = sl("xnT", P, 2, 512)
                fst, fmv, frs = sl("fst", P, 4, 6), sl("fmv", P, 4, 2), sl("frs", P, 4)
                gl, hT = sl("gl", P, 2, 512), sl("hT", P, 2, 3, 512)

                def load_attention(l, *read):
                    WLOAD.after(*read)
                    WLOAD.mark(sp.dma_start(wqkv[:, :], t["l_wqkv"][bass.ds(l, 1), :, :].rearrange("a d n -> (a d) n")))
                    return WLOAD.mark(sp.dma_start(wo[:, :, :], t["l_wo"][bass.ds(l, 1), :, :].rearrange("a (c p) d -> p (a c) d", p=P)))

                def load_scales(l):
                    load(qs[:, :], t["l_qs"][bass.ds(l, 1), :].to_broadcast([P, LD]))
                    return load(ks[:, :], t["l_ks"][bass.ds(l, 1), :].to_broadcast([P, LD]))

                def load_ffn(l):
                    load(w1[:, :], t["l_w1"][bass.ds(l, 1), :, :].rearrange("a d n -> (a d) n"))
                    for c, n in enumerate(HCH):
                        load(w2[0:n, c, :], t["l_w2"][bass.ds(l, 1), c * P:c * P + n, :].rearrange("a p d -> (a p) d"))
                        for k in range(2):
                            load(b1[0:n, k, c:c + 1], t["l_b1"][bass.ds(l, 1), k * HID + c * P:k * HID + c * P + n].rearrange("a (p c) -> p (a c)", c=1))
                    load(w2[HCH[2]:HCH[2] + 1, 2, :], t["l_b2"][bass.ds(l, 1), :])
                    load(lng[:, :], t["l_g"][bass.ds(l, 1), :].rearrange("a (p c) -> p (a c)", c=1))
                    load(lnb[:, :], t["l_b"][bass.ds(l, 1), :].rearrange("a (p c) -> p (a c)", c=1))

                for r in range(4):
                    load(base[:, r, :, :], t["l_rot"][r].rearrange("(i p) d -> p i d", p=P))
                load(mask[:, :, :], t["l_mask"])
                load(ident_b[:, :], t["ident_b"])
                load(keep[:, :], t["l_keep"])
                load_scales(0)
                load_attention(0)
                G.after(G.mark(gp.memset(XST[64:, :], 0.0)))
                G.after(G.mark(gp.memset(xsh[0:1, :, :], 0.0)))
                G.after(G.mark(gp.memset(hT[64:, :, 2, :], 1.0)))
                G.after(G.mark(gp.memset(kT[:, :, :], 0.0)))
                G.after(G.mark(gp.memset(V2[:, :, :, :], 0.0)))
                sp.wait_ge(LOAD.sem, LOAD.count)
                sp.wait_ge(WLOAD.sem, WLOAD.count)
                fence()

                def project_qk(n, c, b):
                    T.after(*used(f"banks {2 * c}-{2 * c + 1} read"))
                    bank = 2 * c + b
                    m = te.matmul(PS[:, bank, :], XST[:, n * P:(n + 1) * P], wqkv[:, bank * 512:(bank + 1) * 512], start=True, stop=True)
                    if b:
                        A.after(T.mark(m), *used(f"sq{c} read"))
                        last[f"sq{c}"] = A.mark(ac.activation(sq[:, c, :], flat(2 * c, 2 * c + 2), ACT.Square))

                def project_norms():
                    for c in range(2):
                        V.after(last[f"sq{c}"])
                        m = last[f"sq{c} read"] = V.mark(ve.tensor_reduce(
                            ssq[:, c * LH:(c + 1) * LH], sq[:, c, :].rearrange("p (h d) -> p h d", d=LD), AX, ALU.add))
                    V.after(m)
                    V.after(V.mark(ve.tensor_scalar(ssq[:, :], ssq[:, :], 1e-24, None, ALU.max)))
                    i32 = mybir.dt.int32
                    V.after(V.mark(ve.tensor_scalar(itm[:, :].bitcast(i32), ssq[:, :].bitcast(i32), 1, None, ALU.logical_shift_right)))
                    V.after(V.mark(ve.tensor_scalar(irt[:, :].bitcast(i32), itm[:, :].bitcast(i32), -1.0, float(0x5F3759DF), ALU.mult, ALU.add)))
                    for _ in range(3):
                        V.after(V.mark(ve.scalar_tensor_tensor(itm[:, :], irt[:, :], -0.5, irt[:, :], ALU.mult, ALU.mult)))
                        V.after(V.mark(ve.tensor_tensor(itm[:, :], itm[:, :], ssq[:, :], ALU.mult)))
                        V.after(V.mark(ve.scalar_tensor_tensor(irt[:, :], itm[:, :], 1.5, irt[:, :], ALU.add, ALU.mult)))

                def project_norm(c):
                    N = (QN, KN)[c]
                    src = PS[:, 2 * c:2 * c + 2, :].rearrange("p b (h d) -> p (b h) d", d=LD)
                    V.after(*used(f"N{c} read"))
                    last[f"N{c}"] = last[f"banks {2 * c}-{2 * c + 1} read"] = V.mark(ve.tensor_tensor(
                        N[:, :, :], src, over(irt[:, c * LH:(c + 1) * LH], 2, [P, LH, LD]), ALU.mult))

                def project_sine(n, c):
                    N, U = ((QN, T2), (KN, T3))[c]
                    G.after(*used(f"N{c}"))
                    half = LD // 2
                    for k in range(2):
                        lo, hi = k * half, (1 - k) * half
                        last[f"U{c}"] = last[f"N{c} read"] = G.mark(gp.tensor_tensor(U[:, :, lo:lo + half], N[:, :, hi:hi + half],
                                                                over(rot[:, 2 * c + 1, n % TB, lo:lo + half], 1, [P, LH, half]), ALU.mult))

                def project_cosine(n, c):
                    N, R = ((QN, QR), (KN, KR))[c]
                    V.after(*used(f"N{c}", f"R{c} read"))
                    last["rot read"] = last[f"C{c}"] = V.mark(ve.tensor_tensor(R[:, :, :], N[:, :, :], over(rot[:, 2 * c, n % TB, :], 1, [P, LH, LD]), ALU.mult))

                def project_sum(c):
                    R, U = ((QR, T2), (KR, T3))[c]
                    G.after(*used(f"U{c}", f"C{c}"))
                    last[f"R{c}"] = G.mark(gp.tensor_tensor(R[:, :, :], R[:, :, :], U[:, :, :], ALU.add))

                def project_v(n):
                    par = n % 2
                    T.after(*used("bank 4 read", "bank 5 read"))
                    for r in range(2):
                        wv = wqkv[:, 2 * INNER:].rearrange("p (c r d) -> p r c d", r=2, d=LD)[:, r, :, :]
                        m = te.matmul(PS[:, 4 + r, :], XST[:, n * P:(n + 1) * P], wv, start=True, stop=True)
                    last["XST read"] = T.mark(m)
                    A.after(last["XST read"], *used(f"V{par} read"))
                    last["bank 4 read"] = last["bank 5 read"] = last[f"V{par}"] = A.mark(ac.copy(Vt[:, par, :], flat(4, 6)))

                def to_bank(bank, blocks):
                    T.after(*used(f"bank {bank} read"))
                    for k, block in enumerate(blocks):
                        m = te.transpose(PS[:, bank, k * P:(k + 1) * P], block, ident[:, :])
                    return T.mark(m)

                def keep_halo(n):
                    G.after(*used("scores", "kT"))
                    last["kT halo"] = G.mark(gp.tensor_tensor(kT[:, :, 0:LW], kT[:, :, P:], over(keep[:, n:n + 1], 1, [P, 8, LW]), ALU.mult))

                def turn(c, b):
                    R, dst, lo = ((QR, qT, 0), (KR, kT, LW))[c]
                    bank = 4 + b
                    T.after(*used(f"R{c}"))
                    m = last[f"R{c} read"] = to_bank(bank, [R[:, 2 * k:2 * k + 2, :].rearrange("p r d -> p (r d)") for k in range(4 * b, 4 * b + 4)])
                    A.after(m, *used("scores", *(["kT halo"] if c else [])))
                    last["kT" if c else "qT"] = last[f"bank {bank} read"] = A.mark(
                        ac.copy(dst[:, 4 * b:4 * b + 4, lo:lo + P], PS[:, bank, :].rearrange("p (c q) -> p c q", c=4)))

                def spread_v(n):
                    par = n % 2
                    HALO.after(*used("pv"), *used("V2"))
                    for r in range(2):
                        halo = HALO.mark(sp.dma_start(V2[64 * r:64 * r + LW, 0, :, :], V2[64 * r + LW:64 * r + 64, 3, :, :]))
                    VDMA.after(*used(f"V{par}"))
                    for w in range(4):
                        if w == 3:
                            VDMA.after(halo)
                        for r in range(2):
                            cols = Vt[:, par, r * 512:(r + 1) * 512].rearrange("p (c d) -> p c d", d=LD)
                            if w == 0:
                                m = VDMA.mark(sp.dma_start(V2[64 * r + LW:64 * r + 64, 0, :, :], cols[0:LW]))
                            else:
                                m = VDMA.mark(sp.dma_start(V2[64 * r:64 * r + 64, w, :, :], cols[LW * (w - 1):LW * (w + 1)]))
                    last["V2"] = last[f"V{par} read"] = m

                def scores(i, r):
                    T.after(*used("qT", "kT", "kT halo", f"bank {6 + r} read"))
                    te.matmul(PS[:, 6 + r, :], ident_b[:, :], over(mask[:, i, :], 1, [P, 8, 2 * LW]),
                              start=True, stop=False, skip_group_check=True)
                    for c in range(8):
                        for w in range(4):
                            m = te.matmul(PS[LW * w:LW * (w + 1), 6 + r, c * 64:(c + 1) * 64],
                                          qT[64 * r:64 * r + 64, c, LW * w:LW * (w + 1)],
                                          kT[64 * r:64 * r + 64, c, LW * w:LW * w + 64], start=False, stop=True,
                                          skip_group_check=True)
                    last["scores"] = last[f"scores{r}"] = T.mark(m)

                def softmax(r):
                    s = PS[:, 6 + r, :].rearrange("p (c k) -> p c k", c=8)
                    V.after(last[f"scores{r}"], *used(f"mx{r} read"))
                    m = V.mark(ve.tensor_reduce(mx[:, r, :], s, AX, ALU.max))
                    V.after(m, *used(f"P{r}"))
                    m = V.mark(ve.tensor_tensor(S[:, r, :, :], s, over(mx[:, r, :], 2, [P, 8, 2 * LW]), ALU.subtract))
                    last[f"mx{r} read"] = last[f"bank {6 + r} read"] = m
                    A.after(m, *used("Pm read", "Pm summed"))
                    last[f"P{r}"] = A.mark(ac.activation(Pm[:, :, r, :], S[:, r, :, :], ACT.Exp))

                def sums():
                    V.after(last["P0"], last["P1"], *used("rs read"))
                    for r in range(2):
                        m = V.mark(ve.tensor_reduce(sm[:, r, :], Pm[:, :, r, :], AX, ALU.add))
                    last["Pm summed"] = m
                    V.after(m)
                    last["rs"] = V.mark(ve.reciprocal(rs[:, :, :], sm[:, :, :]))

                def weights_turn(b):
                    T.after(last["P0"], last["P1"])
                    m = last["Pm read"] = to_bank(6 + b, [Pm[:, c, :, :].rearrange("p r k -> p (r k)") for c in range(4 * b, 4 * b + 4)])
                    A.after(m, *used("pv"))
                    last["pT"] = last[f"bank {6 + b} read"] = A.mark(
                        ac.copy(pT[:, 4 * b:4 * b + 4, :].rearrange("p c q -> p (c q)"), PS[:, 6 + b, :]))

                def values():
                    T.after(last["pT"], *used("V2"))
                    T.after(*used("bank 6 read", "bank 7 read"))
                    for c in range(8):
                        for w in range(4):
                            for r in range(2):
                                m = te.matmul(PS[LW * w:LW * (w + 1), 6 + r, c * LD:(c + 1) * LD],
                                              pT[64 * r:64 * r + 64, c, LW * w:LW * (w + 1)],
                                              V2[64 * r:64 * r + 64, w, c, :], start=True, stop=True, skip_group_check=True)
                    last["pv"] = T.mark(m)

                def divide():
                    for r in range(2):
                        V.after(last["pv"], last["rs"], *used("O read"))
                        last[f"bank {6 + r} read"] = last["O"] = last["rs read"] = V.mark(ve.tensor_tensor(
                            O[:, :, r, :], PS[:, 6 + r, :].rearrange("p (c d) -> p c d", d=LD),
                            over(rs[:, r, :], 2, [P, 8, LD]), ALU.mult))

                def output_turn():
                    T.after(*used("O"))
                    for b in range(2):
                        m = last["O read"] = to_bank(4 + b, [O[:, c, :, :].rearrange("p r d -> p (r d)") for c in range(4 * b, 4 * b + 4)])
                        A.after(m, *used("oT read"))
                        last["oT"] = last[f"bank {4 + b} read"] = A.mark(
                            ac.copy(oT[:, 4 * b:4 * b + 4, :].rearrange("p c q -> p (c q)"), PS[:, 4 + b, :]))

                def output_add(i):
                    T.after(last["oT"])
                    for c in range(8):
                        m = te.matmul(PS[:, 5, 0:D], oT[:, c, :], wo[:, c, :], start=(c == 0), stop=(c == 7))
                    last["oT read"] = m = T.mark(m)
                    V.after(m)
                    yi = Y[:, i, :]
                    last["Y"] = last["bank 5 read"] = V.mark(ve.tensor_tensor(yi, PS[:, 5, 0:D], yi, ALU.add))

                def project_finish(n):
                    project_norm(0)
                    project_sine(n, 0)
                    project_norm(1)
                    project_cosine(n, 0)

                def step(i):
                    attends, outputs = 0 <= i < NT, 0 < i <= NT
                    turns, projects = 0 <= i + 1 < NT, i + 2 < NT
                    if attends:
                        scores(i, 0)
                    if outputs:
                        output_turn()
                    if attends:
                        softmax(0)
                        scores(i, 1)
                        softmax(1)
                    if turns:
                        project_sum(0)
                        project_sine(i + 1, 1)
                        project_cosine(i + 1, 1)
                        project_sum(1)
                        keep_halo(i + 1)
                    if projects:
                        project_qk(i + 2, 0, 0)
                        project_qk(i + 2, 0, 1)
                    if turns:
                        turn(0, 0)
                    if outputs:
                        output_add(i - 1)
                    if projects:
                        project_qk(i + 2, 1, 0)
                    if attends:
                        sums()
                        weights_turn(0)
                        weights_turn(1)
                    if turns:
                        turn(0, 1)
                    if projects:
                        project_qk(i + 2, 1, 1)
                    if turns:
                        turn(1, 0)
                        turn(1, 1)
                    if projects:
                        project_norms()
                    if attends:
                        values()
                        divide()
                    if turns:
                        spread_v(i + 1)
                    if projects:
                        project_finish(i + 2)
                        project_v(i + 2)

                def rotary():
                    half = LD // 2
                    for r, scale in ((0, qs), (2, ks)):
                        V.after(*used("rot read", "U0", "U1"))
                        G.after(*used("rot read", "U0", "U1"))
                        V.mark(ve.tensor_tensor(rot[:, r, :, :], base[:, r, :, :], over(scale[:, :], 1, [P, TB, LD]), ALU.mult))
                        for k in range(2):
                            lo, hi = k * half, (1 - k) * half
                            sine = G.mark(gp.tensor_tensor(rot[:, r + 1, :, lo:lo + half], base[:, r + 1, :, lo:lo + half],
                                                           over(scale[:, hi:hi + half], 1, [P, TB, half]), ALU.mult))
                    G.after(sine)

                def turn_x(g):
                    last["xT"] = to_bank(7, [Y[:, 4 * g + j, :] for j in range(4)])
                    n = 511 if g % 2 else 512
                    A.after(last["xT"], *used("XST read"))
                    A.mark(ac.copy(XST[0:64, g * 512:(g + 1) * 512], PS[0:64, 7, :]))
                    last["XST"] = last["bank 7 read"] = A.mark(ac.copy(XST[64:, g * 512 + 1:g * 512 + 1 + n], PS[64:, 7, 0:n]))

                def shift(g):
                    SHIFT.after(last["Y"], *used("xsh read"))
                    tiles = slice(4 * g, 4 * g + 4)
                    SHIFT.mark(sp.dma_start(xsh[:, tiles, 0:D // 2], Y[:, tiles, 0:D // 2]))
                    SHIFT.mark(sp.dma_start(xsh[1:P, tiles, D // 2:], Y[0:P - 1, tiles, D // 2:]))
                    a = 4 * g + (1 if 4 * g % TB == 0 else 0)
                    last["xsh"] = SHIFT.mark(sp.dma_start(xsh[0:1, a:4 * g + 4, D // 2:], Y[P - 1:P, a - 1:4 * g + 3, D // 2:]))

                def statistics(g):
                    V.after(last["xsh"])
                    for j in range(4):
                        m = V.mark(ve.bn_stats(fst[:, j, :], xsh[:, 4 * g + j, :]))
                    V.after(m)
                    for j in range(4):
                        m = V.mark(ve.bn_aggr(fmv[:, j, :], fst[:, j, :]))
                    V.after(m)
                    G.after(V.mark(ve.tensor_scalar(frs[:, :], fmv[:, :, 1], EPS, None, ALU.add)))
                    last["frs"] = inverse_root(frs[:, :], 4)

                def normalise(g):
                    V.after(last["frs"])
                    for j in range(4):
                        m = V.mark(ve.tensor_scalar(xnorm[:, 4 * g + j, :], xsh[:, 4 * g + j, :], fmv[:, j, 0:1], frs[:, j:j + 1],
                                                    ALU.subtract, ALU.mult))
                    last[f"xnorm{g}"] = last["xsh read"] = m

                def norm_turn(g):
                    par = g % 2
                    T.after(last[f"xnorm{g}"])
                    m = to_bank(7, [xnorm[:, 4 * g + j, :] for j in range(4)])
                    A.after(m, *used(f"xnT{par} read"))
                    last[f"xnT{par}"] = last["bank 7 read"] = A.mark(
                        ac.activation(xnT[:, par, :], PS[:, 7, :], ACT.Identity, scale=lng[:, 0:1], bias=lnb[:, 0:1]))

                def up(g, c):
                    n, par, slot = HCH[c], g % 2, (3 * g + c) % 2
                    T.after(last[f"xnT{par}"], *used(f"up{c} read", f"banks {2 * c}-{2 * c + 1} read", f"bank {2 * c} read", f"bank {2 * c + 1} read"))
                    te.matmul(PS[0:n, 2 * c, :], w1[:, HID + c * P:HID + c * P + n], xnT[:, par, :], start=True, stop=True)
                    m = last[f"xnT{par} read"] = T.mark(te.matmul(PS[0:n, 2 * c + 1, :], w1[:, c * P:c * P + n], xnT[:, par, :], start=True, stop=True))
                    A.after(m, *used(f"gl{slot} read"))
                    m = A.mark(ac.activation(gl[0:n, slot, :], PS[0:n, 2 * c, :], ACT.Gelu, bias=b1[0:n, 1, c:c + 1]))
                    V.after(m, *used(f"hT{par} read"))
                    m = V.mark(ve.scalar_tensor_tensor(hT[0:n, par, c, :], PS[0:n, 2 * c + 1, :], b1[0:n, 0, c:c + 1], gl[0:n, slot, :],
                                                       ALU.add, ALU.mult))
                    for name in (f"hT{par}", f"gl{slot} read", f"up{c} read", f"banks {2 * c}-{2 * c + 1} read", f"bank {2 * c} read", f"bank {2 * c + 1} read"):
                        last[name] = m

                def down(g):
                    par = g % 2
                    T.after(last[f"hT{par}"], *used("bank 6 read"))
                    for j in range(4):
                        for c, n in enumerate((P, P, HCH[2] + 1)):
                            m = te.matmul(PS[:, 6, j * D:(j + 1) * D], hT[0:n, par, c, j * P:(j + 1) * P], w2[0:n, c, :],
                                          start=(c == 0), stop=(c == 2))
                    m = last[f"hT{par} read"] = T.mark(m)
                    V.after(m)
                    yg = Y[:, 4 * g:4 * g + 4, :]
                    last["bank 6 read"] = last["Y"] = V.mark(ve.tensor_tensor(yg, PS[:, 6, :].rearrange("p (j d) -> p j d", j=4), yg, ALU.add))

                def feed_forward(weights):
                    norm_turn(0)
                    for g in range(NG):
                        up(g, 0)
                        if g:
                            down(g - 1)
                        if g == 0:
                            statistics(NG - 1)
                            normalise(NG - 1)
                        up(g, 1)
                        if g < NG - 1:
                            norm_turn(g + 1)
                        up(g, 2)
                        if g == 1:
                            rotary()
                        if g:
                            T.after(last["Y"])
                            turn_x(g - 1)
                    T.after(weights, last["XST"])
                    for c in range(2):
                        for b in range(2):
                            project_qk(0, c, b)
                    down(NG - 1)
                    project_norms()
                    project_finish(0)
                    T.after(last["Y"])
                    turn_x(NG - 1)
                    project_v(0)

                def end_of_layer():
                    for lane in (HALO, VDMA, SHIFT, LOAD, WLOAD):
                        if lane.count:
                            sp.wait_ge(lane.sem, lane.count)
                    fence()

                norm_groups(X, None, keep=Y)
                rotary()
                for g in range(NG):
                    turn_x(g)
                T.after(last["XST"])
                for i in (-2, -1, 0):
                    step(i)
                end_of_layer()
                with nc.Fori(0, DEPTH) as l:
                    load_ffn(l)
                    scales = load_scales(l + 1)
                    for i in range(1, NT + 1):
                        step(i)
                        if i % 4 == 0:
                            shift(i // 4 - 1)
                        if i > 4 and i % 4 == 1:
                            statistics(i // 4 - 1)
                        if i > 4 and i % 4 == 2:
                            normalise(i // 4 - 1)
                    weights = load_attention(l + 1, last["XST read"], last["oT read"])
                    ac.preload_act_table(ACT.Gelu)
                    for lane in (T, V, A, G):
                        lane.after(scales)
                    feed_forward(weights)
                    ac.preload_act_table(ACT.Exp)
                    step(-1)
                    step(0)
                    end_of_layer()
                V.mark(ve.tensor_tensor(X[:, :, :], X[:, :, :], Y[:, :, :], ALU.add))
                fence()

        window_attention()
        mixture("f_")
        causal_attention()
        mixture("g_")
        cope_attention()
        local_stack("l_")
        linear_attention()
        local_stack("m_")
        done = LOAD.mark(sp.dma_start(out.rearrange("b (i p) d -> p (b i) d", p=P), X[:, :, :]))
        sp.wait_ge(LOAD.sem, LOAD.count)


def tables():
    f = np.float32
    c = {"ident": np.eye(P, dtype=f)}
    c["a_headmask"] = (np.arange(P)[:, None] // A_DH == np.arange(A_H)[None, :]).astype(f)
    c["f_lower"] = (np.arange(E_N)[None, :] < np.arange(E_N)[:, None]).astype(f).reshape(-1)
    ahead = np.arange(2 * L - P)[None, :] - (L - P) - np.arange(P)[:, None]
    c["b_future"] = np.where(ahead > 0, NEG, 0.0).astype(f)
    half = np.arange(0, LD, 2, dtype=f)
    freqs = np.arange(L, dtype=f)[:, None] * (f(1) / f(10000) ** (half / f(LD)))[None, :]
    freqs = np.concatenate([freqs, freqs], -1)
    power = (np.arange(L, dtype=f) - L // 2) / f(LW // 2)
    scale = ((half + f(0.4 * LD)) / f(1.4 * LD))[None, :] ** power[:, None]
    scale = np.concatenate([scale, scale], -1)
    cos, sin = np.cos(freqs), np.sin(freqs)
    sin = np.concatenate([-sin[:, :LD // 2], sin[:, LD // 2:]], -1)
    c["l_rot"] = np.stack([8 * cos * scale, 8 * sin * scale, cos / scale, sin / scale]).astype(f)
    a, k = np.arange(P)[:, None] % LW, np.arange(2 * LW)[None, :]
    allowed = (a <= k) & (k <= a + LW)
    first = allowed & ((np.arange(P)[:, None] >= LW) | (k >= LW))
    m = np.stack([first if i % TB == 0 else allowed for i in range(NT)], 1)
    bf16 = mybir.dt.np(BF16)
    c["l_mask"] = np.where(m, 0.0, NEG).astype(bf16)
    c["ident_b"] = np.eye(P, dtype=bf16)
    c["l_keep"] = np.tile((np.arange(NT) % TB != 0).astype(f), (P, 1))
    return c


def kernel(**inputs):
    from concourse import bacc
    from concourse.bass_utils import run_bass_kernel_spmd

    a = {k: np.asarray(v) for k, v in inputs.items()}
    arrays = {"x": a["L0_attn_a_x"]}
    for n in "qkvo":
        arrays[f"a_w{n}T"] = a[f"L0_attn_a_W{n}"].T
        arrays[f"a_b{n}"] = a[f"L0_attn_a_b{n}"]
        arrays[f"c_w{n}"] = a[f"L1_attn_a_W{n}"]
        arrays[f"c_b{n}"] = a[f"L1_attn_a_b{n}"]
        for part in "ASb":
            arrays[f"d_{n}{part}"] = a[f"L1_attn_b_{n}{part}"]
    arrays["b_wqk"], arrays["b_wov"] = a["L0_attn_b_wqk"], a["L0_attn_b_wov"]
    arrays["f_gateT"] = a["L0_ffn_gate_w"].T
    for n in "123":
        arrays[f"f_w{n}T"] = a[f"L0_ffn_w{n}"].transpose(0, 2, 1)
        arrays[f"f_b{n}"] = a[f"L0_ffn_b{n}"]
    arrays["f_sw12T"] = np.concatenate([a["L0_ffn_sw1"].T, a["L0_ffn_sw2"].T], 1)
    arrays["f_sw3T"] = a["L0_ffn_sw3"].T
    arrays["c_pos"] = a["L1_attn_a_pos_emb"]
    for n in ("g1", "b1", "g2", "b2"):
        arrays[f"d_{n}"] = a[f"L1_attn_b_{n}"]
    for n, src in (("wqkv", "Wqkv"), ("wo", "Wo"), ("qs", "q_scale"), ("ks", "k_scale")):
        w = a[f"L1_ffn_{src}"]
        arrays[f"l_{n}"] = np.concatenate([w, w[:1]])
    for n, src in (("w1", "W1"), ("b1", "b1"), ("w2", "W2"), ("b2", "b2"), ("g", "ln_g"), ("b", "ln_b")):
        arrays[f"l_{n}"] = a[f"L1_ffn_{src}"]
    arrays.update(tables())

    nc = bacc.Bacc("TRN2", target_bir_lowering=False, num_devices=1)
    arrays = {k + "_dram": np.ascontiguousarray(v) for k, v in arrays.items()}
    t = {k[:-5]: nc.dram_tensor(k, v.shape, mybir.dt.from_np(v.dtype), kind="ExternalInput").ap() for k, v in arrays.items()}
    out = nc.dram_tensor("out_dram", (B, L, D), F32, kind="ExternalOutput").ap()
    build(nc, t, out)
    r = run_bass_kernel_spmd(nc, [arrays], core_ids=[0])
    return r.results[0]["out_dram"]
```
